# Optimizing a Trainium2 kernel written in Bass

```python
import numpy as np
import jax
import jax.numpy as jnp

def _softmax(x, axis=-1):
    return jax.nn.softmax(x, axis=axis)

def _gelu(x):
    return jax.nn.gelu(x, approximate=True)

def _silu(x):
    return jax.nn.silu(x)

def _sigmoid(x):
    return jax.nn.sigmoid(x)

def _layernorm(x, axis=-1, eps=1e-05):
    m = jnp.mean(x, axis=axis, keepdims=True)
    v = jnp.var(x, axis=axis, keepdims=True)
    return (x - m) / jnp.sqrt(v + eps)

def _scatter_add(tgt, idx, src, axis=0):
    return tgt.at[idx].add(src)

def _segment_sum(src, seg, n):
    return jax.ops.segment_sum(src, seg, n)
kernel_name = 'mk_decoder_postln_d1_seqx_r8_b05a22'

def setup_inputs(seed: int=0):
    np.random.seed(seed)
    _w = jnp.asarray

    def _rec_inputs():
        import jax
        import jax.numpy as jnp
        _rk = jax.random.key(seed)
        x = -0.0002928 + 1 * jax.random.normal(jax.random.fold_in(_rk, 1), (16, 128, 256), jnp.float32)
        _lenS = 128 - jax.random.randint(jax.random.fold_in(_rk, 7), (16,), 0, max(1, 128 // 4) + 1, jnp.int32)
        _lenS2 = 128 - jax.random.randint(jax.random.fold_in(_rk, 8), (16,), 0, max(1, 128 // 4) + 1, jnp.int32)
        _ctx_2048P = jax.random.normal(jax.random.fold_in(_rk, 11), (16, 16, 256), jnp.float32)
        _ctx_2048c = jax.random.dirichlet(jax.random.fold_in(_rk, 511), 0.3 * jnp.ones((16,), jnp.float32), (16, 128))
        _ctx_2048t = jnp.einsum('bsk,bkd->bsd', _ctx_2048c, _ctx_2048P)
        _ctx_2048t = _ctx_2048t * jax.lax.rsqrt(jnp.mean(jnp.square(_ctx_2048t)) + 1e-12) * 0.953939
        ctx_2048 = -1.39393e-06 + 0.999914 * (_ctx_2048t + 0.3 * jax.random.normal(jax.random.fold_in(_rk, 611), (16, 128, 256), jnp.float32))
        _validS = jnp.arange(128)[None, :] < _lenS[:, None]
        _validS2 = jnp.arange(128)[None, :] < _lenS2[:, None]
        _causal = jnp.tril(jnp.ones((128, 128), dtype=bool))
        mask_Bx1x2048_fk1 = jnp.where(jnp.ones((16, 1, 256), dtype=bool), 1.0, 0.0).astype(jnp.float32)
        return (x, ctx_2048, mask_Bx1x2048_fk1)
    x, ctx_2048, mask_Bx1x2048_fk1 = _rec_inputs()

    def _L0_attn_setup():
        import jax, jax.numpy as jnp
        import numpy as np
        B, N, D, H = (2, 256, 256, 16)
        HD = D // H
        CHUNK = 64
        BASE = 10000.0

        def _l2norm(x, eps=1e-06):
            return x * jax.lax.rsqrt(jnp.sum(x * x, axis=-1, keepdims=True) + eps)

        def _rope(x):
            n, d = (x.shape[1], x.shape[-1])
            inv = 1.0 / BASE ** (jnp.arange(0, d, 2, dtype=jnp.float32) / d)
            th = jnp.arange(n, dtype=jnp.float32)[:, None] * inv
            cos = jnp.cos(th)[None, :, None, :]
            sin = jnp.sin(th)[None, :, None, :]
            x1, x2 = jnp.split(x, 2, axis=-1)
            return jnp.concatenate([x1 * cos - x2 * sin, x1 * sin + x2 * cos], axis=-1)

        def _kernel_regression(k, v, beta):
            b, n, h, dk = k.shape
            dv = v.shape[-1]
            nc = n // CHUNK
            Kc = k.reshape(b, nc, CHUNK, h, dk).transpose(1, 0, 3, 2, 4)
            Vc = v.reshape(b, nc, CHUNK, h, dv).transpose(1, 0, 3, 2, 4)
            Bc = beta.reshape(b, nc, CHUNK, h).transpose(1, 0, 3, 2)
            eye = jnp.eye(CHUNK, dtype=k.dtype)

            def step(S, inp):
                K, V, bt = inp
                A = jnp.tril(jnp.einsum('bhik,bhjk->bhij', K, K) * bt[:, :, None, :], -1)
                rhs = V - jnp.einsum('bhck,bhkv->bhcv', K, S)
                Vn = jax.scipy.linalg.solve_triangular(eye + A, rhs, lower=True)
                S = S + jnp.einsum('bhck,bhcv->bhkv', K * bt[..., None], Vn)
                return (S, Vn)
            S0 = jnp.zeros((b, h, dk, dv), k.dtype)
            S, Vn = jax.lax.scan(step, S0, (Kc, Vc, Bc))
            v_new = Vn.transpose(1, 0, 3, 2, 4).reshape(b, n, h, dv)
            return (v_new, S)
        key = jax.random.key(seed)
        ks = jax.random.split(key, 6)
        s = 0.02
        return {'x': jax.random.normal(ks[0], (B, N, D), jnp.float32), 'Wq': jax.random.normal(ks[1], (D, D), jnp.float32) * s, 'Wk': jax.random.normal(ks[2], (D, D), jnp.float32) * s, 'Wv': jax.random.normal(ks[3], (D, D), jnp.float32) * s, 'Wo': jax.random.normal(ks[4], (D, D), jnp.float32) * s, 'Wb': jax.random.normal(ks[5], (D, H), jnp.float32) * s}
    _L0_attn_all = _L0_attn_setup()
    _L0_attn_in = {k: v for k, v in _L0_attn_all.items() if k in ('Wq', 'Wk', 'Wv', 'Wo', 'Wb')}
    del _L0_attn_all

    def _L0_xattn_setup():
        import math
        import jax, jax.numpy as jnp
        import numpy as np
        SIZE = 128
        HEADS = 16
        HEAD_DIM = SIZE // HEADS
        B, T, S = (2, 256, 256)
        NEG = 1000000.0
        key = jax.random.key(seed)
        ks = jax.random.split(key, 10)
        target = jax.random.normal(ks[0], (B, SIZE, T), dtype=jnp.float32)
        source = jax.random.normal(ks[1], (B, SIZE, S), dtype=jnp.float32)
        target_mask = (jax.random.uniform(ks[2], (B, 1, T)) > 0.1).astype(jnp.float32)
        source_mask = (jax.random.uniform(ks[3], (B, 1, S)) > 0.1).astype(jnp.float32)
        scale = 1.0 / math.sqrt(SIZE)
        Wq = jax.random.normal(ks[4], (SIZE, SIZE), dtype=jnp.float32) * scale
        Wk = jax.random.normal(ks[5], (SIZE, SIZE), dtype=jnp.float32) * scale
        Wv = jax.random.normal(ks[6], (SIZE, SIZE), dtype=jnp.float32) * scale
        bq = jax.random.normal(ks[7], (SIZE,), dtype=jnp.float32) * 0.01
        bk = jax.random.normal(ks[8], (SIZE,), dtype=jnp.float32) * 0.01
        bv = jax.random.normal(ks[9], (SIZE,), dtype=jnp.float32) * 0.01
        return {'target': target, 'source': source, 'target_mask': target_mask, 'source_mask': source_mask, 'Wq': Wq, 'bq': bq, 'Wk': Wk, 'bk': bk, 'Wv': Wv, 'bv': bv}
    _L0_xattn_all = _L0_xattn_setup()
    _L0_xattn_in = {k: v for k, v in _L0_xattn_all.items() if k in ('Wq', 'bq', 'Wk', 'bk', 'Wv', 'bv')}
    del _L0_xattn_all

    def _L0_ffn_setup():
        import jax, jax.numpy as jnp
        import numpy as np
        B, S, H, E, D, K = (2, 256, 256, 8, 256, 2)
        key = jax.random.key(seed)
        ks = jax.random.split(key, 4)
        return {'x': jax.random.normal(ks[0], (B, S, H), jnp.float32), 'router_w': jax.random.normal(ks[1], (H, E), jnp.float32) / np.sqrt(H).astype(np.float32), 'router_b': jnp.zeros((E,), jnp.float32), 'expert_w': jax.random.normal(ks[2], (E, H, D), jnp.float32) / np.sqrt(H).astype(np.float32), 'expert_b': jnp.zeros((E, D), jnp.float32), 'out_w': jax.random.normal(ks[3], (D, D), jnp.float32) / np.sqrt(D).astype(np.float32), 'out_b': jnp.zeros((D,), jnp.float32)}
    _L0_ffn_all = _L0_ffn_setup()
    _L0_ffn_in = {k: v for k, v in _L0_ffn_all.items() if k in ('router_w', 'router_b', 'expert_w', 'expert_b', 'out_w', 'out_b')}
    del _L0_ffn_all
    return {'x': x, 'ctx_2048': ctx_2048, 'mask_Bx1x2048_fk1': mask_Bx1x2048_fk1, 'L0_attn_Wq': _L0_attn_in['Wq'], 'L0_attn_Wk': _L0_attn_in['Wk'], 'L0_attn_Wv': _L0_attn_in['Wv'], 'L0_attn_Wo': _L0_attn_in['Wo'], 'L0_attn_Wb': _L0_attn_in['Wb'], 'L0_xattn_Wq': _L0_xattn_in['Wq'], 'L0_xattn_bq': _L0_xattn_in['bq'], 'L0_xattn_Wk': _L0_xattn_in['Wk'], 'L0_xattn_bk': _L0_xattn_in['bk'], 'L0_xattn_Wv': _L0_xattn_in['Wv'], 'L0_xattn_bv': _L0_xattn_in['bv'], 'L0_ffn_router_w': _L0_ffn_in['router_w'], 'L0_ffn_router_b': _L0_ffn_in['router_b'], 'L0_ffn_expert_w': _L0_ffn_in['expert_w'], 'L0_ffn_expert_b': _L0_ffn_in['expert_b'], 'L0_ffn_out_w': _L0_ffn_in['out_w'], 'L0_ffn_out_b': _L0_ffn_in['out_b']}

def reference(x, ctx_2048, mask_Bx1x2048_fk1, L0_attn_Wq, L0_attn_Wk, L0_attn_Wv, L0_attn_Wo, L0_attn_Wb, L0_xattn_Wq, L0_xattn_bq, L0_xattn_Wk, L0_xattn_bk, L0_xattn_Wv, L0_xattn_bv, L0_ffn_router_w, L0_ffn_router_b, L0_ffn_expert_w, L0_ffn_expert_b, L0_ffn_out_w, L0_ffn_out_b):
    import jax
    import jax.numpy as jnp

    def _L0_attn_ref(x, Wq, Wk, Wv, Wo, Wb):
        import jax, jax.numpy as jnp
        import numpy as np
        B, N, D, H = (2, 256, 256, 16)
        HD = D // H
        CHUNK = 64
        BASE = 10000.0

        def _l2norm(x, eps=1e-06):
            return x * jax.lax.rsqrt(jnp.sum(x * x, axis=-1, keepdims=True) + eps)

        def _rope(x):
            n, d = (x.shape[1], x.shape[-1])
            inv = 1.0 / BASE ** (jnp.arange(0, d, 2, dtype=jnp.float32) / d)
            th = jnp.arange(n, dtype=jnp.float32)[:, None] * inv
            cos = jnp.cos(th)[None, :, None, :]
            sin = jnp.sin(th)[None, :, None, :]
            x1, x2 = jnp.split(x, 2, axis=-1)
            return jnp.concatenate([x1 * cos - x2 * sin, x1 * sin + x2 * cos], axis=-1)

        def _kernel_regression(k, v, beta):
            b, n, h, dk = k.shape
            dv = v.shape[-1]
            nc = n // CHUNK
            Kc = k.reshape(b, nc, CHUNK, h, dk).transpose(1, 0, 3, 2, 4)
            Vc = v.reshape(b, nc, CHUNK, h, dv).transpose(1, 0, 3, 2, 4)
            Bc = beta.reshape(b, nc, CHUNK, h).transpose(1, 0, 3, 2)
            eye = jnp.eye(CHUNK, dtype=k.dtype)

            def step(S, inp):
                K, V, bt = inp
                A = jnp.tril(jnp.einsum('bhik,bhjk->bhij', K, K) * bt[:, :, None, :], -1)
                rhs = V - jnp.einsum('bhck,bhkv->bhcv', K, S)
                Vn = jax.scipy.linalg.solve_triangular(eye + A, rhs, lower=True)
                S = S + jnp.einsum('bhck,bhcv->bhkv', K * bt[..., None], Vn)
                return (S, Vn)
            S0 = jnp.zeros((b, h, dk, dv), k.dtype)
            S, Vn = jax.lax.scan(step, S0, (Kc, Vc, Bc))
            v_new = Vn.transpose(1, 0, 3, 2, 4).reshape(b, n, h, dv)
            return (v_new, S)
        b, n, d = x.shape
        q = (x @ Wq).reshape(b, n, H, HD)
        k = _l2norm((x @ Wk).reshape(b, n, H, HD))
        v = (x @ Wv).reshape(b, n, H, HD)
        beta = 2.0 * jax.nn.sigmoid(x @ Wb)
        q = _rope(q)
        k = _rope(k)
        v, _state = _kernel_regression(k, v, beta)
        k = k * beta[..., None]
        scale = HD ** (-0.5)
        scores = jnp.einsum('bqhd,bkhd->bhqk', q, k) * scale
        mask = jnp.tril(jnp.ones((n, n), bool))
        scores = jnp.where(mask, scores, -jnp.inf)
        attn = jax.nn.softmax(scores, axis=-1)
        out = jnp.einsum('bhqk,bkhd->bqhd', attn, v).reshape(b, n, d)
        return out @ Wo

    def _L0_xattn_ref(target, source, target_mask, source_mask, Wq, bq, Wk, bk, Wv, bv):
        import math
        import jax, jax.numpy as jnp
        import numpy as np
        SIZE = 128
        HEADS = 16
        HEAD_DIM = SIZE // HEADS
        B, T, S = (2, 256, 256)
        NEG = 1000000.0
        b, _, t = target.shape
        s = source.shape[-1]
        q = jnp.einsum('oc,bct->bot', Wq, target) + bq[None, :, None]
        k = jnp.einsum('oc,bcs->bos', Wk, source) + bk[None, :, None]
        v = jnp.einsum('oc,bcs->bos', Wv, source) + bv[None, :, None]
        q = q.reshape(b, HEADS, HEAD_DIM, t)
        k = k.reshape(b, HEADS, HEAD_DIM, s)
        v = v.reshape(b, HEADS, HEAD_DIM, s)
        dot = jnp.einsum('bhdt,bhds->bhts', q, k) / math.sqrt(HEAD_DIM)
        mask = target_mask[:, :, :, None] * source_mask[:, :, None, :]
        dot = mask * dot - (1.0 - mask) * NEG
        amap = jax.nn.softmax(dot, axis=-1) * mask
        out = jnp.einsum('bhts,bhds->bhdt', amap, v)
        return out.reshape(b, HEADS * HEAD_DIM, t)

    def _L0_ffn_ref(x, router_w, router_b, expert_w, expert_b, out_w, out_b):
        import jax, jax.numpy as jnp
        import numpy as np
        B, S, H, E, D, K = (2, 256, 256, 8, 256, 2)
        num_experts = expert_w.shape[0]
        router_logits = jnp.einsum('bsh,he->bse', x, router_w) + router_b
        router_probs = jax.nn.softmax(router_logits, axis=-1)
        top_k_probs, top_k_indices = jax.lax.top_k(router_probs, K)
        top_k_probs = top_k_probs / jnp.sum(top_k_probs, axis=-1, keepdims=True)
        onehot = jax.nn.one_hot(top_k_indices, num_experts, dtype=x.dtype)
        gates = jnp.einsum('bsk,bske->bse', top_k_probs, onehot)
        expert_out = jax.nn.gelu(jnp.einsum('bsh,ehd->ebsd', x, expert_w) + expert_b[:, None, None, :])
        combined = jnp.einsum('bse,ebsd->bsd', gates, expert_out)
        return jnp.einsum('bsd,df->bsf', combined, out_w) + out_b
    x = _layernorm(x + _L0_attn_ref(x, L0_attn_Wq, L0_attn_Wk, L0_attn_Wv, L0_attn_Wo, L0_attn_Wb), axis=-1)
    x = _layernorm(x + _L0_xattn_ref(x, ctx_2048, mask_Bx1x2048_fk1, mask_Bx1x2048_fk1, L0_xattn_Wq, L0_xattn_bq, L0_xattn_Wk, L0_xattn_bk, L0_xattn_Wv, L0_xattn_bv), axis=-1)
    x = _layernorm(x + _L0_ffn_ref(x, L0_ffn_router_w, L0_ffn_router_b, L0_ffn_expert_w, L0_ffn_expert_b, L0_ffn_out_w, L0_ffn_out_b), axis=-1)
    return x

_drawn_inputs = setup_inputs


def setup_inputs(seed=0):
    import zlib

    import numpy as np

    out = dict(_drawn_inputs(seed))
    spreads = {'L0_ffn_router_b': (0.0, 0.1), 'L0_ffn_expert_b': (0.0, 0.1), 'L0_ffn_out_b': (0.0, 0.1)}
    factors = {'L0_attn_Wq': 8.0,
     'L0_attn_Wb': 5.43,
     'L0_xattn_bq': 8.0,
     'L0_xattn_bk': 8.0,
     'L0_xattn_bv': 8.0}
    for name, (base, spread) in spreads.items():
        noise = np.random.default_rng([zlib.crc32(name.encode()), seed]).standard_normal(out[name].shape)
        drawn = base * np.exp(spread * noise) if base else spread * noise
        out[name] = jnp.asarray(drawn.astype(out[name].dtype))
    for name, factor in factors.items():
        out[name] = (out[name] * factor).astype(out[name].dtype)
    return out
```

```python
from contextlib import ExitStack

import concourse.bass as bass
from concourse import mybir

F32 = mybir.dt.float32
BF16 = mybir.dt.bfloat16
I32 = mybir.dt.int32
U32 = mybir.dt.uint32
ALU = mybir.AluOpType
ACT = mybir.ActivationFunctionType
AX = mybir.AxisListType

B = 16
N = 128
D = 256
H = 16
HD = D // H
XD = N // H
C = 32
NC = N // C
E = 8
TERMS = 6
PARTS = 3
Q_PARTS = ((0, 3), (1, 2), (2, 1))
K_PARTS = ((0, 3), (0, 2), (0, 1))
NEG = 1.0e6
OUT_OF_SIGHT = -1.0e30
LN_EPS = 1e-5
L2_EPS = 1e-6
RSQRT_MAGIC = 0x5F3759DF


def reached(eng, sem, count):
    if not (isinstance(count, int) and count <= 0):
        eng.wait_ge(sem, count)


def sweep(eng, stages):
    deepest = max(lag for lag, _ in stages)
    first = (deepest + 3) // 2 * 2
    for t in range(first):
        for lag, body in stages:
            if t >= lag:
                body(t - lag, (t - lag) % 2)
    with eng.Fori(0, (B - first) // 2) as i:
        for half in range(2):
            for lag, body in stages:
                body(2 * i + (first + half - lag), (half - lag) % 2)
    for t in range(B, B + deepest):
        for lag, body in stages:
            if t - lag < B:
                body(t - lag, (t - lag) % 2)


class Chain:

    def __init__(self, eng, sem, b, per):
        self.eng, self.sem, self.base, self.per, self.n = eng, sem, b * per, per, 0

    def link(self, ins):
        self.n += 1
        ins.then_inc(self.sem, 1)
        self.eng.wait_ge(self.sem, self.base + self.n)

    def done(self):
        assert self.n == self.per, (self.n, self.per)


RSQRT_LINKS = 11


def rsqrt(eng, chain, y, x, half_x_y, bits):
    chain.link(eng.tensor_scalar(bits, x.bitcast(I32), 1, None, ALU.logical_shift_right))
    chain.link(eng.tensor_scalar(y.bitcast(I32), bits, -1.0, float(RSQRT_MAGIC), ALU.mult, ALU.add))
    for _ in range(3):
        chain.link(eng.tensor_tensor(half_x_y, y, y, ALU.mult))
        chain.link(eng.scalar_tensor_tensor(half_x_y, half_x_y, -0.5, x, ALU.mult, ALU.mult))
        chain.link(eng.scalar_tensor_tensor(y, half_x_y, 1.5, y, ALU.add, ALU.mult))


NORM_LINKS = 3 + RSQRT_LINKS


def layer_norm_stats(eng, chain, y, stats, moments, rstd, tmp, bits):
    chain.link(eng.bn_stats(stats, y))
    eng.memset(bits, 0)
    chain.link(eng.bn_aggr(moments, stats))
    chain.link(eng.tensor_scalar(moments[:, 1:2], moments[:, 1:2], LN_EPS, None, ALU.add))
    rsqrt(eng, chain, rstd, moments[:, 1:2], tmp, bits)


class Phase:

    def __init__(self, nc, ctx, name):
        self.nc, self.ctx, self.name = nc, ctx, name

    def sb(self, name, shape, dt=F32):
        return self.ctx.enter_context(self.nc.sbuf_tensor(f"{self.name}_{name}", shape, dt))

    def two(self, name, shape, dt=F32):
        return [self.sb(f"{name}{u}", shape, dt) for u in range(2)]

    def bank(self, name):
        return self.ctx.enter_context(self.nc.psum_tensor(f"{self.name}_{name}", [128, 512], F32))

    def sem(self, name):
        return self.ctx.enter_context(self.nc.semaphore(f"{self.name}_{name}"))


def project(nc, sems, x, w, rope, identity, in_block, parts_scr, vk_scr, kb_scr, a_scr):
    with ExitStack() as ctx:
        ph = Phase(nc, ctx, "pr")
        sem = lambda name: sems.enter_context(nc.semaphore(f"pr_{name}"))
        w_sb = ph.sb("w", [128, 2, 3 * D + H])
        rope_sb = ph.sb("rope", [128, 2, 2 * D])
        id_sb = ph.sb("id", [128, 128])
        below_sb = ph.sb("below", [128, C])
        x_sb = ph.two("x", [128, D])
        xt_sb = ph.two("xt", [128, 2, 128])
        with_cos = ph.sb("with_cos", [128, 2 * D])
        with_sin = ph.sb("with_sin", [128, 2 * D])
        qk = ph.two("qk", [128, 2 * D])
        ksq = ph.sb("ksq", [128, D])
        ez = ph.two("ez", [128, H])
        beta = ph.sb("beta", [128, H])
        ss = ph.sb("ss", [128, H])
        knorm = ph.sb("knorm", [128, 2, H])
        tmp = ph.sb("tmp", [128, H])
        bits = ph.sb("bits", [128, H], I32)
        vk = ph.two("vk", [128, 2 * HD, H])
        kb = ph.two("kb", [128, D])
        kbh = ph.two("kbh", [128, H, HD])
        rest = ph.two("rest", [128, 3, D])
        parts = ph.two("parts", [128, 3, PARTS, 2, 128], BF16)
        kst = ph.two("kst", [TERMS * HD, H, N], BF16)
        kbst = ph.two("kbst", [TERMS * HD, H, N], BF16)
        a_sb = ph.two("a", [128, H, C])
        ps_qk, ps_vb, ps_qb, ps_xk, ps_a = (ph.bank(n) for n in ("qk", "vb", "qb", "xk", "a"))

        consts = sem("consts")
        x_loaded = [sem(f"x_loaded{u}") for u in range(2)]
        xt_made, xt_copied = sem("xt_made"), sem("xt_copied")
        projected, v_copied, ez_made = sem("projected"), sem("v_copied"), sem("ez_made")
        rope_halves, rotated, squared = sem("rope_halves"), sem("rotated"), sem("squared")
        norm_step, norms_made = sem("norm_step"), sem("norms_made")
        k_scaled, kb_scaled, kb_turned = sem("k_scaled"), sem("kb_scaled"), sem("kb_turned")
        turned, part1, rest_made, part2, part3 = (
            sem("turned"), sem("part1"), sem("rest_made"), sem("part2"), sem("part3"))
        vk_stored = [sem(f"vk_stored{u}") for u in range(2)]
        parts_stored = [sem(f"parts_stored{u}") for u in range(2)]
        a_stored = [sem(f"a_stored{u}") for u in range(2)]
        stacks_loaded = [sem(f"stacks_loaded{u}") for u in range(2)]
        a_made, a_masked = sem("a_made"), sem("a_masked")

        block = ctx.enter_context(nc.Block())

        @block.sync
        def _(sp):
            sp.dma_start(id_sb[:, :], identity[:, :]).then_inc(consts, 16)
            sp.dma_start(w_sb[:, :, :], w.rearrange("(c p) n -> p c n", p=128)).then_inc(consts, 16)
            sp.dma_start(rope_sb[:, :, :], rope[:, :, :]).then_inc(consts, 16)
            sp.dma_start(below_sb[:, :], in_block[:, :]).then_inc(consts, 16)

            def load_x(b, u):
                reached(sp, xt_made, b - 1)
                sp.dma_start(x_sb[u][:, :], x[b]).then_inc(x_loaded[u], 16)

            def store_vk(b, u):
                sp.wait_ge(v_copied, b + 1)
                sp.wait_ge(k_scaled, b + 1)
                sp.dma_start(vk_scr[b], vk[u][:, :, :]).then_inc(vk_stored[u], 16)
                sp.wait_ge(kb_turned, b + 1)
                sp.dma_start(kb_scr[b], kbh[u][:, :, :]).then_inc(vk_stored[u], 16)

            def store_parts(b, u):
                sp.wait_ge(part3, b + 1)
                sp.dma_start(parts_scr[b].rearrange("t c (g d) h n -> (d h) (t c g) n", g=2),
                             parts[u][:, :, :, :, :]).then_inc(parts_stored[u], 16)

            def load_stacks(b, u):
                reached(sp, a_made, b - 1)
                stored(sp, parts_stored, b, u)
                load_stack(sp, kst[u], parts_scr[b, 2], Q_PARTS, True, stacks_loaded[u])
                load_stack(sp, kbst[u], parts_scr[b, 1], K_PARTS, False, stacks_loaded[u])

            def store_a(b, u):
                sp.wait_ge(a_masked, b + 1)
                sp.dma_start(a_scr[b].rearrange("h c i j -> (c i) h j"), a_sb[u][:, :, :])\
                    .then_inc(a_stored[u], 16)

            def stored(eng, pair, b, u):
                eng.wait_ge(pair[u], per_parity(b, u, 16))

            sweep(sp, [(0, load_x), (3, store_vk), (4, store_parts), (5, load_stacks), (8, store_a)])
            for u in range(2):
                sp.wait_ge(vk_stored[u], B // 2 * 32)
                sp.wait_ge(parts_stored[u], B // 2 * 16)
                sp.wait_ge(a_stored[u], B // 2 * 16)

        @block.tensor
        def _(pe):
            pe.wait_ge(consts, 64)

            def transpose_x(b, u):
                pe.wait_ge(x_loaded[u], per_parity(b, u, 16))
                reached(pe, xt_copied, b)
                reached(pe, part1, b - 2)
                reached(pe, rest_made, b - 2)
                for c in range(2):
                    last = pe.transpose(ps_xk[:, c * 128:(c + 1) * 128], x_sb[u][:, c * 128:(c + 1) * 128],
                                        id_sb[:, :])
                last.then_inc(xt_made, 1)

            def gram(b, u):
                pe.wait_ge(stacks_loaded[u], per_parity(b, u, 96))
                reached(pe, a_masked, b)
                for h in range(H):
                    for c in range(NC):
                        t = slice(c * C, (c + 1) * C)
                        last = pe.matmul(ps_a[t, h * C:(h + 1) * C], kst[u][:, h, t], kbst[u][:, h, t],
                                         start=True, stop=True)
                last.then_inc(a_made, 1)

            def transpose_qk(b, u):
                pe.wait_ge(kb_scaled, b + 1)
                reached(pe, part1, b)
                reached(pe, rest_made, b)
                at_most(pe, xt_copied, b, 3)
                k = vk[u][:, HD:2 * HD, :].rearrange("p d h -> p (d h)")
                for g in range(2):
                    half = slice(g * 128, (g + 1) * 128)
                    pe.transpose(ps_qb[:, g * 128:(g + 1) * 128], qk[u][:, half], id_sb[:, :])
                    pe.transpose(ps_qb[:, D + g * 128:D + (g + 1) * 128], kb[u][:, half], id_sb[:, :])
                    last = pe.transpose(ps_xk[:, D + g * 128:D + (g + 1) * 128], k[:, half], id_sb[:, :])
                last.then_inc(turned, 1)

            def products(b, u):
                pe.wait_ge(xt_copied, b + 1)
                reached(pe, rope_halves, b)
                reached(pe, v_copied, b)
                reached(pe, ez_made, b)
                for c in range(2):
                    pe.matmul(ps_qk[:, :], xt_sb[u][:, c, :], w_sb[:, c, 0:2 * D], start=(c == 0), stop=(c == 1))
                for c in range(2):
                    last = pe.matmul(ps_vb[:, 0:D + H], xt_sb[u][:, c, :], w_sb[:, c, 2 * D:3 * D + H],
                                     start=(c == 0), stop=(c == 1))
                last.then_inc(projected, 1)

            sweep(pe, [(0, transpose_x), (7, gram), (2, transpose_qk), (1, products)])

        @block.scalar
        def _(act):
            def copy_xt(b, u):
                act.wait_ge(xt_made, b + 1)
                reached(act, projected, b - 1)
                act.activation(xt_sb[u][:, :, :], ps_xk[:, 0:D].rearrange("p (c n) -> p c n", c=2),
                               ACT.Copy).then_inc(xt_copied, 1)

            def first_part(b, u):
                act.wait_ge(turned, b + 1)
                stored_before(act, parts_stored, b, u, 16)
                act.activation(parts[u][:, 0:2, 0, :, :],
                               ps_qb[:, :].rearrange("p (t g n) -> p t g n", t=2, g=2), ACT.Copy)
                act.activation(parts[u][:, 2, 0, :, :],
                               ps_xk[:, D:2 * D].rearrange("p (g n) -> p g n", g=2), ACT.Copy)\
                   .then_inc(part1, 1)

            def second_part(b, u):
                act.wait_ge(rest_made, b + 1)
                act.activation(parts[u][:, :, 1, :, :], rest[u][:, :, :].rearrange("p t (g n) -> p t g n", g=2),
                               ACT.Copy).then_inc(part2, 1)

            def v_and_beta(b, u):
                act.wait_ge(projected, b + 1)
                stored_before(act, vk_stored, b, u, 32)
                reached(act, norms_made, b - 1)
                act.activation(ez[u][:, :], ps_vb[:, D:D + H], ACT.Exp, scale=-1.0).then_inc(ez_made, 1)
                act.activation(vk[u][:, 0:HD, :].rearrange("p d h -> p (d h)"), ps_vb[:, 0:D],
                               ACT.Copy).then_inc(v_copied, 1)

            def turn_kb(b, u):
                act.wait_ge(kb_scaled, b + 1)
                stored_before(act, vk_stored, b, u, 32)
                act.activation(kbh[u][:, :, :], kb[u][:, :].rearrange("p (d h) -> p h d", h=H), ACT.Copy)\
                   .then_inc(kb_turned, 1)

            sweep(act, [(0, copy_xt), (2, turn_kb), (2, first_part), (1, v_and_beta), (2, second_part)])

        @block.vector
        def _(dve):
            dve.wait_ge(consts, 64)

            def mask_a(b, u):
                dve.wait_ge(a_made, b + 1)
                stored_before(dve, a_stored, b, u, 16)
                dve.tensor_tensor(a_sb[u][:, :, :], ps_a[:, :].rearrange("p (h j) -> p h j", h=H),
                                  below_sb[:, :].unsqueeze(1).broadcast_to([128, H, C]), ALU.mult)\
                   .then_inc(a_masked, 1)

            def residue(b, u):
                dve.wait_ge(part1, b + 1)
                reached(dve, part3, b - 1)
                dve.tensor_tensor(rest[u][:, 0:2, :].rearrange("p t n -> p (t n)"), ps_qb[:, :],
                                  parts[u][:, 0:2, 0, :, :], ALU.subtract)
                dve.tensor_tensor(rest[u][:, 2, :], ps_xk[:, D:2 * D], parts[u][:, 2, 0, :, :],
                                  ALU.subtract).then_inc(rest_made, 1)

            def rotate(b, u):
                dve.wait_ge(projected, b + 1)
                reached(dve, rotated, b)
                dve.tensor_tensor(with_cos[:, :], ps_qk[:, :], rope_sb[:, 0, :], ALU.mult)
                swapped = ps_qk[:, :].rearrange("p (t s m) -> p t s m", t=2, s=2)[:, :, ::-1, :]
                dve.tensor_tensor(with_sin[:, :].rearrange("p (t s m) -> p t s m", t=2, s=2), swapped,
                                  rope_sb[:, 1, :].rearrange("p (t s m) -> p t s m", t=2, s=2),
                                  ALU.mult).then_inc(rope_halves, 1)

            def norms(b, u):
                chain = Chain(dve, norm_step, b, RSQRT_LINKS + 5)
                dve.wait_ge(ez_made, b + 1)
                chain.link(dve.tensor_scalar(beta[:, :], ez[u][:, :], 0.5, 0.5, ALU.mult, ALU.add))
                reached(dve, kb_scaled, b)
                chain.link(dve.reciprocal(knorm[:, 1, :], beta[:, :]))
                dve.wait_ge(squared, b + 1)
                chain.link(dve.tensor_reduce(ss[:, :], ksq[:, :].rearrange("p (d h) -> p h d", h=H), AX.X, ALU.add))
                chain.link(dve.tensor_scalar(ss[:, :], ss[:, :], L2_EPS, None, ALU.add))
                rsqrt(dve, chain, knorm[:, 0, :], ss[:, :], tmp[:, :], bits[:, :])
                chain.link(dve.tensor_tensor(knorm[:, 1, :], knorm[:, 1, :], knorm[:, 0, :], ALU.mult))
                chain.done()
                dve.tensor_copy(tmp[:, 0:1], knorm[:, 0, 0:1]).then_inc(norms_made, 1)

            sweep(dve, [(7, mask_a), (2, residue), (1, rotate), (1, norms)])

        @block.gpsimd
        def _(pool):
            def third_part(b, u):
                pool.wait_ge(part2, b + 1)
                pool.tensor_tensor(parts[u][:, :, 2, :, :].rearrange("p t g n -> p t (g n)"), rest[u][:, :, :],
                                   parts[u][:, :, 1, :, :].rearrange("p t g n -> p t (g n)"),
                                   ALU.subtract).then_inc(part3, 1)

            def rotate_sum(b, u):
                pool.wait_ge(rope_halves, b + 1)
                reached(pool, turned, b - 1)
                pool.tensor_tensor(qk[u][:, :], with_cos[:, :], with_sin[:, :], ALU.add).then_inc(rotated, 1)
                pool.wait_ge(rotated, b + 1)
                pool.tensor_tensor(ksq[:, :], qk[u][:, D:2 * D], qk[u][:, D:2 * D], ALU.mult)\
                    .then_inc(squared, 1)

            def scale_k(b, u):
                pool.wait_ge(norms_made, b + 1)
                stored_before(pool, vk_stored, b, u, 32)
                reached(pool, turned, b - 1)
                reached(pool, kb_turned, b - 1)
                k = qk[u][:, D:2 * D].rearrange("p (d h) -> p d h", h=H)
                pool.tensor_tensor(vk[u][:, HD:2 * HD, :], k,
                                   knorm[:, 0, :].unsqueeze(1).broadcast_to([128, HD, H]),
                                   ALU.mult).then_inc(k_scaled, 1)
                pool.tensor_tensor(kb[u][:, :].rearrange("p (d h) -> p d h", h=H), k,
                                   knorm[:, 1, :].unsqueeze(1).broadcast_to([128, HD, H]),
                                   ALU.mult).then_inc(kb_scaled, 1)

            sweep(pool, [(2, third_part), (1, rotate_sum), (1, scale_k)])


def per_parity(b, u, per):
    return b * (per // 2) + (2 - u) * (per // 2)


def stored_before(eng, pair, b, u, per):
    reached(eng, pair[u], (b - u) * (per // 2))


def at_most(eng, sem, b, ahead):
    eng.wait_ge(sem, min(b + ahead, B) if isinstance(b, int) else b + ahead)


def entry(a, b):
    rest = " ".join("abcd"[:len(a.shape) - 3])
    return a[:, bass.ds(b, 1)].rearrange(f"p o n {rest} -> p (o n) {rest}")


def load_stack(eng, stack, parts, which, repeats, loaded):
    row = 0
    d = parts.shape[1]
    for part, n in which:
        src = parts[part:part + (1 if repeats else n)].rearrange("c d h n -> c d (h n)")
        if repeats:
            src = src.broadcast_to([n, d, src.shape[2]])
        else:
            src = src.rearrange("c d m -> (c d) m")
        eng.dma_start(stack[row:row + n * d, :, :].rearrange("p h n -> p (h n)"), src).then_inc(loaded, 16)
        row += n * d


def invert(nc, sems, a_scr, t_scr, dve_groups):
    groups = B * H * NC // 128
    with ExitStack() as ctx:
        ph = Phase(nc, ctx, "inv")
        sem = lambda name: sems.enter_context(nc.semaphore(f"inv_{name}"))
        shares = (("dve", 0, dve_groups), ("pool", dve_groups, groups))
        tiles = {}
        for who, first, end in shares:
            n = end - first
            tiles[who] = (ph.sb(f"a_{who}", [128, n, C, C]),
                          ph.sb(f"t_{who}", [128, n, C, C]),
                          ph.sb(f"product_{who}", [128, n, C * C]))
        a_loaded = {who: sem(f"a_loaded_{who}") for who, _, _ in shares}
        step = {who: sem(f"step_{who}") for who, _, _ in shares}
        t_stored = sem("t_stored")
        a_sys = a_scr.rearrange("(g b) h c i j -> (b h c) g (i j)", b=2)
        t_sys = t_scr.rearrange("(g b) h c j i -> (b h c) g (j i)", b=2)

        def eliminate(eng, who):
            a, t, product = tiles[who]
            n = a.shape[1]
            chain = Chain(eng, step[who], 0, 1 + C + 2 * (C - 2))
            eng.wait_ge(a_loaded[who], 16)
            chain.link(eng.tensor_copy(t[:, :, :, :].rearrange("p n j i -> p n i j"), a[:, :, :, :]))
            for j in range(C):
                chain.link(eng.memset(t[:, :, j, j:j + 1], 1.0))
            for j in range(1, C - 1):
                rows = C - 1 - j
                shape = [128, n, j, rows]
                a_col = a[:, :, j + 1:C, j].unsqueeze(2).broadcast_to(shape)
                t_row = t[:, :, 0:j, j:j + 1].broadcast_to(shape)
                part = product[:, :, 0:j * rows].rearrange("p n (c i) -> p n c i", c=j)
                chain.link(eng.tensor_tensor(part, a_col, t_row, ALU.mult))
                below = t[:, :, 0:j, j + 1:C]
                chain.link(eng.tensor_tensor(below, below, part, ALU.add))
            chain.done()

        block = ctx.enter_context(nc.Block())

        @block.sync
        def _(sp):
            for who, first, end in shares:
                sp.dma_start(tiles[who][0][:, :, :, :].rearrange("p n i j -> p n (i j)"),
                             a_sys[:, first:end]).then_inc(a_loaded[who], 16)
            for who, first, end in shares:
                sp.wait_ge(step[who], 1 + C + 2 * (C - 2))
                sp.dma_start(t_sys[:, first:end],
                             tiles[who][1][:, :, :, :].rearrange("p n j i -> p n (j i)")).then_inc(t_stored, 16)
            sp.wait_ge(t_stored, 16 * len(shares))

        @block.vector
        def _(dve):
            eliminate(dve, "dve")

        @block.gpsimd
        def _(pool):
            eliminate(pool, "pool")


def attend(nc, sems, x, wo, identity, same_head, hidden, pick_head, parts_scr, vk_scr, kb_scr, t_scr, x1_scr):
    HV = HD + 1
    G = 2
    QUADS = H // 4
    with ExitStack() as ctx:
        ph = Phase(nc, ctx, "at")
        sem = lambda name: sems.enter_context(nc.semaphore(f"at_{name}"))
        wo_sb = ph.sb("wo", [128, 2, D])
        id_sb = ph.sb("id", [128, 128])
        idb_sb = ph.sb("idb", [128, 128], BF16)
        same_sb = ph.sb("same", [128, 128])
        hidden_sb = ph.sb("hidden", [128, 2, 128], BF16)
        pick_sb = ph.sb("pick", [3 * H, H, 128], BF16)
        t_sb = ph.two("t", [128, H, C])
        vk = ph.two("vk", [128, 2 * HD, H])
        kb = ph.two("kb", [128, D])
        qst = ph.two("qst", [TERMS * HD, H, N], BF16)
        kst = ph.two("kst", [TERMS * HD, H, N], BF16)
        x_sb = ph.two("x", [128, D])
        xa = ph.two("xa", [128, H, HV])
        tk = ph.two("tk", [128, H, HD])
        tkt = ph.two("tkt", [128, G, 128])
        state = ph.sb("state", [128, G, 128])
        nmax = ph.two("nmax", [128, H])
        nmaxt = ph.two("nmaxt", [3 * H, N], BF16)
        p = ph.two("p", [128, 4, N])
        rden = ph.sb("rden", [128, H])
        o = ph.two("o", [128, D])
        ot = ph.two("ot", [128, 2, 128])
        y = ph.sb("y", [128, D])
        x1 = ph.two("x1", [128, D])
        stats, moments = ph.sb("stats", [128, 6]), ph.sb("moments", [128, 2])
        rstd, tmp, bits = ph.sb("rstd", [128, 1]), ph.sb("tmp", [128, 1]), ph.sb("bits", [128, 1], I32)
        ps_x, ps_c, ps_o, ps_w = (ph.bank(n) for n in ("x", "c", "o", "w"))
        ps_s1 = [ph.bank(f"s1{i}") for i in range(2)]
        ps_s2 = [ph.bank(f"s2{i}") for i in range(2)]
        nmaxt_ps = ps_o[0:H, 384:512]

        consts, consts_made = sem("consts"), sem("consts_made")
        tv_loaded = [sem(f"tv_loaded{u}") for u in range(2)]
        st_loaded = [sem(f"st_loaded{u}") for u in range(2)]
        x_loaded = [sem(f"x_loaded{u}") for u in range(2)]
        applied, x_copied, tk_turned, tkt_copied = (
            sem("applied"), sem("x_copied"), sem("tk_turned"), sem("tkt_copied"))
        u_made, state_made, r_made, xa_made = sem("u_made"), sem("state_made"), sem("r_made"), sem("xa_made")
        s1_made, max_made, max_turned = sem("s1_made"), sem("max_made"), sem("max_turned")
        max_hi, max_lo = sem("max_hi"), sem("max_lo")
        s2_made, exp_made, pv_made, rden_made, o_made = (
            sem("s2_made"), sem("exp_made"), sem("pv_made"), sem("rden_made"), sem("o_made"))
        o_turned, ot_copied, wo_made, norm_step, x1_made = (
            sem("o_turned"), sem("ot_copied"), sem("wo_made"), sem("norm_step"), sem("x1_made"))
        x1_stored = [sem(f"x1_stored{u}") for u in range(2)]
        STEPS = NC - 1

        block = ctx.enter_context(nc.Block())

        @block.sync
        def _(sp):
            sp.dma_start(id_sb[:, :], identity[:, :]).then_inc(consts, 16)
            sp.dma_start(wo_sb[:, :, :], wo.rearrange("(c p) n -> p c n", p=128)).then_inc(consts, 16)
            sp.dma_start(same_sb[:, :], same_head[:, :]).then_inc(consts, 16)
            sp.dma_start(hidden_sb[:, :, :], hidden[:, :, :]).then_inc(consts, 16)
            sp.dma_start(pick_sb[:, :, :], pick_head[:, :, :]).then_inc(consts, 16)

            def load_tv(b, u):
                reached(sp, applied, b - 1)
                sp.dma_start(t_sb[u][:, :, :], t_scr[b].rearrange("h c j i -> (c j) h i")).then_inc(tv_loaded[u], 16)
                sp.dma_start(vk[u][:, :, :], vk_scr[b].rearrange("p (d h) -> p d h", h=H)).then_inc(tv_loaded[u], 16)
                reached(sp, u_made, STEPS * (b - 1))
                sp.dma_start(kb[u][:, :], kb_scr[b]).then_inc(tv_loaded[u], 16)

            def load_st(b, u):
                reached(sp, s2_made, QUADS * (b - 1))
                load_stack(sp, qst[u], parts_scr[b, 0], Q_PARTS, True, st_loaded[u])
                load_stack(sp, kst[u], parts_scr[b, 1], K_PARTS, False, st_loaded[u])

            def load_x(b, u):
                reached(sp, x1_made, b - 1)
                sp.dma_start(x_sb[u][:, :], x[b]).then_inc(x_loaded[u], 16)

            def store_x1(b, u):
                sp.wait_ge(x1_made, b + 1)
                sp.dma_start(x1_scr[b], x1[u][:, :]).then_inc(x1_stored[u], 16)

            sweep(sp, [(0, load_tv), (1, load_st), (2, load_x), (5, store_x1)])
            for u in range(2):
                sp.wait_ge(x1_stored[u], B // 2 * 16)

        @block.tensor
        def _(pe):
            pe.wait_ge(consts, 80)
            pe.wait_ge(consts_made, 5)

            def apply_t(b, u):
                pe.wait_ge(tv_loaded[u], per_parity(b, u, 48))
                reached(pe, x_copied, b)
                pe.matmul(ps_x[:, 0:1], idb_sb[:, :], idb_sb[:, 0:1], start=True, stop=True)
                for h in range(H):
                    for c in range(NC):
                        t = slice(c * C, (c + 1) * C)
                        last = pe.matmul(ps_x[t, h * C:(h + 1) * C], t_sb[u][t, h, :], vk[u][t, :, h],
                                         start=True, stop=True)
                last.then_inc(applied, 1)

            def turn_tk(b, u):
                pe.wait_ge(x_copied, b + 1)
                reached(pe, xa_made, STEPS * b)
                for g in range(G):
                    last = pe.transpose(ps_c[:, D + g * 128:D + (g + 1) * 128],
                                        tk[u][:, g * 8:(g + 1) * 8, :].rearrange("p h d -> p (h d)"), id_sb[:, :])
                last.then_inc(tk_turned, 1)

            def new_state(c):
                def body(b, u):
                    if c == 1:
                        pe.wait_ge(tkt_copied, b + 1)
                    else:
                        pe.wait_ge(xa_made, STEPS * b + c - 1)
                    for g in range(G):
                        last = pe.matmul(ps_c[:, g * 128:(g + 1) * 128], kb[u][0:c * C, g * 128:(g + 1) * 128],
                                         xa[u][0:c * C, g * 8:(g + 1) * 8, 0:HD], start=True, stop=True)
                    last.then_inc(u_made, 1)
                return body

            def read_state(c):
                def body(b, u):
                    pe.wait_ge(state_made, STEPS * b + c)
                    t = slice(c * C, (c + 1) * C)
                    for g in range(G):
                        last = pe.matmul(ps_c[t, D + g * 128:D + (g + 1) * 128], tkt[u][:, g, t], state[:, g, :],
                                         start=True, stop=True)
                    last.then_inc(r_made, 1)
                return body

            def scores(ps, kind, left, right, q, extra):
                pe.matmul(ps[:, :], idb_sb[:, :], hidden_sb[:, kind, :].unsqueeze(1).broadcast_to([128, 4, 128]),
                          start=True, stop=False, skip_group_check=True)
                for j in range(4):
                    h = 4 * q + j
                    out = ps[:, j * 128:(j + 1) * 128]
                    last = pe.matmul(out, left[:, h, :], right[:, h, :], start=False, stop=extra is None,
                                     skip_group_check=True)
                    if extra is not None:
                        last = pe.matmul(out, pick_sb[:, h, :], extra, start=False, stop=True,
                                         skip_group_check=True)
                return last

            def by_query(q):
                def body(b, u):
                    if q == 0:
                        pe.wait_ge(st_loaded[u], per_parity(b, u, 96))
                    reached(pe, max_made, QUADS * b + q - 1)
                    scores(ps_s1[q % 2], 0, qst[u], kst[u], q, None).then_inc(s1_made, 1)
                return body

            def turn_max(b, u):
                pe.wait_ge(max_made, QUADS * (b + 1))
                reached(pe, o_made, b)
                pe.transpose(nmaxt_ps, nmax[u][:, :], id_sb[:, :]).then_inc(max_turned, 1)

            def by_key(q):
                def body(b, u):
                    if q == 0:
                        pe.wait_ge(max_hi, b + 1)
                        pe.wait_ge(max_lo, b + 1)
                    reached(pe, exp_made, QUADS * b + q - 1)
                    scores(ps_s2[q % 2], 1, kst[u], qst[u], q, nmaxt[u][:, :]).then_inc(s2_made, 1)
                return body

            def values(q):
                def body(b, u):
                    if q == 0:
                        pe.wait_ge(xa_made, STEPS * (b + 1))
                    pe.wait_ge(exp_made, QUADS * b + q + 1)
                    for j in range(4):
                        h = 4 * q + j
                        last = pe.matmul(ps_o[:, h * HV:(h + 1) * HV], p[q % 2][:, j, :], xa[u][:, h, :],
                                         start=True, stop=True)
                    last.then_inc(pv_made, 1)
                return body

            def turn_o(b, u):
                pe.wait_ge(o_made, b + 1)
                reached(pe, x1_made, b)
                for c in range(2):
                    last = pe.transpose(ps_w[:, c * 128:(c + 1) * 128], o[u][:, c * 128:(c + 1) * 128], id_sb[:, :])
                last.then_inc(o_turned, 1)

            def times_wo(b, u):
                pe.wait_ge(ot_copied, b + 1)
                for c in range(2):
                    last = pe.matmul(ps_w[:, D:2 * D], ot[u][:, c, :], wo_sb[:, c, :], start=(c == 0), stop=(c == 1))
                last.then_inc(wo_made, 1)

            sweep(pe, [(4, turn_o), (2, turn_tk), (3, by_query(0)), (2, new_state(1)), (4, times_wo),
                       (3, by_query(1)), (2, read_state(1)), (3, by_query(2)), (2, new_state(2)),
                       (3, by_query(3)), (2, read_state(2)), (3, turn_max), (2, new_state(3)),
                       (3, by_key(0)), (2, read_state(3)), (3, by_key(1)), (3, values(0)), (3, by_key(2)),
                       (3, values(1)), (3, by_key(3)), (3, values(2)), (1, apply_t), (3, values(3))])

        @block.scalar
        def _(act):
            act.wait_ge(consts, 80)
            act.activation(idb_sb[:, :], id_sb[:, :], ACT.Copy).then_inc(consts_made, 1)

            def copy_x(b, u):
                act.wait_ge(applied, b + 1)
                reached(act, pv_made, QUADS * (b - 1))
                reached(act, tk_turned, b - 1)
                both = ps_x[:, :].rearrange("p (h s d) -> p h s d", s=2, d=HD)
                act.activation(xa[u][:, :, 0:HD], both[:, :, 0, :], ACT.Copy)
                act.activation(tk[u][:, :, :], both[:, :, 1, :], ACT.Copy).then_inc(x_copied, 1)

            def copy_tkt(b, u):
                act.wait_ge(tk_turned, b + 1)
                reached(act, r_made, STEPS * (b - 1))
                act.activation(tkt[u][:, :, :], ps_c[:, D:2 * D].rearrange("p (g n) -> p g n", g=G), ACT.Copy)\
                   .then_inc(tkt_copied, 1)

            def max_parts(b, u):
                act.wait_ge(max_turned, b + 1)
                reached(act, s2_made, QUADS * (b - 1))
                act.activation(nmaxt[u][0:H, :], nmaxt_ps, ACT.Copy).then_inc(max_hi, 1)

            def exps(q):
                def body(b, u):
                    act.wait_ge(s2_made, QUADS * b + q + 1)
                    reached(act, pv_made, QUADS * b + q - 1)
                    act.activation(p[q % 2][:, :, :], ps_s2[q % 2][:, :].rearrange("p (h n) -> p h n", h=4),
                                   ACT.Exp).then_inc(exp_made, 1)
                return body

            def copy_ot(b, u):
                act.wait_ge(o_turned, b + 1)
                reached(act, wo_made, b - 1)
                act.activation(ot[u][:, :, :], ps_w[:, 0:D].rearrange("p (c n) -> p c n", c=2), ACT.Copy)\
                   .then_inc(ot_copied, 1)

            sweep(act, [(4, copy_ot), (2, copy_tkt), (3, max_parts)] + [(3, exps(q)) for q in range(QUADS)] + [(1, copy_x)])

        @block.vector
        def _(dve):
            for u in range(2):
                dve.memset(xa[u][:, :, HD:HV], 1.0).then_inc(consts_made, 1)
                dve.memset(nmaxt[u][:, :], 0.0).then_inc(consts_made, 1)
            dve.wait_ge(consts_made, 5)
            dve.wait_ge(consts, 80)

            def maxima(q):
                def body(b, u):
                    if q == 0:
                        reached(dve, max_turned, b - 1)
                    dve.wait_ge(s1_made, QUADS * b + q + 1)
                    dve.tensor_reduce(nmax[u][:, 4 * q:4 * q + 4], ps_s1[q % 2][:, :].rearrange("p (h k) -> p h k", h=4),
                                      AX.X, ALU.max, negate=True).then_inc(max_made, 1)
                return body

            def keep_state(c):
                def body(b, u):
                    dve.wait_ge(u_made, STEPS * b + c)
                    reached(dve, r_made, STEPS * b + c - 1)
                    dve.tensor_tensor(state[:, :, :], ps_c[:, 0:D].rearrange("p (g n) -> p g n", g=G),
                                      same_sb[:, :].unsqueeze(1).broadcast_to([128, G, 128]), ALU.mult)\
                       .then_inc(state_made, 1)
                return body

            def new_values(c):
                def body(b, u):
                    dve.wait_ge(r_made, STEPS * b + c)
                    t = slice(c * C, (c + 1) * C)
                    dve.tensor_tensor(xa[u][t, :, 0:HD], xa[u][t, :, 0:HD],
                                      ps_c[t, D:2 * D].rearrange("p (h d) -> p h d", h=H), ALU.subtract)\
                       .then_inc(xa_made, 1)
                return body

            def max_rest(b, u):
                dve.wait_ge(max_hi, b + 1)
                dve.tensor_tensor(nmaxt[u][2 * H:3 * H, :], nmaxt_ps, nmaxt[u][0:H, :], ALU.subtract)\
                   .then_inc(max_lo, 1)

            def normalise(b, u):
                dve.wait_ge(pv_made, QUADS * (b + 1))
                reached(dve, o_turned, b - 1)
                heads = ps_o[:, 0:H * HV].rearrange("p (h d) -> p h d", h=H)
                dve.reciprocal(rden[:, :].unsqueeze(2), heads[:, :, HD:HV]).then_inc(rden_made, 1)
                dve.wait_ge(rden_made, b + 1)
                dve.tensor_tensor(o[u][:, :].rearrange("p (h d) -> p h d", h=H), heads[:, :, 0:HD],
                                  rden[:, :].unsqueeze(2).broadcast_to([128, H, HD]), ALU.mult).then_inc(o_made, 1)

            def residual_norm(b, u):
                chain = Chain(dve, norm_step, b, 1 + NORM_LINKS)
                dve.wait_ge(wo_made, b + 1)
                dve.wait_ge(x_loaded[u], per_parity(b, u, 16))
                chain.link(dve.tensor_tensor(y[:, :], ps_w[:, D:2 * D], x_sb[u][:, :], ALU.add))
                layer_norm_stats(dve, chain, y[:, :], stats[:, :], moments[:, :], rstd[:, :], tmp[:, :], bits[:, :])
                chain.done()
                stored_before(dve, x1_stored, b, u, 16)
                dve.tensor_scalar(x1[u][:, :], y[:, :], moments[:, 0:1], rstd[:, 0:1], ALU.subtract, ALU.mult)\
                   .then_inc(x1_made, 1)

            sweep(dve, [(3, maxima(0)), (2, keep_state(1)), (3, maxima(1)), (2, new_values(1)), (3, maxima(2)),
                        (2, keep_state(2)), (3, maxima(3)), (2, new_values(2)), (3, max_rest), (2, keep_state(3)),
                        (2, new_values(3)), (4, residual_norm), (3, normalise)])


def cross_attend(nc, sems, x1_scr, ctx_in, mask, wq, wk, wv, bias_qk, bv, identity, pick_head, gather, parts_scr,
                 x2_scr):
    T = D
    XF = XD + 1
    SCALE = float(XD) ** -0.5
    SIDES = 2
    HALF = H // 2
    NG = H // 4
    with ExitStack() as ctx:
        ph = Phase(nc, ctx, "xa")
        sem = lambda name: sems.enter_context(nc.semaphore(f"xa_{name}"))
        w_sb = ph.sb("w", [128, 3, N])
        b_sb = ph.sb("b", [128, 2])
        bv_sb = ph.sb("bv", [128, N])
        id_sb = ph.sb("id", [128, 128])
        pick_sb = ph.sb("pick", [3 * H, H, 128], BF16)
        gather_sb = ph.sb("gather", [128, 2, 32])
        mcol_sb = ph.sb("mcol", [128, 2, B])
        m16 = ph.sb("m16", [B, SIDES, T])
        m16_rest = ph.sb("m16_rest", [B, SIDES, T])
        m16_parts = ph.sb("m16_parts", [B, SIDES, PARTS, T], BF16)
        x1 = ph.two("x1", [128, T])
        cx = ph.two("cx", [128, T])
        mrow = ph.two("mrow", [128, T])
        mq = ph.sb("mq", [128, T])
        scale_sb = ph.sb("scale", [128, 1])
        qk = ph.two("qk", [128, SIDES, T])
        rest = ph.two("rest", [128, SIDES, T])
        parts = ph.two("parts", [128, SIDES, PARTS, T], BF16)
        qst = ph.two("qst", [TERMS * XF, H, T], BF16)
        kst = ph.two("kst", [TERMS * XF, H, T], BF16)
        va = ph.two("va", [128, 2, H, 32])
        vb = ph.sb("vb", [128, 2, N])
        nmax = ph.two("nmax", [128, 2, H])
        nmaxt = ph.two("nmaxt", [3 * H, T], BF16)
        p = ph.two("p", [128, 2, T])
        r = ph.two("r", [128, T])
        rden = ph.sb("rden", [128, T])
        o = ph.two("o", [128, T])
        y = ph.two("y", [128, T])
        cv = ph.two("cv", [128, T])
        x1r = ph.two("x1r", [128, T])
        mr = ph.two("mr", [128, T])
        x2 = ph.two("x2", [128, T])
        stats, moments = ph.sb("stats", [128, 6]), ph.sb("moments", [128, 2])
        rstd, tmp, bits = ph.sb("rstd", [128, 1]), ph.sb("tmp", [128, 1]), ph.sb("bits", [128, 1], I32)
        ps_a, ps_n = ph.bank("projections"), ph.bank("gathered")
        ps_s1 = [ph.bank(f"s1{i}") for i in range(2)]
        ps_s2 = [ph.bank(f"s2{i}") for i in range(2)]
        ps_r = [ph.bank(f"group{i}") for i in range(2)]
        nmaxt_ps = ps_a[0:H, 0:T]

        consts, made, m_step, m_part = sem("consts"), sem("made"), sem("m_step"), sem("m_part")
        m_stored = sem("m_stored")
        in_loaded = [sem(f"in_loaded{u}") for u in range(2)]
        qk_made, mq_made, qk_masked, part1, rest_made, part2, part3 = (
            sem(n) for n in ("qk_made", "mq_made", "qk_masked", "part1", "rest_made", "part2", "part3"))
        v_made, vb_made, v_masked = sem("v_made"), sem("vb_made"), sem("v_masked")
        parts_stored = [sem(f"parts_stored{u}") for u in range(2)]
        st_loaded = [[sem(f"st_loaded{u}{i}") for i in range(2)] for u in range(2)]
        s1_made, max_made, max_turned, max_hi, max_lo = (
            sem(n) for n in ("s1_made", "max_made", "max_turned", "max_hi", "max_lo"))
        s2_made, exp_made, pv_made, r_copied, gathered = (
            sem(n) for n in ("s2_made", "exp_made", "pv_made", "r_copied", "gathered"))
        rden_made, o_made, o_masked, y_made, norm_step, x2_made = (
            sem(n) for n in ("rden_made", "o_made", "o_masked", "y_made", "norm_step", "x2_made"))
        cv_loaded = [sem(f"cv_loaded{u}") for u in range(2)]
        res_loaded = [sem(f"res_loaded{u}") for u in range(2)]
        x2_stored = [sem(f"x2_stored{u}") for u in range(2)]
        mcol_turned, scale_made = sem("mcol_turned"), sem("scale_made")
        MADE = 5
        LAG = 5

        block = ctx.enter_context(nc.Block())

        @block.sync
        def _(sp):
            for side in range(SIDES):
                sp.dma_start(m16[:, side, :], mask.rearrange("b a t -> (b a) t")).then_inc(consts, 16)
            sp.dma_start(id_sb[:, :], identity[:, :]).then_inc(consts, 16)
            for n, w in enumerate((wq, wk, wv)):
                sp.dma_start(w_sb[:, n, :], w[:, :]).then_inc(consts, 16)
            sp.dma_start(b_sb[:, :], bias_qk[:, :]).then_inc(consts, 16)
            sp.dma_start(bv_sb[:, :], bv.partition_broadcast(128)).then_inc(consts, 16)
            sp.dma_start(pick_sb[:, :, :], pick_head[:, :, :]).then_inc(consts, 16)
            sp.dma_start(gather_sb[:, :, :], gather[:, :, :]).then_inc(consts, 16)
            sp.wait_ge(m_part, 3 * 1)
            for side in range(SIDES):
                for part in range(PARTS):
                    sp.dma_start(parts_scr[:, side, part, XD],
                                 m16_parts[:, side, part, :].unsqueeze(1).broadcast_to([B, H, T])).then_inc(m_stored, 16)

            def load_in(b, u):
                reached(sp, qk_masked, b - 1)
                sp.dma_start(x1[u][:, :], x1_scr[b]).then_inc(in_loaded[u], 16)
                sp.dma_start(cx[u][:, :], ctx_in[b]).then_inc(in_loaded[u], 16)
                sp.dma_start(mrow[u][:, :], mask[b, 0].partition_broadcast(128)).then_inc(in_loaded[u], 16)

            def store_parts(b, u):
                sp.wait_ge(part3, b + 1)
                sp.dma_start(parts_scr[b].rearrange("s c f h t -> s c (f h) t")[:, :, 0:XD * H]
                             .rearrange("s c m t -> m (s c) t"),
                             parts[u][:, :, :, :].rearrange("p s c t -> p (s c) t")).then_inc(parts_stored[u], 16)

            def load_stacks(half):
                heads = slice(half * HALF, (half + 1) * HALF)

                def body(b, u):
                    if half == 0:
                        if isinstance(b, int) and b == 0:
                            sp.wait_ge(m_stored, 16 * SIDES * PARTS)
                        sp.wait_ge(parts_stored[u], per_parity(b, u, 16))
                    reached(sp, s2_made, H * (b - 2) + (half + 1) * HALF)
                    for side, stack, which in ((0, qst, Q_PARTS), (1, kst, K_PARTS)):
                        load_stack(sp, stack[u][:, heads, :], parts_scr[b, side][:, :, heads, :], which, side == 0,
                                   st_loaded[u][half])
                return body

            def load_cv(b, u):
                reached(sp, v_made, b - 1)
                sp.dma_start(cv[u][:, :], ctx_in[b]).then_inc(cv_loaded[u], 16)

            def load_residual(b, u):
                reached(sp, y_made, b - 1)
                sp.dma_start(x1r[u][:, :], x1_scr[b]).then_inc(res_loaded[u], 16)
                sp.dma_start(mr[u][:, :], mask[b, 0].partition_broadcast(128)).then_inc(res_loaded[u], 16)

            def store_x2(b, u):
                sp.wait_ge(x2_made, b + 1)
                sp.dma_start(x2_scr[b], x2[u][:, :]).then_inc(x2_stored[u], 16)

            sweep(sp, [(0, load_in), (3, store_parts), (LAG - 1, load_stacks(0)), (LAG - 1, load_stacks(1)),
                       (LAG - 1, load_cv), (LAG, load_residual), (LAG + 3, store_x2)])
            for u in range(2):
                sp.wait_ge(x2_stored[u], B // 2 * 16)

        @block.tensor
        def _(pe):
            pe.wait_ge(consts, 16 * 10)
            for c in range(2):
                last = pe.transpose(ps_n[:, c * B:(c + 1) * B], m16[:, 0, c * 128:(c + 1) * 128], id_sb[0:B, 0:B])
            last.then_inc(mcol_turned, 1)
            pe.wait_ge(made, MADE)

            def project_qk(b, u):
                pe.wait_ge(in_loaded[u], per_parity(b, u, 48))
                reached(pe, qk_masked, b)
                reached(pe, max_lo, b - LAG + 1)
                pe.matmul(ps_a[:, 0:T], w_sb[:, 0, :], x1[u][:, :], start=True, stop=True)
                pe.matmul(ps_a[:, T:2 * T], w_sb[:, 1, :], cx[u][:, :], start=True, stop=True).then_inc(qk_made, 1)

            def project_v(b, u):
                pe.wait_ge(cv_loaded[u], per_parity(b, u, 16))
                at_most(pe, qk_masked, b, LAG)
                reached(pe, max_lo, b)
                for c in range(2):
                    last = pe.matmul(ps_a[:, c * N:(c + 1) * N], cv[u][:, c * 128:(c + 1) * 128], w_sb[:, 2, :],
                                     start=True, stop=True)
                last.then_inc(v_made, 1)

            def by_query(h):
                def body(b, u):
                    if h % HALF == 0:
                        pe.wait_ge(st_loaded[u][h // HALF], per_parity(b, u, 96))
                    reached(pe, max_made, H * b + h - 1)
                    for c in range(2):
                        last = pe.matmul(ps_s1[h % 2][:, c * T:(c + 1) * T], qst[u][:, h, c * 128:(c + 1) * 128],
                                         kst[u][:, h, :], start=True, stop=True)
                    last.then_inc(s1_made, 1)
                return body

            def turn_max(b, u):
                pe.wait_ge(max_made, H * (b + 1))
                pe.wait_ge(v_masked, b + 1)
                for c in range(2):
                    last = pe.transpose(ps_a[0:H, c * 128:(c + 1) * 128], nmax[u][:, c, :], id_sb[:, :])
                last.then_inc(max_turned, 1)

            def by_key(h):
                def body(b, u):
                    if h == 0:
                        pe.wait_ge(max_hi, b + 1)
                        pe.wait_ge(max_lo, b + 1)
                    reached(pe, exp_made, H * b + h - 1)
                    ps = ps_s2[h % 2]
                    pe.matmul(ps[:, :], pick_sb[:, h, :], nmaxt[u][:, :].unsqueeze(1).broadcast_to([3 * H, 2, T]),
                              start=True, stop=False, skip_group_check=True)
                    for c in range(2):
                        last = pe.matmul(ps[:, c * T:(c + 1) * T], kst[u][:, h, c * 128:(c + 1) * 128],
                                         qst[u][:, h, :], start=False, stop=True, skip_group_check=True)
                    last.then_inc(s2_made, 1)
                return body

            def values(h):
                def body(b, u):
                    g, j = h // 4, h % 4
                    if h == 0:
                        pe.wait_ge(v_masked, b + 1)
                    if j == 0:
                        reached(pe, r_copied, NG * b + g - 1)
                    pe.wait_ge(exp_made, H * b + h + 1)
                    for c in range(2):
                        last = pe.matmul(ps_r[g % 2][32 * j:32 * j + 32, 0:T], va[u][:, c, h, :], p[h % 2][:, c, :],
                                         start=(c == 0), stop=(c == 1))
                    last.then_inc(pv_made, 1)
                return body

            def gather_group(g):
                def body(b, u):
                    pe.wait_ge(r_copied, NG * b + g + 1)
                    if g == 0:
                        reached(pe, o_made, b)
                    for n in range(2):
                        last = pe.matmul(ps_n[32 * g:32 * g + 32, n * T:(n + 1) * T], gather_sb[:, n, :], r[g % 2][:, :],
                                         start=True, stop=True)
                    last.then_inc(gathered, 1)
                return body

            stages = []
            for h in range(H):
                stages.append((LAG, by_query(h)))
                stages.append((LAG + 1, by_key(h)))
                if h:
                    stages.append((LAG + 1, values(h - 1)))
                if h % 4 == 2 and h > 4:
                    stages.append((LAG + 1, gather_group(h // 4 - 1)))
                if h == 3:
                    stages.append((1, project_qk))
                if h == 8:
                    stages.append((LAG, project_v))
            stages += [(LAG + 1, values(H - 1)), (LAG, turn_max), (LAG + 1, gather_group(NG - 1))]
            sweep(pe, stages)

        @block.scalar
        def _(act):
            act.wait_ge(mcol_turned, 1)
            act.activation(mcol_sb[:, :, :], ps_n[:, 0:2 * B].rearrange("p (c b) -> p c b", c=2), ACT.Copy)\
               .then_inc(made, 1)

            def first_part(b, u):
                act.wait_ge(qk_masked, b + 1)
                stored_before(act, parts_stored, b, u, 16)
                act.activation(parts[u][:, :, 0, :], qk[u][:, :, :], ACT.Copy).then_inc(part1, 1)

            def second_part(b, u):
                act.wait_ge(rest_made, b + 1)
                act.activation(parts[u][:, :, 1, :], rest[u][:, :, :], ACT.Copy).then_inc(part2, 1)

            def max_parts(b, u):
                act.wait_ge(max_turned, b + 1)
                reached(act, s2_made, H * (b - 1))
                act.activation(nmaxt[u][0:H, :], nmaxt_ps, ACT.Copy).then_inc(max_hi, 1)

            def exps(h):
                def body(b, u):
                    act.wait_ge(s2_made, H * b + h + 1)
                    reached(act, pv_made, H * b + h - 1)
                    act.activation(p[h % 2][:, :, :], ps_s2[h % 2][:, :].rearrange("p (c t) -> p c t", c=2), ACT.Exp)\
                       .then_inc(exp_made, 1)
                return body

            def copy_r(g):
                def body(b, u):
                    act.wait_ge(pv_made, H * b + 4 * g + 4)
                    reached(act, gathered, NG * b + g - 1)
                    act.activation(r[g % 2][:, :], ps_r[g % 2][:, 0:T], ACT.Copy).then_inc(r_copied, 1)
                return body

            stages = []
            for h in range(H):
                stages.append((LAG + 1, exps(h)))
                if h % 4 == 1 and h > 4:
                    stages.append((LAG + 1, copy_r(h // 4 - 1)))
                if h == 2:
                    stages.append((2, second_part))
                if h == 10:
                    stages.append((1, first_part))
            stages += [(LAG + 1, copy_r(NG - 1)), (LAG, max_parts)]
            sweep(act, stages)

        @block.vector
        def _(dve):
            for u in range(2):
                dve.memset(va[u][:, :, :, :], 0.0).then_inc(m_step, 1)
                dve.memset(nmaxt[u][:, :], 0.0).then_inc(made, 1)
            dve.wait_ge(m_step, 2)
            for u in range(2):
                dve.memset(va[u][:, :, :, XD:XD + 1], 1.0).then_inc(made, 1)
            dve.wait_ge(consts, 16 * 10)
            dve.tensor_scalar(m16[:, 1, :], m16[:, 1, :], 1.0, NEG, ALU.subtract, ALU.mult).then_inc(m_step, 1)
            dve.wait_ge(m_step, 3)
            dve.tensor_copy(m16_parts[:, :, 0, :], m16[:, :, :]).then_inc(m_part, 1)
            dve.wait_ge(m_part, 1)
            dve.tensor_tensor(m16_rest[:, :, :], m16[:, :, :], m16_parts[:, :, 0, :], ALU.subtract).then_inc(m_step, 1)
            dve.wait_ge(m_step, 4)
            dve.tensor_copy(m16_parts[:, :, 1, :], m16_rest[:, :, :]).then_inc(m_part, 1)
            dve.wait_ge(m_part, 2)
            dve.tensor_tensor(m16_parts[:, :, 2, :], m16_rest[:, :, :], m16_parts[:, :, 1, :],
                              ALU.subtract).then_inc(m_part, 1)
            dve.wait_ge(made, MADE)

            def mask_qk(b, u):
                dve.wait_ge(qk_made, b + 1)
                dve.wait_ge(mq_made, b + 1)
                reached(dve, rest_made, b - 1)
                dve.scalar_tensor_tensor(qk[u][:, 0, :], ps_a[:, 0:T], b_sb[:, 0:1], mq[:, :], ALU.add, ALU.mult)
                dve.scalar_tensor_tensor(qk[u][:, 1, :], ps_a[:, T:2 * T], b_sb[:, 1:2], mrow[u][:, :], ALU.add,
                                         ALU.mult).then_inc(qk_masked, 1)

            def mask_v(b, u):
                dve.wait_ge(v_made, b + 1)
                dve.tensor_tensor(vb[:, :, :], ps_a[:, 0:2 * N].rearrange("p (c n) -> p c n", c=2),
                                  bv_sb[:, :].unsqueeze(1).broadcast_to([128, 2, N]), ALU.add).then_inc(vb_made, 1)
                dve.wait_ge(vb_made, b + 1)
                reached(dve, pv_made, H * (b - 1))
                for c in range(2):
                    ins = dve.tensor_scalar(va[u][:, c, :, 0:XD], vb[:, c, :].rearrange("p (h d) -> p h d", h=H),
                                            mcol_sb[:, c, bass.ds(b, 1)] if not isinstance(b, int) else
                                            mcol_sb[:, c, b:b + 1], None, ALU.mult)
                ins.then_inc(v_masked, 1)

            def maximum(h):
                def body(b, u):
                    if h == 0:
                        reached(dve, max_turned, b - 1)
                    dve.wait_ge(s1_made, H * b + h + 1)
                    dve.tensor_reduce(nmax[u][:, :, h], ps_s1[h % 2][:, :].rearrange("p (c s) -> p c s", c=2),
                                      AX.X, ALU.max, negate=True).then_inc(max_made, 1)
                return body

            def max_rest(b, u):
                dve.wait_ge(max_hi, b + 1)
                dve.tensor_tensor(nmaxt[u][2 * H:3 * H, :], nmaxt_ps, nmaxt[u][0:H, :], ALU.subtract)\
                   .then_inc(max_lo, 1)

            def normalise(b, u):
                dve.wait_ge(gathered, NG * (b + 1))
                dve.reciprocal(rden[:, :], ps_n[:, T:2 * T]).then_inc(rden_made, 1)
                dve.wait_ge(rden_made, b + 1)
                reached(dve, o_masked, b - 1)
                dve.tensor_tensor(o[u][:, :], ps_n[:, 0:T], rden[:, :], ALU.mult).then_inc(o_made, 1)

            def norm(b, u):
                chain = Chain(dve, norm_step, b, NORM_LINKS)
                dve.wait_ge(y_made, b + 1)
                layer_norm_stats(dve, chain, y[u][:, :], stats[:, :], moments[:, :], rstd[:, :], tmp[:, :], bits[:, :])
                chain.done()
                stored_before(dve, x2_stored, b, u, 16)
                dve.tensor_scalar(x2[u][:, :], y[u][:, :], moments[:, 0:1], rstd[:, 0:1], ALU.subtract, ALU.mult)\
                   .then_inc(x2_made, 1)

            stages = []
            for h in range(H):
                stages.append((LAG, maximum(h)))
                if h == 1:
                    stages.append((LAG + 2, normalise))
                if h == 5:
                    stages.append((LAG + 2, norm))
                if h == 7:
                    stages.append((1, mask_qk))
                if h == 12:
                    stages.append((LAG, mask_v))
            stages.append((LAG, max_rest))
            sweep(dve, stages)

        @block.gpsimd
        def _(pool):
            pool.memset(scale_sb[:, :], SCALE).then_inc(scale_made, 1)
            pool.wait_ge(scale_made, 1)

            def scale_mask(b, u):
                pool.wait_ge(in_loaded[u], per_parity(b, u, 48))
                reached(pool, qk_masked, b)
                pool.tensor_tensor(mq[:, :], mrow[u][:, :], scale_sb[:, :].broadcast_to([128, T]), ALU.mult).then_inc(mq_made, 1)

            def residue(b, u):
                pool.wait_ge(part1, b + 1)
                reached(pool, part3, b - 1)
                pool.tensor_tensor(rest[u][:, :, :], qk[u][:, :, :], parts[u][:, :, 0, :], ALU.subtract)\
                    .then_inc(rest_made, 1)

            def third_part(b, u):
                pool.wait_ge(part2, b + 1)
                pool.tensor_tensor(parts[u][:, :, 2, :], rest[u][:, :, :], parts[u][:, :, 1, :], ALU.subtract)\
                    .then_inc(part3, 1)

            def add_residual(b, u):
                pool.wait_ge(o_made, b + 1)
                pool.wait_ge(res_loaded[u], per_parity(b, u, 32))
                pool.tensor_tensor(o[u][:, :], o[u][:, :], mr[u][:, :], ALU.mult).then_inc(o_masked, 1)
                pool.wait_ge(o_masked, b + 1)
                reached(pool, x2_made, b - 1)
                pool.tensor_tensor(y[u][:, :], o[u][:, :], x1r[u][:, :], ALU.add).then_inc(y_made, 1)

            sweep(pool, [(1, scale_mask), (LAG + 2, add_residual), (2, third_part), (1, residue)])


def feed_forward(nc, sems, x2_scr, router_w, router_b, expert_w, expert_b, out_w, out_b, identity, expert_ids,
                 bias_scr, out):
    TOP = 2
    PAIRS = E // 2
    ROWS = (E + 1) * D // 128
    with ExitStack() as ctx:
        ph = Phase(nc, ctx, "ff")
        sem = lambda name: sems.enter_context(nc.semaphore(f"ff_{name}"))
        id_sb = ph.sb("id", [128, 128])
        rw_sb = ph.sb("rw", [128, 2, E])
        rb_sb = ph.sb("rb", [128, E])
        ids_sb = ph.sb("ids", [128, E])
        ew_sb = ph.sb("ew", [128, 2, E, D])
        ow_sb = ph.sb("ow", [128, 2, D])
        bias = ph.sb("bias", [ROWS, 128])
        bias_rest = ph.sb("bias_rest", [ROWS, 128])
        bias_parts = ph.sb("bias_parts", [ROWS, PARTS, 128], BF16)
        bias_sb = ph.sb("bias_stack", [PARTS, (E + 1) * D], BF16)
        ones = ph.sb("ones", [PARTS, 128], BF16)
        x2_sb = ph.two("x2", [128, D])
        x2_all = ph.sb("x2_all", [128, B, D])
        xt_all = ph.sb("xt_all", [128, B, 2, 128])
        xt = ph.two("xt", [128, 2, 128])
        probs = ph.sb("probs", [128, B, E])
        row = ph.sb("row", [128, B])
        row_inv = ph.sb("row_inv", [128, B])
        best = ph.sb("best", [128, B, 8])
        best_at = ph.sb("best_at", [128, B, 8], U32)
        at = ph.sb("at", [128, TOP, B])
        share = ph.sb("share", [128, TOP, B])
        chosen = ph.sb("chosen", [128, TOP, B, E])
        gates = ph.sb("gates", [128, B, E])
        ge = ph.two("gelu", [128, E, D])
        comb = ph.two("comb", [128, D])
        combt = ph.two("combt", [128, 2, 128])
        y = ph.sb("y", [128, D])
        res = ph.two("out", [128, D])
        stats, moments = ph.sb("stats", [128, 6]), ph.sb("moments", [128, 2])
        rstd, tmp, bits = ph.sb("rstd", [128, 1]), ph.sb("tmp", [128, 1]), ph.sb("bits", [128, 1], I32)
        ps_t = [ph.bank(f"t{i}") for i in range(2)]
        ps_c, ps_o = ps_t
        ps_l = ph.bank("logits")
        ps_e = [ph.bank(f"e{i}") for i in range(PAIRS)]

        consts, weights, b_step, b_stored, b_loaded = (
            sem(n) for n in ("consts", "weights", "b_step", "b_stored", "b_loaded"))
        xt_made, xt_copied, logits_made, logits_less_max, exps_made, gate_step, gates_made = (
            sem(n) for n in ("xt_made", "xt_copied", "logits_made", "logits_less_max", "exps_made", "gate_step",
                             "gates_made"))
        expert_made, gelu_made, comb_step, combined, comb_turned, comb_copied, out_made, norm_step, normed = (
            sem(n) for n in ("expert_made", "gelu_made", "comb_step", "combined", "comb_turned", "comb_copied",
                             "out_made", "norm_step", "normed"))
        x2_loaded = [sem(f"x2_loaded{u}") for u in range(2)]
        xt_moved = sem("xt_moved")
        out_stored = [sem(f"out_stored{u}") for u in range(2)]

        block = ctx.enter_context(nc.Block())

        @block.sync
        def _(sp):
            sp.dma_start(id_sb[:, :], identity[:, :]).then_inc(consts, 16)

            def load_x2(b, u):
                reached(sp, xt_made, b - 1)
                sp.dma_start(x2_sb[u][:, :], x2_scr[b]).then_inc(x2_loaded[u], 16)

            sp.dma_start(rw_sb[:, :, :], router_w.rearrange("(c p) e -> p c e", p=128)).then_inc(consts, 16)
            sp.dma_start(rb_sb[:, :], router_b.partition_broadcast(128)).then_inc(consts, 16)
            sp.dma_start(ids_sb[:, :], expert_ids.partition_broadcast(128)).then_inc(consts, 16)
            sp.dma_start(bias[0:ROWS - 2, :], expert_b.rearrange("e (r n) -> (e r) n", n=128)).then_inc(consts, 16)
            sp.dma_start(bias[ROWS - 2:ROWS, :], out_b.rearrange("(r n) -> r n", n=128)).then_inc(consts, 16)
            for c in range(2):
                sp.dma_start(ew_sb[:, c, :, :], expert_w[:, c * 128:(c + 1) * 128, :].rearrange("e p d -> p e d"))\
                    .then_inc(weights, 16)
            sp.dma_start(ow_sb[:, :, :], out_w.rearrange("(c p) n -> p c n", p=128)).then_inc(weights, 16)
            sp.dma_start(x2_all[:, :, :], x2_scr.rearrange("b p d -> p b d")).then_inc(weights, 16)
            sweep(sp, [(0, load_x2)])
            sp.wait_ge(b_step, 6)
            sp.dma_start(bias_scr.rearrange("c (r n) -> r c n", n=128), bias_parts[:, :, :]).then_inc(b_stored, 16)
            sp.wait_ge(b_stored, 16)
            sp.dma_start(bias_sb[:, :], bias_scr[:, :]).then_inc(b_loaded, 16)

            def store_out(b, u):
                sp.wait_ge(normed, b + 1)
                sp.dma_start(out[b], res[u][:, :]).then_inc(out_stored[u], 16)

            sweep(sp, [(3, store_out)])
            for u in range(2):
                sp.wait_ge(out_stored[u], B // 2 * 16)

        @block.tensor
        def _(pe):
            pe.wait_ge(consts, 16 * 6)

            def turn_x2(b, u):
                pe.wait_ge(x2_loaded[u], per_parity(b, u, 16))
                reached(pe, xt_copied, b - 1)
                for c in range(2):
                    last = pe.transpose(ps_t[u][:, c * 128:(c + 1) * 128], x2_sb[u][:, c * 128:(c + 1) * 128],
                                        id_sb[:, :])
                last.then_inc(xt_made, 1)

            def logits(b, u):
                pe.wait_ge(xt_moved, b + 1)
                for c in range(2):
                    last = pe.matmul(ps_l[:, bass.ds(b * E, E)], xt[u][:, c, :], rw_sb[:, c, :],
                                     start=(c == 0), stop=(c == 1))
                last.then_inc(logits_made, 1)

            sweep(pe, [(0, turn_x2), (1, logits)])
            pe.wait_ge(weights, 64)
            pe.wait_ge(b_loaded, 16)

            def expert(j):
                def body(b, u):
                    if j == 0:
                        pe.wait_ge(xt_moved, B + b + 1)
                    reached(pe, gelu_made, PAIRS * (b - 1) + j + 1)
                    pe.matmul(ps_e[j][:, :], ones[:, :], bias_sb[:, 2 * j * D:2 * (j + 1) * D], start=True, stop=False)
                    for c in range(2):
                        last = pe.matmul(ps_e[j][:, :], xt[u][:, c, :],
                                         ew_sb[:, c, 2 * j:2 * j + 2, :].rearrange("p e d -> p (e d)"),
                                         start=False, stop=(c == 1))
                    last.then_inc(expert_made, 1)
                return body

            def turn_comb(b, u):
                pe.wait_ge(combined, b + 1)
                reached(pe, comb_copied, b)
                for c in range(2):
                    last = pe.transpose(ps_c[:, c * 128:(c + 1) * 128], comb[u][:, c * 128:(c + 1) * 128], id_sb[:, :])
                last.then_inc(comb_turned, 1)

            def output(b, u):
                pe.wait_ge(comb_copied, b + 1)
                reached(pe, norm_step, (1 + NORM_LINKS) * (b - 1) + 1)
                pe.matmul(ps_o[:, 0:D], ones[:, :], bias_sb[:, E * D:], start=True, stop=False)
                for c in range(2):
                    last = pe.matmul(ps_o[:, 0:D], combt[u][:, c, :], ow_sb[:, c, :], start=False, stop=(c == 1))
                last.then_inc(out_made, 1)

            sweep(pe, [(0, expert(0)), (0, expert(1)), (1, turn_comb), (0, expert(2)), (1, output), (0, expert(3))])

        @block.scalar
        def _(act):
            def copy_xt(b, u):
                act.wait_ge(xt_made, b + 1)
                act.activation(entry(xt_all, b), ps_t[u][:, 0:D].rearrange("p (c n) -> p c n", c=2), ACT.Copy)\
                   .then_inc(xt_copied, 1)

            sweep(act, [(0, copy_xt)])
            act.wait_ge(logits_less_max, 1)
            act.activation(probs[:, :, :], probs[:, :, :], ACT.Exp).then_inc(exps_made, 1)

            def gelus(j):
                def body(b, u):
                    act.wait_ge(expert_made, PAIRS * b + j + 1)
                    if j == 0:
                        reached(act, combined, b - 1)
                    act.activation(ge[u][:, 2 * j:2 * j + 2, :], ps_e[j][:, :].rearrange("p (e d) -> p e d", e=2),
                                   ACT.Gelu_apprx_tanh).then_inc(gelu_made, 1)
                return body

            def copy_combt(b, u):
                act.wait_ge(comb_turned, b + 1)
                reached(act, out_made, b - 1)
                act.activation(combt[u][:, :, :], ps_c[:, 0:D].rearrange("p (c n) -> p c n", c=2), ACT.Copy)\
                   .then_inc(comb_copied, 1)

            sweep(act, [(0, gelus(0)), (0, gelus(1)), (1, copy_combt), (0, gelus(2)), (0, gelus(3))])

        @block.vector
        def _(dve):
            dve.wait_ge(consts, 16 * 6)
            dve.memset(ones[:, :], 1.0).then_inc(b_step, 1)
            chain = Chain(dve, b_step, 0, 0)
            chain.n = 1
            chain.link(dve.tensor_copy(bias_parts[:, 0, :], bias[:, :]))
            chain.link(dve.tensor_tensor(bias_rest[:, :], bias[:, :], bias_parts[:, 0, :], ALU.subtract))
            chain.link(dve.tensor_copy(bias_parts[:, 1, :], bias_rest[:, :]))
            chain.link(dve.tensor_tensor(bias_rest[:, :], bias_rest[:, :], bias_parts[:, 1, :], ALU.subtract))
            chain.link(dve.tensor_copy(bias_parts[:, 2, :], bias_rest[:, :]))

            def by_expert(a):
                return a.unsqueeze(len(a.shape)).broadcast_to([*a.shape, E])

            chain = Chain(dve, gate_step, 0, 0)
            dve.wait_ge(logits_made, B)
            chain.link(dve.tensor_tensor(probs[:, :, :], ps_l[:, 0:B * E].rearrange("p (b e) -> p b e", e=E),
                                         rb_sb[:, :].unsqueeze(1).broadcast_to([128, B, E]), ALU.add))
            chain.link(dve.tensor_reduce(row[:, :], probs[:, :, :], AX.X, ALU.max))
            chain.link(dve.tensor_tensor(probs[:, :, :], probs[:, :, :], by_expert(row[:, :]), ALU.subtract))
            dve.tensor_copy(row_inv[:, :], row[:, :]).then_inc(logits_less_max, 1)
            dve.wait_ge(exps_made, 1)
            chain.link(dve.tensor_reduce(row[:, :], probs[:, :, :], AX.X, ALU.add))
            dve.wait_ge(logits_less_max, 1)
            chain.link(dve.reciprocal(row_inv[:, :], row[:, :]))
            chain.link(dve.tensor_tensor(probs[:, :, :], probs[:, :, :], by_expert(row_inv[:, :]), ALU.mult))
            for b in range(B):
                dve.max(best[:, b, :], probs[:, b, :]).then_inc(gate_step, 1)
                chain.n += 1
            dve.wait_ge(gate_step, chain.n)
            for b in range(B):
                dve.max_index(best_at[:, b, :], best[:, b, :], probs[:, b, :]).then_inc(gate_step, 1)
                chain.n += 1
            dve.wait_ge(gate_step, chain.n)
            chain.link(dve.tensor_tensor(row[:, :], best[:, :, 0], best[:, :, 1], ALU.add))
            chain.link(dve.reciprocal(row_inv[:, :], row[:, :]))
            chain.link(dve.tensor_tensor(share[:, :, :], best[:, :, 0:TOP].rearrange("p b k -> p k b"),
                                         row_inv[:, :].unsqueeze(1).broadcast_to([128, TOP, B]), ALU.mult))
            chain.link(dve.tensor_copy(at[:, :, :], best_at[:, :, 0:TOP].rearrange("p b k -> p k b")))
            for k in range(TOP):
                chain.link(dve.tensor_tensor(chosen[:, k, :, :], ids_sb[:, :].unsqueeze(1).broadcast_to([128, B, E]),
                                             by_expert(at[:, k, :]), ALU.is_equal))
                chain.link(dve.tensor_tensor(chosen[:, k, :, :], chosen[:, k, :, :], by_expert(share[:, k, :]), ALU.mult))
            dve.tensor_tensor(gates[:, :, :], chosen[:, 0, :, :], chosen[:, 1, :, :], ALU.add).then_inc(gates_made, 1)
            dve.wait_ge(gates_made, 1)

            def combine(half):
                def body(b, u):
                    chain = Chain(dve, comb_step, b, E - 1)
                    chain.n = half * E // 2
                    for e in range(half * E // 2, (half + 1) * E // 2):
                        if e % 2 == 0:
                            dve.wait_ge(gelu_made, PAIRS * b + e // 2 + 1)
                        gate = entry(gates, b)[:, e:e + 1]
                        if e == 0:
                            reached(dve, comb_turned, b - 1)
                            ins = dve.tensor_scalar(comb[u][:, :], ge[u][:, e, :], gate, None, ALU.mult)
                        else:
                            ins = dve.scalar_tensor_tensor(comb[u][:, :], ge[u][:, e, :], gate, comb[u][:, :], ALU.mult,
                                                           ALU.add)
                        if e == E - 1:
                            ins.then_inc(combined, 1)
                            dve.wait_ge(combined, b + 1)
                        else:
                            chain.link(ins)
                return body

            def residual_norm(b, u):
                chain = Chain(dve, norm_step, b, 1 + NORM_LINKS)
                dve.wait_ge(out_made, b + 1)
                reached(dve, normed, b)
                chain.link(dve.tensor_tensor(y[:, :], ps_o[:, 0:D], entry(x2_all, b), ALU.add))
                layer_norm_stats(dve, chain, y[:, :], stats[:, :], moments[:, :], rstd[:, :], tmp[:, :], bits[:, :])
                chain.done()
                stored_before(dve, out_stored, b, u, 16)
                dve.tensor_scalar(res[u][:, :], y[:, :], moments[:, 0:1], rstd[:, 0:1], ALU.subtract, ALU.mult)\
                   .then_inc(normed, 1)

            sweep(dve, [(0, combine(0)), (2, residual_norm), (0, combine(1))])

        @block.gpsimd
        def _(pool):
            def move_xt(first):
                def body(b, u):
                    if first:
                        pool.wait_ge(xt_copied, b + 1)
                        reached(pool, logits_made, b - 1)
                    else:
                        reached(pool, logits_made, B)
                        reached(pool, expert_made, PAIRS * (b - 1))
                    pool.tensor_copy(xt[u][:, :, :], entry(xt_all, b)).then_inc(xt_moved, 1)
                return body

            sweep(pool, [(0, move_xt(True))])
            sweep(pool, [(0, move_xt(False))])


def decoder_layer(nc, x, ctx_in, mask, attn_w, attn_wo, xattn_wq, xattn_wk, xattn_wv, xattn_bias_qk, xattn_bv,
                  router_w, router_b, expert_w, expert_b, out_w, out_b, rope, identity, in_block, same_head, hidden,
                  pick_head, gather, expert_ids, out):
    scratch = lambda name, shape, dt=F32: nc.dram_tensor(f"scratch_{name}", shape, dt, kind="Internal").ap()
    self_parts = scratch("self_parts", [B, 3, PARTS, HD, H, N], BF16)
    cross_parts = scratch("cross_parts", [B, 2, PARTS, XD + 1, H, D], BF16)
    bias_parts = scratch("bias_parts", [PARTS, (E + 1) * D], BF16)
    vk, kb = scratch("vk", [B, N, 2 * D]), scratch("kb", [B, N, D])
    a, t = (scratch(n, [B, H, NC, C, C]) for n in ("a", "t"))
    x1, x2 = (scratch(n, [B, N, D]) for n in ("x1", "x2"))
    with ExitStack() as sems:
        project(nc, sems, x, attn_w, rope, identity, in_block, self_parts, vk, kb, a)
        invert(nc, sems, a, t, 6)
        attend(nc, sems, x, attn_wo, identity, same_head, hidden, pick_head, self_parts, vk, kb, t, x1)
        cross_attend(nc, sems, x1, ctx_in, mask, xattn_wq, xattn_wk, xattn_wv, xattn_bias_qk, xattn_bv, identity,
                     pick_head, gather, cross_parts, x2)
        feed_forward(nc, sems, x2, router_w, router_b, expert_w, expert_b, out_w, out_b, identity, expert_ids,
                     bias_parts, out)


def features_first(w):
    return w.reshape(D, H, HD).transpose(0, 2, 1).reshape(D, D)


def features_first_rows(w):
    return w.reshape(H, XD, -1).swapaxes(0, 1).reshape(w.shape)


def shape_constants():
    import numpy as np

    bf16 = np.dtype("bfloat16")
    f32 = np.float32
    inv = (1.0 / f32(10000.0) ** (np.arange(0, HD, 2, dtype=f32) / f32(HD))).astype(f32)
    angle = np.arange(N, dtype=f32)[:, None] * inv
    cos, sin = np.cos(angle), np.sin(angle)
    cos = np.repeat(np.concatenate([cos, cos], 1), H, 1)
    sin = np.repeat(np.concatenate([-sin, sin], 1), H, 1)
    scale = f32(HD ** -0.5)
    seen = np.tril(np.ones((N, N), bool))
    hidden = np.where(seen, 0.0, OUT_OF_SIGHT)
    pick = np.zeros((3 * H, H, 128), bf16)
    gather = np.zeros((128, 2, 32), f32)
    for h in range(H):
        pick[h, h] = pick[2 * H + h, h] = 1
    for j in range(4):
        for d in range(XD):
            gather[32 * j + d, 0, XD * j + d] = 1
            gather[32 * j + XD, 1, XD * j + d] = 1
    return {
        "rope": np.stack([np.concatenate([cos * scale, cos], 1), np.concatenate([sin * scale, sin], 1)], 1).astype(f32),
        "identity": np.eye(128, dtype=f32),
        "in_block": -np.tile(np.tril(np.ones((C, C), f32), -1), (NC, 1)),
        "same_head": np.kron(np.eye(8), np.ones((HD, HD))).astype(f32),
        "hidden": np.stack([hidden, hidden.T], 1).astype(bf16),
        "pick_head": pick,
        "gather": gather,
        "expert_ids": np.arange(E, dtype=f32),
    }


def kernel(x, ctx_2048, mask_Bx1x2048_fk1, L0_attn_Wq, L0_attn_Wk, L0_attn_Wv, L0_attn_Wo, L0_attn_Wb,
           L0_xattn_Wq, L0_xattn_bq, L0_xattn_Wk, L0_xattn_bk, L0_xattn_Wv, L0_xattn_bv, L0_ffn_router_w,
           L0_ffn_router_b, L0_ffn_expert_w, L0_ffn_expert_b, L0_ffn_out_w, L0_ffn_out_b):
    import numpy as np
    import concourse.bacc as bacc
    from concourse.bass_utils import run_bass_kernel_spmd

    a = np.asarray
    arrays = {
        "x": a(x), "ctx": a(ctx_2048), "mask": a(mask_Bx1x2048_fk1),
        "attn_w": np.concatenate([*(features_first(a(w)) for w in (L0_attn_Wq, L0_attn_Wk, L0_attn_Wv)),
                                  a(L0_attn_Wb)], 1),
        "attn_wo": a(L0_attn_Wo),
        "xattn_wq": features_first_rows(a(L0_xattn_Wq)).T,
        "xattn_wk": features_first_rows(a(L0_xattn_Wk)).T,
        "xattn_wv": a(L0_xattn_Wv).T,
        "xattn_bias_qk": np.stack([features_first_rows(a(L0_xattn_bq)), features_first_rows(a(L0_xattn_bk))], 1),
        "xattn_bv": a(L0_xattn_bv),
        "router_w": a(L0_ffn_router_w), "router_b": a(L0_ffn_router_b),
        "expert_w": a(L0_ffn_expert_w), "expert_b": a(L0_ffn_expert_b),
        "out_w": a(L0_ffn_out_w), "out_b": a(L0_ffn_out_b),
        **shape_constants(),
    }
    nc = bacc.Bacc("TRN2", target_bir_lowering=False, num_devices=1)
    arrays = {f"in_{name}": np.ascontiguousarray(v) for name, v in arrays.items()}
    args = [nc.dram_tensor(name, v.shape, mybir.dt.from_np(v.dtype), kind="ExternalInput").ap()
            for name, v in arrays.items()]
    out = nc.dram_tensor("out", (B, N, D), F32, kind="ExternalOutput").ap()
    decoder_layer(nc, *args, out)
    results = run_bass_kernel_spmd(nc, [arrays], core_ids=[0])
    return results.results[0]["out"]
```

```python
from contextlib import ExitStack

import concourse.bass as bass
from concourse import mybir

F32 = mybir.dt.float32
BF16 = mybir.dt.bfloat16
I32 = mybir.dt.int32
U32 = mybir.dt.uint32
ALU = mybir.AluOpType
ACT = mybir.ActivationFunctionType
AX = mybir.AxisListType

B = 16
N = 128
D = 256
H = 16
HD = D // H
XD = N // H
C = 32
NC = N // C
E = 8
TERMS = 6
PARTS = 3
Q_PARTS = ((0, 3), (1, 2), (2, 1))
K_PARTS = ((0, 3), (0, 2), (0, 1))
NEG = 1.0e6
OUT_OF_SIGHT = -1.0e30
LN_EPS = 1e-5
L2_EPS = 1e-6
RSQRT_MAGIC = 0x5F3759DF


def reached(eng, sem, count):
    if not (isinstance(count, int) and count <= 0):
        eng.wait_ge(sem, count)


def sweep(eng, stages):
    deepest = max(lag for lag, _ in stages)
    first = (deepest + 3) // 2 * 2
    for t in range(first):
        for lag, body in stages:
            if t >= lag:
                body(t - lag, (t - lag) % 2)
    with eng.Fori(0, (B - first) // 2) as i:
        for half in range(2):
            for lag, body in stages:
                body(2 * i + (first + half - lag), (half - lag) % 2)
    for t in range(B, B + deepest):
        for lag, body in stages:
            if t - lag < B:
                body(t - lag, (t - lag) % 2)


class Chain:

    def __init__(self, eng, sem, b, per):
        self.eng, self.sem, self.base, self.per, self.n = eng, sem, b * per, per, 0

    def link(self, ins):
        self.n += 1
        ins.then_inc(self.sem, 1)
        self.eng.wait_ge(self.sem, self.base + self.n)

    def done(self):
        assert self.n == self.per, (self.n, self.per)


RSQRT_OPS = 11


def rsqrt_op(eng, k, y, x, tmp, bits):
    if k == 0:
        return eng.tensor_scalar(bits, x.bitcast(I32), 1, None, ALU.logical_shift_right)
    if k == 1:
        return eng.tensor_scalar(y.bitcast(I32), bits, -1.0, float(RSQRT_MAGIC), ALU.mult, ALU.add)
    if k % 3 == 2:
        return eng.tensor_tensor(tmp, y, y, ALU.mult)
    if k % 3 == 0:
        return eng.scalar_tensor_tensor(tmp, tmp, -0.5, x, ALU.mult, ALU.mult)
    return eng.scalar_tensor_tensor(y, tmp, 1.5, y, ALU.add, ALU.mult)


NORM_OPS = 3 + RSQRT_OPS


def layer_norm_op(eng, k, y, stats, moments, rstd, tmp, bits):
    if k == 0:
        return eng.bn_stats(stats, y)
    if k == 1:
        eng.memset(bits, 0)
        return eng.bn_aggr(moments, stats)
    if k == 2:
        return eng.tensor_scalar(moments[:, 1:2], moments[:, 1:2], LN_EPS, None, ALU.add)
    return rsqrt_op(eng, k - 3, rstd, moments[:, 1:2], tmp, bits)


def rsqrt(eng, chain, y, x, tmp, bits):
    for k in range(RSQRT_OPS):
        chain.link(rsqrt_op(eng, k, y, x, tmp, bits))


def layer_norm_stats(eng, chain, y, stats, moments, rstd, tmp, bits):
    for k in range(NORM_OPS):
        chain.link(layer_norm_op(eng, k, y, stats, moments, rstd, tmp, bits))


class Phase:

    def __init__(self, nc, ctx, name):
        self.nc, self.ctx, self.name = nc, ctx, name

    def sb(self, name, shape, dt=F32):
        return self.ctx.enter_context(self.nc.sbuf_tensor(f"{self.name}_{name}", shape, dt))

    def two(self, name, shape, dt=F32):
        return [self.sb(f"{name}{u}", shape, dt) for u in range(2)]

    def bank(self, name):
        return self.ctx.enter_context(self.nc.psum_tensor(f"{self.name}_{name}", [128, 512], F32))

    def sem(self, name):
        return self.ctx.enter_context(self.nc.semaphore(f"{self.name}_{name}"))


def project(nc, sems, x, w, rope, identity, in_block, parts_scr, vk_scr, kb_scr, a_scr):
    with ExitStack() as ctx:
        ph = Phase(nc, ctx, "pr")
        sem = lambda name: sems.enter_context(nc.semaphore(f"pr_{name}"))
        w_sb = ph.sb("w", [128, 2, 3 * D + H])
        rope_sb = ph.sb("rope", [128, 2, 2 * D])
        id_sb = ph.sb("id", [128, 128])
        below_sb = ph.sb("below", [128, C])
        x_sb = ph.two("x", [128, D])
        xt_sb = ph.two("xt", [128, 2, 128])
        with_cos = ph.sb("with_cos", [128, 2 * D])
        with_sin = ph.sb("with_sin", [128, 2 * D])
        qk = ph.two("qk", [128, 2 * D])
        ksq = ph.two("ksq", [128, D])
        ez = ph.two("ez", [128, H])
        beta = ph.sb("beta", [128, H])
        ss = ph.sb("ss", [128, H])
        knorm = ph.sb("knorm", [128, 2, H])
        tmp = ph.sb("tmp", [128, H])
        bits = ph.sb("bits", [128, H], I32)
        vk = ph.two("vk", [128, 2 * HD, H])
        kb = ph.two("kb", [128, D])
        kbh = ph.two("kbh", [128, H, HD])
        rest = ph.two("rest", [128, 3, D])
        parts = ph.two("parts", [128, 3, PARTS, 2, 128], BF16)
        kst = ph.two("kst", [TERMS * HD, H, N], BF16)
        kbst = ph.two("kbst", [TERMS * HD, H, N], BF16)
        a_sb = ph.two("a", [128, H, C])
        ps_x, ps_qk, ps_vb, ps_qb, ps_k, ps_a = (ph.bank(n) for n in ("x", "qk", "vb", "qb", "k", "a"))

        consts = sem("consts")
        x_loaded = [sem(f"x_loaded{u}") for u in range(2)]
        xt_made, xt_copied = sem("xt_made"), sem("xt_copied")
        projected, v_copied, ez_made = sem("projected"), sem("v_copied"), sem("ez_made")
        rope_halves, rotated, squared = sem("rope_halves"), sem("rotated"), sem("squared")
        norm_step, norms_made = sem("norm_step"), sem("norms_made")
        k_scaled, kb_scaled, kb_turned = sem("k_scaled"), sem("kb_scaled"), sem("kb_turned")
        turned, part1, rest_made, part2, part3 = (
            sem("turned"), sem("part1"), sem("rest_made"), sem("part2"), sem("part3"))
        kb_stored = [sem(f"kb_stored{u}") for u in range(2)]
        vk_stored = [sem(f"vk_stored{u}") for u in range(2)]
        parts_stored = [sem(f"parts_stored{u}") for u in range(2)]
        a_stored = [sem(f"a_stored{u}") for u in range(2)]
        stacks_loaded = [sem(f"stacks_loaded{u}") for u in range(2)]
        a_made, a_masked = sem("a_made"), sem("a_masked")

        block = ctx.enter_context(nc.Block())

        @block.sync
        def _(sp):
            sp.dma_start(id_sb[:, :], identity[:, :]).then_inc(consts, 16)
            sp.dma_start(w_sb[:, :, :], w.rearrange("(c p) n -> p c n", p=128)).then_inc(consts, 16)
            sp.dma_start(rope_sb[:, :, :], rope[:, :, :]).then_inc(consts, 16)
            sp.dma_start(below_sb[:, :], in_block[:, :]).then_inc(consts, 16)

            def load_x(b, u):
                reached(sp, xt_made, b - 1)
                sp.dma_start(x_sb[u][:, :], x[b]).then_inc(x_loaded[u], 16)

            def store_vk(b, u):
                sp.wait_ge(v_copied, b + 1)
                sp.wait_ge(k_scaled, b + 1)
                sp.dma_start(vk_scr[b], vk[u][:, :, :]).then_inc(vk_stored[u], 16)

            def store_kb(b, u):
                sp.wait_ge(kb_turned, b + 1)
                sp.dma_start(kb_scr[b], kbh[u][:, :, :]).then_inc(kb_stored[u], 16)

            def store_parts(b, u):
                sp.wait_ge(part3, b + 1)
                sp.dma_start(parts_scr[b].rearrange("t c (g d) h n -> (d h) (t c g) n", g=2),
                             parts[u][:, :, :, :, :]).then_inc(parts_stored[u], 16)

            def load_stacks(b, u):
                reached(sp, a_made, b - 1)
                stored(sp, parts_stored, b, u)
                load_stack(sp, kst[u], parts_scr[b, 2], Q_PARTS, True, stacks_loaded[u])
                load_stack(sp, kbst[u], parts_scr[b, 1], K_PARTS, False, stacks_loaded[u])

            def store_a(b, u):
                sp.wait_ge(a_masked, b + 1)
                sp.dma_start(a_scr[b].rearrange("h c i j -> (c i) h j"), a_sb[u][:, :, :])\
                    .then_inc(a_stored[u], 16)

            def stored(eng, pair, b, u):
                eng.wait_ge(pair[u], per_parity(b, u, 16))

            sweep(sp, [(4, store_kb), (5, store_parts), (9, store_a), (6, load_stacks), (0, load_x), (3, store_vk)])
            for u in range(2):
                sp.wait_ge(vk_stored[u], B // 2 * 16)
                sp.wait_ge(kb_stored[u], B // 2 * 16)
                sp.wait_ge(parts_stored[u], B // 2 * 16)
                sp.wait_ge(a_stored[u], B // 2 * 16)

        @block.tensor
        def _(pe):
            pe.wait_ge(consts, 64)

            def transpose_x(b, u):
                pe.wait_ge(x_loaded[u], per_parity(b, u, 16))
                reached(pe, xt_copied, b)
                for c in range(2):
                    last = pe.transpose(ps_x[:, c * 128:(c + 1) * 128], x_sb[u][:, c * 128:(c + 1) * 128],
                                        id_sb[:, :])
                last.then_inc(xt_made, 1)

            def gram(b, u):
                pe.wait_ge(stacks_loaded[u], per_parity(b, u, 96))
                reached(pe, a_masked, b)
                for h in range(H):
                    for c in range(NC):
                        t = slice(c * C, (c + 1) * C)
                        last = pe.matmul(ps_a[t, h * C:(h + 1) * C], kst[u][:, h, t], kbst[u][:, h, t],
                                         start=True, stop=True)
                last.then_inc(a_made, 1)

            def transpose_qk(b, u):
                pe.wait_ge(kb_scaled, b + 1)
                reached(pe, part1, b)
                reached(pe, rest_made, b)
                k = vk[u][:, HD:2 * HD, :].rearrange("p d h -> p (d h)")
                for g in range(2):
                    half = slice(g * 128, (g + 1) * 128)
                    pe.transpose(ps_qb[:, g * 128:(g + 1) * 128], qk[u][:, half], id_sb[:, :])
                    pe.transpose(ps_qb[:, D + g * 128:D + (g + 1) * 128], kb[u][:, half], id_sb[:, :])
                    last = pe.transpose(ps_k[:, g * 128:(g + 1) * 128], k[:, half], id_sb[:, :])
                last.then_inc(turned, 1)

            def products(b, u):
                pe.wait_ge(xt_copied, b + 1)
                reached(pe, rope_halves, b)
                reached(pe, v_copied, b)
                reached(pe, ez_made, b)
                for c in range(2):
                    pe.matmul(ps_qk[:, :], xt_sb[u][:, c, :], w_sb[:, c, 0:2 * D], start=(c == 0), stop=(c == 1))
                for c in range(2):
                    last = pe.matmul(ps_vb[:, 0:D + H], xt_sb[u][:, c, :], w_sb[:, c, 2 * D:3 * D + H],
                                     start=(c == 0), stop=(c == 1))
                last.then_inc(projected, 1)

            sweep(pe, [(1, products), (3, transpose_qk), (0, transpose_x), (7, gram)])

        @block.scalar
        def _(act):
            def copy_xt(b, u):
                act.wait_ge(xt_made, b + 1)
                reached(act, projected, b - 1)
                act.activation(xt_sb[u][:, :, :], ps_x[:, 0:D].rearrange("p (c n) -> p c n", c=2),
                               ACT.Copy).then_inc(xt_copied, 1)

            def first_part(b, u):
                act.wait_ge(turned, b + 1)
                stored_before(act, parts_stored, b, u, 16)
                act.activation(parts[u][:, 0:2, 0, :, :],
                               ps_qb[:, :].rearrange("p (t g n) -> p t g n", t=2, g=2), ACT.Copy)
                act.activation(parts[u][:, 2, 0, :, :],
                               ps_k[:, 0:D].rearrange("p (g n) -> p g n", g=2), ACT.Copy)\
                   .then_inc(part1, 1)

            def second_part(b, u):
                act.wait_ge(rest_made, b + 1)
                act.activation(parts[u][:, :, 1, :, :], rest[u][:, :, :].rearrange("p t (g n) -> p t g n", g=2),
                               ACT.Copy).then_inc(part2, 1)

            def v_and_beta(b, u):
                act.wait_ge(projected, b + 1)
                stored_before(act, vk_stored, b, u, 16)
                reached(act, norms_made, b - 1)
                act.activation(ez[u][:, :], ps_vb[:, D:D + H], ACT.Exp, scale=-1.0).then_inc(ez_made, 1)
                act.activation(vk[u][:, 0:HD, :].rearrange("p d h -> p (d h)"), ps_vb[:, 0:D],
                               ACT.Copy).then_inc(v_copied, 1)

            def turn_kb(b, u):
                act.wait_ge(kb_scaled, b + 1)
                stored_before(act, kb_stored, b, u, 16)
                act.activation(kbh[u][:, :, :], kb[u][:, :].rearrange("p (d h) -> p h d", h=H), ACT.Copy)\
                   .then_inc(kb_turned, 1)

            sweep(act, [(4, second_part), (3, turn_kb), (1, v_and_beta), (3, first_part), (0, copy_xt)])

        @block.vector
        def _(dve):
            dve.wait_ge(consts, 64)

            def mask_a(b, u):
                dve.wait_ge(a_made, b + 1)
                stored_before(dve, a_stored, b, u, 16)
                dve.tensor_tensor(a_sb[u][:, :, :], ps_a[:, :].rearrange("p (h j) -> p h j", h=H),
                                  below_sb[:, :].unsqueeze(1).broadcast_to([128, H, C]), ALU.mult)\
                   .then_inc(a_masked, 1)

            def residue(b, u):
                dve.wait_ge(part1, b + 1)
                reached(dve, part3, b - 1)
                dve.tensor_tensor(rest[u][:, 0:2, :].rearrange("p t n -> p (t n)"), ps_qb[:, :],
                                  parts[u][:, 0:2, 0, :, :], ALU.subtract)
                dve.tensor_tensor(rest[u][:, 2, :], ps_k[:, 0:D], parts[u][:, 2, 0, :, :],
                                  ALU.subtract).then_inc(rest_made, 1)

            def rotate(b, u):
                dve.wait_ge(projected, b + 1)
                reached(dve, rotated, b)
                dve.tensor_tensor(with_cos[:, :], ps_qk[:, :], rope_sb[:, 0, :], ALU.mult)
                swapped = ps_qk[:, :].rearrange("p (t s m) -> p t s m", t=2, s=2)[:, :, ::-1, :]
                dve.tensor_tensor(with_sin[:, :].rearrange("p (t s m) -> p t s m", t=2, s=2), swapped,
                                  rope_sb[:, 1, :].rearrange("p (t s m) -> p t s m", t=2, s=2),
                                  ALU.mult).then_inc(rope_halves, 1)

            def norms(b, u):
                chain = Chain(dve, norm_step, b, RSQRT_OPS + 5)
                dve.wait_ge(ez_made, b + 1)
                chain.link(dve.tensor_scalar(beta[:, :], ez[u][:, :], 0.5, 0.5, ALU.mult, ALU.add))
                reached(dve, kb_scaled, b)
                chain.link(dve.reciprocal(knorm[:, 1, :], beta[:, :]))
                dve.wait_ge(squared, b + 1)
                chain.link(dve.tensor_reduce(ss[:, :], ksq[u][:, :].rearrange("p (d h) -> p h d", h=H), AX.X, ALU.add))
                chain.link(dve.tensor_scalar(ss[:, :], ss[:, :], L2_EPS, None, ALU.add))
                rsqrt(dve, chain, knorm[:, 0, :], ss[:, :], tmp[:, :], bits[:, :])
                chain.link(dve.tensor_tensor(knorm[:, 1, :], knorm[:, 1, :], knorm[:, 0, :], ALU.mult))
                chain.done()
                dve.tensor_copy(tmp[:, 0:1], knorm[:, 0, 0:1]).then_inc(norms_made, 1)

            sweep(dve, [(1, rotate), (2, norms), (3, residue), (7, mask_a)])

        @block.gpsimd
        def _(pool):
            def third_part(b, u):
                pool.wait_ge(part2, b + 1)
                pool.tensor_tensor(parts[u][:, :, 2, :, :].rearrange("p t g n -> p t (g n)"), rest[u][:, :, :],
                                   parts[u][:, :, 1, :, :].rearrange("p t g n -> p t (g n)"),
                                   ALU.subtract).then_inc(part3, 1)

            def rotate_sum(b, u):
                pool.wait_ge(rope_halves, b + 1)
                reached(pool, turned, b - 1)
                pool.tensor_tensor(qk[u][:, :], with_cos[:, :], with_sin[:, :], ALU.add).then_inc(rotated, 1)
                pool.wait_ge(rotated, b + 1)
                pool.tensor_tensor(ksq[u][:, :], qk[u][:, D:2 * D], qk[u][:, D:2 * D], ALU.mult)\
                    .then_inc(squared, 1)

            def scale_k(b, u):
                pool.wait_ge(norms_made, b + 1)
                stored_before(pool, vk_stored, b, u, 16)
                reached(pool, turned, b - 1)
                reached(pool, kb_turned, b - 1)
                k = qk[u][:, D:2 * D].rearrange("p (d h) -> p d h", h=H)
                pool.tensor_tensor(vk[u][:, HD:2 * HD, :], k,
                                   knorm[:, 0, :].unsqueeze(1).broadcast_to([128, HD, H]),
                                   ALU.mult).then_inc(k_scaled, 1)
                pool.tensor_tensor(kb[u][:, :].rearrange("p (d h) -> p d h", h=H), k,
                                   knorm[:, 1, :].unsqueeze(1).broadcast_to([128, HD, H]),
                                   ALU.mult).then_inc(kb_scaled, 1)

            sweep(pool, [(4, third_part), (1, rotate_sum), (2, scale_k)])


def per_parity(b, u, per):
    return b * (per // 2) + (2 - u) * (per // 2)


def stored_before(eng, pair, b, u, per):
    reached(eng, pair[u], (b - u) * (per // 2))


def at_most(eng, sem, b, ahead):
    eng.wait_ge(sem, min(b + ahead, B) if isinstance(b, int) else b + ahead)


def entry(a, b):
    rest = " ".join("abcd"[:len(a.shape) - 3])
    return a[:, bass.ds(b, 1)].rearrange(f"p o n {rest} -> p (o n) {rest}")


def load_stack(eng, stack, parts, which, repeats, loaded):
    row = 0
    d = parts.shape[1]
    for part, n in which:
        src = parts[part:part + (1 if repeats else n)].rearrange("c d h n -> c d (h n)")
        if repeats:
            src = src.broadcast_to([n, d, src.shape[2]])
        else:
            src = src.rearrange("c d m -> (c d) m")
        eng.dma_start(stack[row:row + n * d, :, :].rearrange("p h n -> p (h n)"), src).then_inc(loaded, 16)
        row += n * d


FIRST = 4


def invert_step(eng, j, half, t, a, product):
    n, rows = a.shape[1], C - 1 - j
    shape = [128, n, j, rows]
    part = product[:, :, 0:j * rows].rearrange("p n (c i) -> p n c i", c=j)
    below = t[:, :, 0:j, j + 1:C]
    if half == 0:
        return eng.tensor_tensor(part, a[:, :, j + 1:C, j].unsqueeze(2).broadcast_to(shape),
                                 t[:, :, 0:j, j:j + 1].broadcast_to(shape), ALU.mult)
    return eng.tensor_tensor(below, below, part, ALU.add)


INVERT_STEPS = 2 * (C - 2)
DIAGONAL = slice(0, C * C, C + 1)


def invert_first(nc, sems, a_scr, t_scr):
    groups = FIRST // 2
    with ExitStack() as ctx:
        ph = Phase(nc, ctx, "inv")
        sem = lambda name: sems.enter_context(nc.semaphore(f"inv_{name}"))
        a, t = (ph.sb(n, [128, groups, C, C]) for n in ("a", "t"))
        product = ph.sb("product", [128, groups, C * C])
        loaded, step, stored = sem("loaded"), sem("step"), sem("stored")
        block = ctx.enter_context(nc.Block())

        @block.sync
        def _(sp):
            sp.dma_start(a[:, :, :, :].rearrange("p n i j -> p n (i j)"),
                         a_scr[0:FIRST].rearrange("(g b) h c i j -> (b h c) g (i j)", b=2)).then_inc(loaded, 16)
            sp.wait_ge(step, 2 + INVERT_STEPS)
            sp.dma_start(t_scr[0:FIRST].rearrange("(g b) h c j i -> (b h c) g (j i)", b=2),
                         t[:, :, :, :].rearrange("p n j i -> p n (j i)")).then_inc(stored, 16)
            sp.wait_ge(stored, 16)

        @block.vector
        def _(dve):
            chain = Chain(dve, step, 0, 2 + INVERT_STEPS)
            dve.wait_ge(loaded, 16)
            chain.link(dve.tensor_copy(t[:, :, :, :].rearrange("p n j i -> p n i j"), a[:, :, :, :]))
            chain.link(dve.memset(t[:, :, :, :].rearrange("p n j i -> p n (j i)")[:, :, DIAGONAL], 1.0))
            for j in range(1, C - 1):
                for half in range(2):
                    chain.link(invert_step(dve, j, half, t, a, product))
            chain.done()


def attend(nc, sems, x, wo, identity, same_head, hidden, gather, parts_scr, vk_scr, kb_scr, a_scr, t_scr,
           x1_scr):
    HV = 32
    G = 2
    QUADS = H // 4
    MAX_ROW = TERMS * HD
    with ExitStack() as ctx:
        ph = Phase(nc, ctx, "at")
        sem = lambda name: sems.enter_context(nc.semaphore(f"at_{name}"))
        wo_sb = ph.sb("wo", [128, 2, D])
        id_sb = ph.sb("id", [128, 128])
        idb_sb = ph.sb("idb", [128, 128], BF16)
        same_sb = ph.sb("same", [128, 128])
        hidden_sb = ph.sb("hidden", [128, 2, 128], BF16)
        a_sys = ph.sb("a_sys", [128, 1, C, C])
        t_sys = ph.sb("t_sys", [128, 1, C, C])
        product = ph.sb("product", [128, 1, C * C])
        unit = ph.sb("unit", [128, C * C])
        t_sb = ph.two("t", [128, H, C])
        vk = ph.two("vk", [128, 2 * HD, H])
        kb = ph.two("kb", [128, D])
        qst = ph.two("qst", [MAX_ROW + 2, H, N], BF16)
        kst = ph.two("kst", [MAX_ROW + 2, H, N], BF16)
        x_sb = ph.two("x", [128, D])
        xa = ph.two("xa", [128, H, HV])
        tk = ph.two("tk", [128, H, HD])
        tkt = ph.two("tkt", [128, G, 128])
        state = ph.sb("state", [128, G, 128])
        nmax = ph.two("nmax", [128, H])
        nmaxt = ph.two("nmaxt", [H, 2, N], BF16)
        p = ph.two("p", [128, 4, N])
        gather_sb = ph.sb("gather", [128, 2, 4 * HD])
        r_sb = ph.sb("r", [128, QUADS, N])
        rden = ph.sb("rden", [128, 2 * N])
        ot = ph.two("ot", [128, 2, N])
        y = ph.two("y", [128, D])
        x1 = ph.two("x1", [128, D])
        stats, moments = ph.sb("stats", [128, 6]), ph.sb("moments", [128, 2])
        rstd, tmp, bits = ph.sb("rstd", [128, 1]), ph.sb("tmp", [128, 1]), ph.sb("bits", [128, 1], I32)
        ps_x, ps_c, ps_o, ps_w = (ph.bank(n) for n in ("x", "c", "o", "w"))
        ps_s1 = [ph.bank(f"s1{i}") for i in range(2)]
        ps_s2 = [ph.bank(f"s2{i}") for i in range(2)]
        nmaxt_ps = ps_w[0:H, 0:128]

        consts, consts_made = sem("consts"), sem("consts_made")
        kb_loaded = [sem(f"kb_loaded{u}") for u in range(2)]
        y_made, ones_step = sem("y_made"), sem("ones_step")
        tv_loaded = [sem(f"tv_loaded{u}") for u in range(2)]
        st_loaded = [sem(f"st_loaded{u}") for u in range(2)]
        x_loaded = [sem(f"x_loaded{u}") for u in range(2)]
        applied, x_copied, tk_turned, tkt_copied = (
            sem("applied"), sem("x_copied"), sem("tk_turned"), sem("tkt_copied"))
        u_made, state_made, r_made, xa_made = sem("u_made"), sem("state_made"), sem("r_made"), sem("xa_made")
        s1_made, max_made, max_turned = sem("s1_made"), sem("max_made"), sem("max_turned")
        max_hi, max_lo = sem("max_hi"), sem("max_lo")
        s2_made, exp_made, pv_made, rden_made, o_made = (
            sem("s2_made"), sem("exp_made"), sem("pv_made"), sem("rden_made"), sem("o_made"))
        r_copied, gathered, wo_made, norm_step, x1_made = (
            sem("r_copied"), sem("gathered"), sem("wo_made"), sem("norm_step"), sem("x1_made"))
        x1_stored = [sem(f"x1_stored{u}") for u in range(2)]
        max_placed = [sem(f"max_placed{u}") for u in range(2)]
        a_loaded, t_stored, t_step, unit_made = sem("a_loaded"), sem("t_stored"), sem("t_step"), sem("unit_made")
        STEPS = NC - 1

        block = ctx.enter_context(nc.Block())

        @block.gpsimd
        def _(pool):
            def group(n):
                e = n * 2 + FIRST
                base = n * (2 + INVERT_STEPS)
                a_flat, t_flat = (x[:, 0, :, :].rearrange("p i j -> p (i j)") for x in (a_sys, t_sys))
                pool.dma_start(a_flat, a_scr[bass.ds(e, 2)].rearrange("b h c i j -> (b h c) (i j)")).then_inc(a_loaded, 16)
                pool.wait_ge(a_loaded, n * 16 + 16)
                if not isinstance(n, int):
                    pool.wait_ge(t_stored, n * 16)
                pool.tensor_tensor(t_sys[:, 0, :, :].rearrange("p j i -> p i j"), a_sys[:, 0, :, :],
                                   unit[:, :].rearrange("p (i j) -> p i j", i=C), ALU.add).then_inc(t_step, 1)
                for j in range(1, C - 1):
                    for half in range(2):
                        pool.wait_ge(t_step, base + 2 * j - 1 + half)
                        invert_step(pool, j, half, t_sys, a_sys, product).then_inc(t_step, 1)
                pool.wait_ge(t_step, base + 1 + INVERT_STEPS)
                pool.tensor_tensor(product[:, 0, 0:1], unit[:, 0:1], unit[:, 0:1], ALU.add).then_inc(t_step, 1)
                pool.dma_start(t_scr[bass.ds(e, 2)].rearrange("b h c j i -> (b h c) (j i)"), t_flat).then_inc(t_stored, 16)

            pool.memset(unit[:, :], 0.0).then_inc(unit_made, 1)
            pool.wait_ge(unit_made, 1)
            pool.memset(unit[:, DIAGONAL], 1.0).then_inc(unit_made, 1)
            pool.wait_ge(unit_made, 2)
            group(0)
            with pool.Fori(1, (B - FIRST) // 2) as i:
                group(i)
            pool.wait_ge(t_stored, 16 * (B - FIRST) // 2)

        @block.sync
        def _(sp):
            sp.dma_start(id_sb[:, :], identity[:, :]).then_inc(consts, 16)
            sp.dma_start(wo_sb[:, :, :], wo.rearrange("(c p) n -> p c n", p=128)).then_inc(consts, 16)
            sp.dma_start(same_sb[:, :], same_head[:, :]).then_inc(consts, 16)
            sp.dma_start(hidden_sb[:, :, :], hidden[:, :, :]).then_inc(consts, 16)
            sp.dma_start(gather_sb[:, :, :], gather[:, :, :]).then_inc(consts, 16)

            def load_tv(b, u):
                reached(sp, applied, b - 1)
                reached(sp, t_stored, b * 8 + (2 - u - FIRST) * 8)
                sp.dma_start(t_sb[u][:, :, :], t_scr[b].rearrange("h c j i -> (c j) h i")).then_inc(tv_loaded[u], 16)
                sp.dma_start(vk[u][:, :, :], vk_scr[b].rearrange("p (d h) -> p d h", h=H)).then_inc(tv_loaded[u], 16)

            def load_kb(b, u):
                reached(sp, u_made, STEPS * (b - 1))
                sp.dma_start(kb[u][:, :], kb_scr[b]).then_inc(kb_loaded[u], 16)

            def load_st(b, u):
                reached(sp, s2_made, QUADS * (b - 1))
                load_stack(sp, qst[u][0:MAX_ROW], parts_scr[b, 0], Q_PARTS, True, st_loaded[u])
                load_stack(sp, kst[u][0:MAX_ROW], parts_scr[b, 1], K_PARTS, False, st_loaded[u])

            def load_x(b, u):
                reached(sp, y_made, b - 1)
                sp.dma_start(x_sb[u][:, :], x[b]).then_inc(x_loaded[u], 16)

            def store_x1(b, u):
                sp.wait_ge(x1_made, b + 1)
                sp.dma_start(x1_scr[b], x1[u][:, :]).then_inc(x1_stored[u], 16)

            sweep(sp, [(0, load_tv), (7, store_x1), (2, load_kb), (4, load_x), (2, load_st)])
            for u in range(2):
                sp.wait_ge(x1_stored[u], B // 2 * 16)

        @block.tensor
        def _(pe):
            pe.wait_ge(consts, 80)
            pe.wait_ge(consts_made, 5)

            def apply_t(q):
                def body(b, u):
                    if q == 0:
                        pe.wait_ge(tv_loaded[u], per_parity(b, u, 32))
                        reached(pe, x_copied, b)
                        pe.matmul(ps_x[:, 0:1], idb_sb[:, :], idb_sb[:, 0:1], start=True, stop=True)
                    for h in range(4 * q, 4 * q + 4):
                        for c in range(NC):
                            t = slice(c * C, (c + 1) * C)
                            last = pe.matmul(ps_x[t, h * C:(h + 1) * C], t_sb[u][t, h, :], vk[u][t, :, h],
                                             start=True, stop=True)
                    if q == QUADS - 1:
                        last.then_inc(applied, 1)
                return body

            def turn_tk(b, u):
                pe.wait_ge(x_copied, b + 1)
                reached(pe, xa_made, STEPS * b)
                for g in range(G):
                    last = pe.transpose(ps_c[:, D + g * 128:D + (g + 1) * 128],
                                        tk[u][:, g * 8:(g + 1) * 8, :].rearrange("p h d -> p (h d)"), id_sb[:, :])
                last.then_inc(tk_turned, 1)

            def new_state(c):
                def body(b, u):
                    if c == 1:
                        pe.wait_ge(kb_loaded[u], per_parity(b, u, 16))
                        pe.wait_ge(tkt_copied, b + 1)
                    else:
                        pe.wait_ge(xa_made, STEPS * b + c - 1)
                    for g in range(G):
                        last = pe.matmul(ps_c[:, g * 128:(g + 1) * 128], kb[u][0:c * C, g * 128:(g + 1) * 128],
                                         xa[u][0:c * C, g * 8:(g + 1) * 8, 0:HD], start=True, stop=True)
                    last.then_inc(u_made, 1)
                return body

            def read_state(c):
                def body(b, u):
                    pe.wait_ge(state_made, STEPS * b + c)
                    t = slice(c * C, (c + 1) * C)
                    for g in range(G):
                        last = pe.matmul(ps_c[t, D + g * 128:D + (g + 1) * 128], tkt[u][:, g, t], state[:, g, :],
                                         start=True, stop=True)
                    last.then_inc(r_made, 1)
                return body

            def scores(ps, kind, left, right, q, rows):
                pe.matmul(ps[:, :], idb_sb[:, :], hidden_sb[:, kind, :].unsqueeze(1).broadcast_to([128, 4, 128]),
                          start=True, stop=False, skip_group_check=True)
                for j in range(4):
                    h = 4 * q + j
                    out = ps[:, j * 128:(j + 1) * 128]
                    last = pe.matmul(out, left[0:rows, h, :], right[0:rows, h, :], start=False, stop=True,
                                     skip_group_check=True)
                return last

            def by_query(q):
                def body(b, u):
                    if q == 0:
                        pe.wait_ge(st_loaded[u], per_parity(b, u, 96))
                    reached(pe, max_made, QUADS * b + q - 1)
                    scores(ps_s1[q % 2], 0, qst[u], kst[u], q, MAX_ROW).then_inc(s1_made, 1)
                return body

            def turn_max(b, u):
                pe.wait_ge(max_made, QUADS * (b + 1))
                reached(pe, y_made, b - 1)
                pe.transpose(nmaxt_ps, nmax[u][:, :], id_sb[:, :]).then_inc(max_turned, 1)

            def by_key(q):
                def body(b, u):
                    if q == 0:
                        pe.wait_ge(max_placed[u], per_parity(b, u, 32))
                    reached(pe, exp_made, QUADS * b + q - 1)
                    scores(ps_s2[q % 2], 1, kst[u], qst[u], q, MAX_ROW + 2).then_inc(s2_made, 1)
                return body

            def values(q):
                def body(b, u):
                    if q == 0:
                        pe.wait_ge(xa_made, STEPS * (b + 1))
                        reached(pe, o_made, b)
                    pe.wait_ge(exp_made, QUADS * b + q + 1)
                    for j in range(4):
                        h = 4 * q + j
                        last = pe.matmul(ps_o[32 * j:32 * j + 32, q * N:(q + 1) * N], xa[u][:, h, :], p[q % 2][:, j, :],
                                         start=True, stop=True)
                    last.then_inc(pv_made, 1)
                return body

            def gather_quads(b, u):
                pe.wait_ge(r_copied, b + 1)
                for n in range(2):
                    for q in range(QUADS):
                        rows = slice(64 * (q % 2), 64 * (q % 2) + 64)
                        col = n * 2 * N + q // 2 * N
                        last = pe.matmul(ps_o[rows, col:col + N], gather_sb[:, n, :], r_sb[:, q, :], start=True, stop=True)
                last.then_inc(gathered, 1)

            def times_wo(b, u):
                pe.wait_ge(o_made, b + 1)
                reached(pe, y_made, b)
                at_most(pe, max_hi, b, 2)
                at_most(pe, max_lo, b, 2)
                for c in range(2):
                    last = pe.matmul(ps_w[:, D:2 * D], ot[u][:, c, :], wo_sb[:, c, :], start=(c == 0), stop=(c == 1))
                last.then_inc(wo_made, 1)

            sweep(pe, [(4, turn_max), (5, gather_quads), (3, turn_tk), (2, apply_t(0)), (3, new_state(1)),
                       (2, apply_t(1)), (4, by_key(0)), (3, read_state(1)), (4, by_key(1)), (3, new_state(2)),
                       (4, values(0)), (4, by_key(2)), (3, read_state(2)), (4, values(1)), (2, apply_t(2)),
                       (4, by_key(3)), (3, new_state(3)), (4, values(2)), (5, times_wo), (3, by_query(0)),
                       (4, values(3)), (3, read_state(3)), (3, by_query(1)), (2, apply_t(3)), (3, by_query(2)),
                       (3, by_query(3))])

        @block.scalar
        def _(act):
            act.wait_ge(consts, 80)
            act.activation(idb_sb[:, :], id_sb[:, :], ACT.Copy).then_inc(consts_made, 1)

            def copy_x(b, u):
                act.wait_ge(applied, b + 1)
                reached(act, pv_made, QUADS * (b - 1))
                reached(act, tk_turned, b - 1)
                both = ps_x[:, :].rearrange("p (h s d) -> p h s d", s=2, d=HD)
                act.activation(xa[u][:, :, 0:HD], both[:, :, 0, :], ACT.Copy)
                act.activation(tk[u][:, :, :], both[:, :, 1, :], ACT.Copy).then_inc(x_copied, 1)

            def copy_tkt(b, u):
                act.wait_ge(tk_turned, b + 1)
                reached(act, r_made, STEPS * (b - 1))
                act.activation(tkt[u][:, :, :], ps_c[:, D:2 * D].rearrange("p (g n) -> p g n", g=G), ACT.Copy)\
                   .then_inc(tkt_copied, 1)

            def max_parts(b, u):
                act.wait_ge(max_turned, b + 1)
                stored_before(act, max_placed, b, u, 32)
                act.activation(nmaxt[u][:, 0, :], nmaxt_ps, ACT.Copy).then_inc(max_hi, 1)

            def place_max(b, u):
                act.wait_ge(max_lo, b + 1)
                for part in range(2):
                    row = MAX_ROW + part
                    act.dma_start(qst[u][row:row + 1, :, :], nmaxt[u][:, part, :]).then_inc(max_placed[u], 16)

            def exps(q):
                def body(b, u):
                    act.wait_ge(s2_made, QUADS * b + q + 1)
                    reached(act, pv_made, QUADS * b + q - 1)
                    act.activation(p[q % 2][:, :, :], ps_s2[q % 2][:, :].rearrange("p (h n) -> p h n", h=4),
                                   ACT.Exp).then_inc(exp_made, 1)
                return body

            def copy_r(b, u):
                act.wait_ge(pv_made, QUADS * (b + 1))
                reached(act, gathered, b)
                act.activation(r_sb[:, :, :], ps_o[:, :].rearrange("p (q n) -> p q n", q=QUADS), ACT.Copy)\
                   .then_inc(r_copied, 1)

            sweep(act, [(4, max_parts), (3, copy_tkt), (4, place_max), (4, exps(0)), (4, exps(1)), (4, exps(2)), (4, exps(3)),
                        (4, copy_r), (2, copy_x)])

        @block.vector
        def _(dve):
            for u in range(2):
                dve.memset(xa[u][:, :, :], 0.0).then_inc(ones_step, 1)
                dve.wait_ge(ones_step, u + 1)
                dve.memset(xa[u][:, :, HD:HD + 1], 1.0).then_inc(consts_made, 1)
                dve.memset(kst[u][MAX_ROW:MAX_ROW + 2, :, :], 1.0).then_inc(consts_made, 1)
            dve.wait_ge(consts_made, 5)
            dve.wait_ge(consts, 80)

            def maxima(q):
                def body(b, u):
                    if q == 0:
                        reached(dve, max_turned, b - 1)
                    dve.wait_ge(s1_made, QUADS * b + q + 1)
                    dve.tensor_reduce(nmax[u][:, 4 * q:4 * q + 4], ps_s1[q % 2][:, :].rearrange("p (h k) -> p h k", h=4),
                                      AX.X, ALU.max, negate=True).then_inc(max_made, 1)
                return body

            def keep_state(c):
                def body(b, u):
                    dve.wait_ge(u_made, STEPS * b + c)
                    reached(dve, r_made, STEPS * b + c - 1)
                    dve.tensor_tensor(state[:, :, :], ps_c[:, 0:D].rearrange("p (g n) -> p g n", g=G),
                                      same_sb[:, :].unsqueeze(1).broadcast_to([128, G, 128]), ALU.mult)\
                       .then_inc(state_made, 1)
                return body

            def new_values(c):
                def body(b, u):
                    dve.wait_ge(r_made, STEPS * b + c)
                    t = slice(c * C, (c + 1) * C)
                    dve.tensor_tensor(xa[u][t, :, 0:HD], xa[u][t, :, 0:HD],
                                      ps_c[t, D:2 * D].rearrange("p (h d) -> p h d", h=H), ALU.subtract)\
                       .then_inc(xa_made, 1)
                return body

            def max_rest(b, u):
                dve.wait_ge(max_hi, b + 1)
                dve.tensor_tensor(nmaxt[u][:, 1, :], nmaxt_ps, nmaxt[u][:, 0, :], ALU.subtract)\
                   .then_inc(max_lo, 1)

            def invert_half(n):
                def body(b, u):
                    if n == 0:
                        dve.wait_ge(gathered, b + 1)
                        reached(dve, o_made, b)
                    half = slice(n * N, (n + 1) * N)
                    dve.reciprocal(rden[:, half], ps_o[:, 2 * N:4 * N][:, half]).then_inc(rden_made, 1)
                return body

            def normalise(b, u):
                dve.wait_ge(rden_made, 2 * (b + 1))
                reached(dve, wo_made, b - 1)
                dve.tensor_tensor(ot[u][:, :, :].rearrange("p c n -> p (c n)"), ps_o[:, 0:2 * N], rden[:, :],
                                  ALU.mult).then_inc(o_made, 1)

            def residual(b, u):
                dve.wait_ge(wo_made, b + 1)
                dve.wait_ge(x_loaded[u], per_parity(b, u, 16))
                reached(dve, x1_made, b - 1)
                dve.tensor_tensor(y[u][:, :], ps_w[:, D:2 * D], x_sb[u][:, :], ALU.add).then_inc(y_made, 1)

            def norm(k):
                def body(b, u):
                    if k == 0:
                        dve.wait_ge(y_made, b + 1)
                    else:
                        dve.wait_ge(norm_step, NORM_OPS * b + k)
                    if k < NORM_OPS:
                        layer_norm_op(dve, k, y[u][:, :], stats[:, :], moments[:, :], rstd[:, :], tmp[:, :],
                                      bits[:, :]).then_inc(norm_step, 1)
                    else:
                        stored_before(dve, x1_stored, b, u, 16)
                        dve.tensor_scalar(x1[u][:, :], y[u][:, :], moments[:, 0:1], rstd[:, 0:1], ALU.subtract,
                                          ALU.mult).then_inc(x1_made, 1)
                return body

            main = [(4, max_rest), (5, invert_half(0)), (5, invert_half(1)), (5, normalise), (3, keep_state(1)),
                    (3, new_values(1)), (3, keep_state(2)), (3, new_values(2)), (3, keep_state(3)), (5, residual),
                    (3, maxima(0)), (3, new_values(3)), (3, maxima(1)), (3, maxima(2)), (3, maxima(3))]
            stages = []
            for n, stage in enumerate(main):
                stages += [stage, (6, norm(n))]
            sweep(dve, stages + [(6, norm(k)) for k in range(len(main), NORM_OPS + 1)])


def cross_attend(nc, sems, x1_scr, ctx_in, mask, wq, wk, wv, bias_qk, bv, identity, gather, stacks_scr,
                 x2_scr):
    T = D
    XF = XD + 1
    SCALE = float(XD) ** -0.5
    SIDES = 2
    HALF = H // 2
    NG = H // 4
    MAX_ROW = 96
    P_BUFS = 8
    ORDER = ((0, 0, 0, 1, 1, 2), (0, 1, 2, 0, 1, 0))
    OFF = 5
    with ExitStack() as ctx:
        ph = Phase(nc, ctx, "xa")
        sem = lambda name: sems.enter_context(nc.semaphore(f"xa_{name}"))
        w_sb = ph.sb("w", [128, 3, N])
        b_sb = ph.sb("b", [128, 2])
        bv_sb = ph.sb("bv", [128, N])
        id_sb = ph.sb("id", [128, 128])
        gather_sb = ph.sb("gather", [128, 2, 32])
        mcol_sb = ph.sb("mcol", [128, 2, B])
        m16 = ph.sb("m16", [B, SIDES, T])
        m16_rest = ph.sb("m16_rest", [B, SIDES, T])
        m16_parts = ph.sb("m16_parts", [B, SIDES, PARTS, T], BF16)
        x1 = ph.two("x1", [128, T])
        cx = ph.two("cx", [128, T])
        mrow = ph.two("mrow", [128, T])
        mq = ph.sb("mq", [128, T])
        scale_sb = ph.sb("scale", [128, 1])
        qk = ph.two("qk", [128, SIDES, T])
        rest = ph.two("rest", [128, SIDES, T])
        parts = ph.two("parts", [128, SIDES, PARTS, T], BF16)
        qst = ph.two("qst", [MAX_ROW + 2, H, T], BF16)
        kst = ph.two("kst", [MAX_ROW + 2, H, T], BF16)
        va = ph.two("va", [128, 2, H, 32])
        vb = ph.sb("vb", [128, 2, N])
        nmax = ph.two("nmax", [128, 2, H])
        nmaxt = ph.two("nmaxt", [H, 2, T], BF16)
        p = [ph.sb(f"p{i}", [128, 2, T]) for i in range(P_BUFS)]
        r = ph.sb("r", [128, NG, T])
        rden = ph.sb("rden", [128, T])
        o = ph.two("o", [128, T])
        y = ph.two("y", [128, T])
        cv = ph.two("cv", [128, T])
        x1r = ph.two("x1r", [128, T])
        mr = ph.two("mr", [128, T])
        x2 = ph.two("x2", [128, T])
        stats, moments = ph.sb("stats", [128, 6]), ph.sb("moments", [128, 2])
        rstd, tmp, bits = ph.sb("rstd", [128, 1]), ph.sb("tmp", [128, 1]), ph.sb("bits", [128, 1], I32)
        ps_a, ps_n = ph.bank("projections"), ph.bank("gathered")
        ps_s1 = [ph.bank(f"s1{i}") for i in range(2)]
        ps_s2 = [ph.bank(f"s2{i}") for i in range(2)]
        ps_r = [ph.bank(f"group{i}") for i in range(2)]
        nmaxt_ps = ps_a[0:H, 0:T]

        consts, made, m_step, m_part = sem("consts"), sem("made"), sem("m_step"), sem("m_part")
        m_stored = sem("m_stored")
        in_loaded = [sem(f"in_loaded{u}") for u in range(2)]
        qk_made, mq_made, qk_masked, part1, rest_made, part2, part3 = (
            sem(n) for n in ("qk_made", "mq_made", "qk_masked", "part1", "rest_made", "part2", "part3"))
        v_made, vb_made, v_masked = sem("v_made"), sem("vb_made"), sem("v_masked")
        parts_stored = [sem(f"parts_stored{u}") for u in range(2)]
        max_placed = [sem(f"max_placed{u}") for u in range(2)]
        st_loaded = [[sem(f"st_loaded{u}{i}") for i in range(2)] for u in range(2)]
        s1_made, max_made, max_turned, max_hi, max_lo = (
            sem(n) for n in ("s1_made", "max_made", "max_turned", "max_hi", "max_lo"))
        s2_made, exp_made, pv_made, r_copied, gathered = (
            sem(n) for n in ("s2_made", "exp_made", "pv_made", "r_copied", "gathered"))
        rden_made, o_made, o_masked, y_made, norm_step, x2_made = (
            sem(n) for n in ("rden_made", "o_made", "o_masked", "y_made", "norm_step", "x2_made"))
        cv_loaded = [sem(f"cv_loaded{u}") for u in range(2)]
        res_loaded = [sem(f"res_loaded{u}") for u in range(2)]
        x2_stored = [sem(f"x2_stored{u}") for u in range(2)]
        mcol_turned, scale_made = sem("mcol_turned"), sem("scale_made")
        MADE = 7
        LAG = 4

        def shifted(slot):
            return (slot - OFF) % H, LAG + 1 if slot >= OFF else LAG + 2

        block = ctx.enter_context(nc.Block())

        @block.sync
        def _(sp):
            for side in range(SIDES):
                sp.dma_start(m16[:, side, :], mask.rearrange("b a t -> (b a) t")).then_inc(consts, 16)
            sp.dma_start(id_sb[:, :], identity[:, :]).then_inc(consts, 16)
            for n, w in enumerate((wq, wk, wv)):
                sp.dma_start(w_sb[:, n, :], w[:, :]).then_inc(consts, 16)
            sp.dma_start(b_sb[:, :], bias_qk[:, :]).then_inc(consts, 16)
            sp.dma_start(bv_sb[:, :], bv.partition_broadcast(128)).then_inc(consts, 16)
            sp.dma_start(gather_sb[:, :, :], gather[:, :, :]).then_inc(consts, 16)
            sp.wait_ge(m_part, 3 * 1)
            for side in range(SIDES):
                for row, part in enumerate(ORDER[side]):
                    sp.dma_start(stacks_scr[:, side, row, XD],
                                 m16_parts[:, side, part, :].unsqueeze(1).broadcast_to([B, H, T])).then_inc(m_stored, 16)

            def load_in(b, u):
                reached(sp, qk_masked, b - 1)
                sp.dma_start(x1[u][:, :], x1_scr[b]).then_inc(in_loaded[u], 16)
                sp.dma_start(cx[u][:, :], ctx_in[b]).then_inc(in_loaded[u], 16)
                sp.dma_start(mrow[u][:, :], mask[b, 0].partition_broadcast(128)).then_inc(in_loaded[u], 16)

            def store_parts(b, u):
                sp.wait_ge(part3, b + 1)
                rows = stacks_scr[b].rearrange("s c f h t -> s c (f h) t")[:, :, 0:XD * H]
                row = 0
                for part, n in Q_PARTS:
                    sp.dma_start(rows[0, row:row + n].rearrange("c m t -> m c t"),
                                 parts[u][:, 0, part, :].unsqueeze(1).broadcast_to([128, n, T]))\
                        .then_inc(parts_stored[u], 16)
                    row += n
                row = 0
                for part, n in K_PARTS:
                    sp.dma_start(rows[1, row:row + n].rearrange("c m t -> m c t"), parts[u][:, 1, part:part + n, :])\
                        .then_inc(parts_stored[u], 16)
                    row += n

            def load_stacks(half):
                heads = slice(half * HALF, (half + 1) * HALF)

                def body(b, u):
                    if isinstance(b, int) and b < 2:
                        sp.wait_ge(made, MADE)
                    if half == 0:
                        if isinstance(b, int) and b == 0:
                            sp.wait_ge(m_stored, 16 * SIDES * TERMS)
                        sp.wait_ge(parts_stored[u], per_parity(b, u, 16 * TERMS))
                    reached(sp, s2_made, H * (b - 2) + (half + 1) * HALF)
                    for side, stack in enumerate((qst, kst)):
                        sp.dma_start(stack[u][0:TERMS * XF, heads, :],
                                     stacks_scr[b, side].rearrange("c f h t -> (c f) h t")[:, heads, :])\
                            .then_inc(st_loaded[u][half], 16)
                return body

            def place_max(b, u):
                sp.wait_ge(max_lo, b + 1)
                for part in range(2):
                    row = MAX_ROW + part
                    sp.dma_start(qst[u][row:row + 1, :, :], nmaxt[u][:, part, :]).then_inc(max_placed[u], 16)

            def load_cv(b, u):
                reached(sp, v_made, b - 1)
                sp.dma_start(cv[u][:, :], ctx_in[b]).then_inc(cv_loaded[u], 16)

            def load_residual(b, u):
                reached(sp, y_made, b - 1)
                sp.dma_start(x1r[u][:, :], x1_scr[b]).then_inc(res_loaded[u], 16)
                sp.dma_start(mr[u][:, :], mask[b, 0].partition_broadcast(128)).then_inc(res_loaded[u], 16)

            def store_x2(b, u):
                sp.wait_ge(x2_made, b + 1)
                sp.dma_start(x2_scr[b], x2[u][:, :]).then_inc(x2_stored[u], 16)

            sweep(sp, [(LAG + 1, place_max), (LAG, load_stacks(1)), (2, store_parts), (LAG + 4, store_x2), (0, load_in),
                       (LAG - 1, load_cv), (LAG + 1, load_residual), (LAG - 1, load_stacks(0))])
            for u in range(2):
                sp.wait_ge(x2_stored[u], B // 2 * 16)

        @block.tensor
        def _(pe):
            pe.wait_ge(consts, 16 * 9)
            for c in range(2):
                last = pe.transpose(ps_n[:, c * B:(c + 1) * B], m16[:, 0, c * 128:(c + 1) * 128], id_sb[0:B, 0:B])
            last.then_inc(mcol_turned, 1)
            pe.wait_ge(made, MADE)

            def project_qk(b, u):
                pe.wait_ge(in_loaded[u], per_parity(b, u, 48))
                reached(pe, qk_masked, b)
                reached(pe, max_lo, b - LAG + 1)
                pe.matmul(ps_a[:, 0:T], w_sb[:, 0, :], x1[u][:, :], start=True, stop=True)
                pe.matmul(ps_a[:, T:2 * T], w_sb[:, 1, :], cx[u][:, :], start=True, stop=True).then_inc(qk_made, 1)

            def project_v(b, u):
                pe.wait_ge(cv_loaded[u], per_parity(b, u, 16))
                at_most(pe, qk_masked, b, LAG)
                reached(pe, max_lo, b)
                for c in range(2):
                    last = pe.matmul(ps_a[:, c * N:(c + 1) * N], cv[u][:, c * 128:(c + 1) * 128], w_sb[:, 2, :],
                                     start=True, stop=True)
                last.then_inc(v_made, 1)

            def by_query(h):
                def body(b, u):
                    if h % HALF == 0:
                        pe.wait_ge(st_loaded[u][h // HALF], per_parity(b, u, 32))
                    reached(pe, max_made, H * b + h - 1)
                    for c in range(2):
                        last = pe.matmul(ps_s1[h % 2][:, c * T:(c + 1) * T], qst[u][0:MAX_ROW, h, c * 128:(c + 1) * 128],
                                         kst[u][0:MAX_ROW, h, :], start=True, stop=True)
                    last.then_inc(s1_made, 1)
                return body

            def turn_max(b, u):
                pe.wait_ge(max_made, H * (b + 1))
                pe.wait_ge(v_masked, b + 1)
                for c in range(2):
                    last = pe.transpose(ps_a[0:H, c * 128:(c + 1) * 128], nmax[u][:, c, :], id_sb[:, :])
                last.then_inc(max_turned, 1)

            def by_key(h):
                def body(b, u):
                    if h == 0:
                        pe.wait_ge(max_placed[u], per_parity(b, u, 32))
                    reached(pe, exp_made, H * b + h - 1)
                    for c in range(2):
                        last = pe.matmul(ps_s2[h % 2][:, c * T:(c + 1) * T], kst[u][:, h, c * 128:(c + 1) * 128],
                                         qst[u][:, h, :], start=True, stop=True)
                    last.then_inc(s2_made, 1)
                return body

            def values(g, c):
                def body(b, u):
                    if c == 0:
                        reached(pe, r_copied, NG * b + g - 1)
                        pe.wait_ge(exp_made, H * b + 4 * g + 4)
                    for j in range(4):
                        h = 4 * g + j
                        last = pe.matmul(ps_r[g % 2][32 * j:32 * j + 32, 0:T], va[u][:, c, h, :],
                                         p[h % P_BUFS][:, c, :], start=(c == 0), stop=(c == 1))
                    if c == 1:
                        last.then_inc(pv_made, 1)
                return body

            def gather_groups(n):
                def body(b, u):
                    if n == 0:
                        pe.wait_ge(r_copied, NG * (b + 1))
                        reached(pe, o_made, b)
                    for g in range(NG):
                        last = pe.matmul(ps_n[32 * g:32 * g + 32, n * T:(n + 1) * T], gather_sb[:, n, :], r[:, g, :],
                                         start=True, stop=True)
                    if n == 1:
                        last.then_inc(gathered, 1)
                return body

            stages = []
            for slot in range(H):
                stages.append((LAG, by_query(slot)))
                h, lag = shifted(slot)
                stages.append((lag, by_key(h)))
                if h % 4 in (1, 2):
                    c = h % 4 - 1
                    stages.append((lag, values(h // 4 - 1, c)) if h > 4 else (lag + 1, values(NG - 1, c)))
                if slot == 0:
                    stages.append((LAG + 1, turn_max))
                if slot == 3:
                    stages.append((1, project_qk))
                if h in (4, 7):
                    stages.append((lag + 1, gather_groups(h // 7)))
                if slot == 9:
                    stages.append((LAG, project_v))
            sweep(pe, stages)

        @block.scalar
        def _(act):
            act.wait_ge(mcol_turned, 1)
            act.activation(mcol_sb[:, :, :], ps_n[:, 0:2 * B].rearrange("p (c b) -> p c b", c=2), ACT.Copy)\
               .then_inc(made, 1)

            def first_part(b, u):
                act.wait_ge(qk_masked, b + 1)
                stored_before(act, parts_stored, b, u, 16 * TERMS)
                act.activation(parts[u][:, :, 0, :], qk[u][:, :, :], ACT.Copy).then_inc(part1, 1)

            def second_part(b, u):
                act.wait_ge(rest_made, b + 1)
                act.activation(parts[u][:, :, 1, :], rest[u][:, :, :], ACT.Copy).then_inc(part2, 1)

            def max_parts(b, u):
                act.wait_ge(max_turned, b + 1)
                stored_before(act, max_placed, b, u, 32)
                act.activation(nmaxt[u][:, 0, :], nmaxt_ps, ACT.Copy).then_inc(max_hi, 1)

            def exps(h):
                def body(b, u):
                    act.wait_ge(s2_made, H * b + h + 1)
                    if h % 4 == 0:
                        reached(act, pv_made, NG * b + h // 4 + 1 - P_BUFS // 4)
                    act.activation(p[h % P_BUFS][:, :, :], ps_s2[h % 2][:, :].rearrange("p (c t) -> p c t", c=2),
                                   ACT.Exp).then_inc(exp_made, 1)
                return body

            def copy_r(g):
                def body(b, u):
                    act.wait_ge(pv_made, NG * b + g + 1)
                    if g == 0:
                        reached(act, gathered, b)
                    act.activation(r[:, g, :], ps_r[g % 2][:, 0:T], ACT.Copy).then_inc(r_copied, 1)
                return body

            stages = []
            for slot in range(H):
                h, lag = shifted(slot)
                stages.append((lag, exps(h)))
                if h % 4 == 3:
                    stages.append((lag, copy_r(h // 4 - 1)) if h > 4 else (lag + 1, copy_r(NG - 1)))
                if slot == 0:
                    stages.append((LAG + 1, max_parts))
                if slot == 6:
                    stages.append((1, first_part))
                if slot == 10:
                    stages.append((1, second_part))
            sweep(act, stages)

        @block.vector
        def _(dve):
            for u in range(2):
                dve.memset(va[u][:, :, :, :], 0.0).then_inc(m_step, 1)
            dve.wait_ge(m_step, 2)
            for u in range(2):
                dve.memset(va[u][:, :, :, XD:XD + 1], 1.0).then_inc(made, 1)
            dve.wait_ge(consts, 16 * 9)
            dve.tensor_scalar(m16[:, 1, :], m16[:, 1, :], 1.0, NEG, ALU.subtract, ALU.mult).then_inc(m_step, 1)
            dve.wait_ge(m_step, 3)
            dve.tensor_copy(m16_parts[:, :, 0, :], m16[:, :, :]).then_inc(m_part, 1)
            dve.wait_ge(m_part, 1)
            dve.tensor_tensor(m16_rest[:, :, :], m16[:, :, :], m16_parts[:, :, 0, :], ALU.subtract).then_inc(m_step, 1)
            dve.wait_ge(m_step, 4)
            dve.tensor_copy(m16_parts[:, :, 1, :], m16_rest[:, :, :]).then_inc(m_part, 1)
            dve.wait_ge(m_part, 2)
            dve.tensor_tensor(m16_parts[:, :, 2, :], m16_rest[:, :, :], m16_parts[:, :, 1, :],
                              ALU.subtract).then_inc(m_part, 1)
            dve.wait_ge(made, MADE)

            def mask_qk(b, u):
                dve.wait_ge(qk_made, b + 1)
                dve.wait_ge(mq_made, b + 1)
                reached(dve, rest_made, b - 1)
                dve.scalar_tensor_tensor(qk[u][:, 0, :], ps_a[:, 0:T], b_sb[:, 0:1], mq[:, :], ALU.add, ALU.mult)
                dve.scalar_tensor_tensor(qk[u][:, 1, :], ps_a[:, T:2 * T], b_sb[:, 1:2], mrow[u][:, :], ALU.add,
                                         ALU.mult).then_inc(qk_masked, 1)

            def mask_v(b, u):
                dve.wait_ge(v_made, b + 1)
                dve.tensor_tensor(vb[:, :, :], ps_a[:, 0:2 * N].rearrange("p (c n) -> p c n", c=2),
                                  bv_sb[:, :].unsqueeze(1).broadcast_to([128, 2, N]), ALU.add).then_inc(vb_made, 1)
                dve.wait_ge(vb_made, b + 1)
                reached(dve, pv_made, NG * (b - 1))
                for c in range(2):
                    ins = dve.tensor_scalar(va[u][:, c, :, 0:XD], vb[:, c, :].rearrange("p (h d) -> p h d", h=H),
                                            mcol_sb[:, c, bass.ds(b, 1)] if not isinstance(b, int) else
                                            mcol_sb[:, c, b:b + 1], None, ALU.mult)
                ins.then_inc(v_masked, 1)

            def maximum(h):
                def body(b, u):
                    if h == 0:
                        reached(dve, max_turned, b - 1)
                    dve.wait_ge(s1_made, H * b + h + 1)
                    dve.tensor_reduce(nmax[u][:, :, h], ps_s1[h % 2][:, :].rearrange("p (c s) -> p c s", c=2),
                                      AX.X, ALU.max, negate=True).then_inc(max_made, 1)
                return body

            def max_rest(b, u):
                dve.wait_ge(max_hi, b + 1)
                dve.tensor_tensor(nmaxt[u][:, 1, :], nmaxt_ps, nmaxt[u][:, 0, :], ALU.subtract)\
                   .then_inc(max_lo, 1)

            def invert_half(n):
                def body(b, u):
                    if n == 0:
                        dve.wait_ge(gathered, b + 1)
                    half = slice(n * T // 2, (n + 1) * T // 2)
                    dve.reciprocal(rden[:, half], ps_n[:, T:2 * T][:, half]).then_inc(rden_made, 1)
                return body

            def normalise(b, u):
                dve.wait_ge(rden_made, 2 * (b + 1))
                reached(dve, o_masked, b - 1)
                dve.tensor_tensor(o[u][:, :], ps_n[:, 0:T], rden[:, :], ALU.mult).then_inc(o_made, 1)

            def norm(k):
                def body(b, u):
                    if k == 0:
                        dve.wait_ge(y_made, b + 1)
                    else:
                        dve.wait_ge(norm_step, NORM_OPS * b + k)
                    if k < NORM_OPS:
                        layer_norm_op(dve, k, y[u][:, :], stats[:, :], moments[:, :], rstd[:, :], tmp[:, :],
                                      bits[:, :]).then_inc(norm_step, 1)
                    else:
                        stored_before(dve, x2_stored, b, u, 16)
                        dve.tensor_scalar(x2[u][:, :], y[u][:, :], moments[:, 0:1], rstd[:, 0:1], ALU.subtract,
                                          ALU.mult).then_inc(x2_made, 1)
                return body

            stages = []
            for slot in range(H):
                stages.append((LAG, maximum(slot)))
                if slot == 1:
                    stages.append((LAG + 1, max_rest))
                if slot == 4:
                    stages.append((1, mask_qk))
                if slot == 10:
                    stages.append((LAG, mask_v))
                if slot in (12, 13):
                    stages.append((LAG + 2, invert_half(slot - 12)))
                if slot == 14:
                    stages.append((LAG + 2, normalise))
                if slot <= NORM_OPS:
                    stages.append((LAG + 3, norm(slot)))
            sweep(dve, stages)

        @block.gpsimd
        def _(pool):
            pool.memset(scale_sb[:, :], SCALE).then_inc(scale_made, 1)
            for u in range(2):
                pool.memset(qst[u][:, :, :], 0.0).then_inc(made, 1)
                pool.memset(kst[u][:, :, :], 0.0).then_inc(scale_made, 1)
            pool.wait_ge(scale_made, 3)
            for u in range(2):
                pool.memset(kst[u][MAX_ROW:MAX_ROW + 2, :, :], 1.0).then_inc(made, 1)
            pool.wait_ge(made, MADE)
            pool.wait_ge(scale_made, 1)

            def scale_mask(b, u):
                pool.wait_ge(in_loaded[u], per_parity(b, u, 48))
                reached(pool, qk_masked, b)
                pool.tensor_tensor(mq[:, :], mrow[u][:, :], scale_sb[:, :].broadcast_to([128, T]), ALU.mult).then_inc(mq_made, 1)

            def residue(b, u):
                pool.wait_ge(part1, b + 1)
                reached(pool, part3, b - 1)
                pool.tensor_tensor(rest[u][:, :, :], qk[u][:, :, :], parts[u][:, :, 0, :], ALU.subtract)\
                    .then_inc(rest_made, 1)

            def third_part(b, u):
                pool.wait_ge(part2, b + 1)
                pool.tensor_tensor(parts[u][:, :, 2, :], rest[u][:, :, :], parts[u][:, :, 1, :], ALU.subtract)\
                    .then_inc(part3, 1)

            def add_residual(b, u):
                pool.wait_ge(o_made, b + 1)
                pool.wait_ge(res_loaded[u], per_parity(b, u, 32))
                pool.tensor_tensor(o[u][:, :], o[u][:, :], mr[u][:, :], ALU.mult).then_inc(o_masked, 1)
                pool.wait_ge(o_masked, b + 1)
                reached(pool, x2_made, b - 1)
                pool.tensor_tensor(y[u][:, :], o[u][:, :], x1r[u][:, :], ALU.add).then_inc(y_made, 1)

            sweep(pool, [(1, scale_mask), (1, residue), (1, third_part), (LAG + 2, add_residual)])


def feed_forward(nc, sems, x2_scr, router_w, router_b, expert_w, expert_b, out_w, out_b, identity, expert_ids,
                 bias_scr, out):
    TOP = 2
    PAIRS = E // 2
    ROWS = (E + 1) * D // 128
    with ExitStack() as ctx:
        ph = Phase(nc, ctx, "ff")
        sem = lambda name: sems.enter_context(nc.semaphore(f"ff_{name}"))
        id_sb = ph.sb("id", [128, 128])
        rw_sb = ph.sb("rw", [128, 2, E])
        rb_sb = ph.sb("rb", [128, E])
        ids_sb = ph.sb("ids", [128, E])
        ew_sb = ph.sb("ew", [128, 2, E, D])
        ow_sb = ph.sb("ow", [128, 2, D])
        bias = ph.sb("bias", [ROWS, 128])
        bias_rest = ph.sb("bias_rest", [ROWS, 128])
        bias_parts = ph.sb("bias_parts", [ROWS, PARTS, 128], BF16)
        bias_sb = ph.sb("bias_stack", [PARTS, (E + 1) * D], BF16)
        ones = ph.sb("ones", [PARTS, 128], BF16)
        x2_sb = ph.two("x2", [128, D])
        x2_all = ph.sb("x2_all", [128, B, D])
        xt_all = ph.sb("xt_all", [128, B, 2, 128])
        xt = ph.two("xt", [128, 2, 128])
        probs = ph.sb("probs", [128, B, E])
        row = ph.sb("row", [128, B])
        row_inv = ph.sb("row_inv", [128, B])
        best = ph.sb("best", [128, B, 8])
        best_at = ph.sb("best_at", [128, B, 8], U32)
        at = ph.sb("at", [128, TOP, B])
        share = ph.sb("share", [128, TOP, B])
        chosen = ph.sb("chosen", [128, TOP, B, E])
        gates = ph.sb("gates", [128, B, E])
        ge = ph.two("gelu", [128, E, D])
        comb = ph.two("comb", [128, D])
        combt = ph.two("combt", [128, 2, 128])
        y = ph.sb("y", [128, D])
        res = ph.two("out", [128, D])
        stats, moments = ph.sb("stats", [128, 6]), ph.sb("moments", [128, 2])
        rstd, tmp, bits = ph.sb("rstd", [128, 1]), ph.sb("tmp", [128, 1]), ph.sb("bits", [128, 1], I32)
        ps_t = [ph.bank(f"t{i}") for i in range(2)]
        ps_c, ps_o = ps_t
        ps_l = ph.bank("logits")
        ps_e = [ph.bank(f"e{i}") for i in range(PAIRS)]

        consts, weights, b_step, b_stored, b_loaded = (
            sem(n) for n in ("consts", "weights", "b_step", "b_stored", "b_loaded"))
        xt_made, xt_copied, logits_made, logits_less_max, exps_made, gate_step, gates_made = (
            sem(n) for n in ("xt_made", "xt_copied", "logits_made", "logits_less_max", "exps_made", "gate_step",
                             "gates_made"))
        expert_made, gelu_made, comb_step, combined, comb_turned, comb_copied, out_made, norm_step, normed = (
            sem(n) for n in ("expert_made", "gelu_made", "comb_step", "combined", "comb_turned", "comb_copied",
                             "out_made", "norm_step", "normed"))
        x2_loaded = [sem(f"x2_loaded{u}") for u in range(2)]
        xt_moved = sem("xt_moved")
        out_stored = [sem(f"out_stored{u}") for u in range(2)]

        block = ctx.enter_context(nc.Block())

        @block.sync
        def _(sp):
            sp.dma_start(id_sb[:, :], identity[:, :]).then_inc(consts, 16)

            def load_x2(b, u):
                reached(sp, xt_made, b - 1)
                sp.dma_start(x2_sb[u][:, :], x2_scr[b]).then_inc(x2_loaded[u], 16)

            sp.dma_start(rw_sb[:, :, :], router_w.rearrange("(c p) e -> p c e", p=128)).then_inc(consts, 16)
            sp.dma_start(rb_sb[:, :], router_b.partition_broadcast(128)).then_inc(consts, 16)
            sp.dma_start(ids_sb[:, :], expert_ids.partition_broadcast(128)).then_inc(consts, 16)
            sp.dma_start(bias[0:ROWS - 2, :], expert_b.rearrange("e (r n) -> (e r) n", n=128)).then_inc(consts, 16)
            sp.dma_start(bias[ROWS - 2:ROWS, :], out_b.rearrange("(r n) -> r n", n=128)).then_inc(consts, 16)
            for c in range(2):
                sp.dma_start(ew_sb[:, c, :, :], expert_w[:, c * 128:(c + 1) * 128, :].rearrange("e p d -> p e d"))\
                    .then_inc(weights, 16)
            sp.dma_start(ow_sb[:, :, :], out_w.rearrange("(c p) n -> p c n", p=128)).then_inc(weights, 16)
            sp.dma_start(x2_all[:, :, :], x2_scr.rearrange("b p d -> p b d")).then_inc(weights, 16)
            sweep(sp, [(0, load_x2)])
            sp.wait_ge(b_step, 6)
            sp.dma_start(bias_scr.rearrange("c (r n) -> r c n", n=128), bias_parts[:, :, :]).then_inc(b_stored, 16)
            sp.wait_ge(b_stored, 16)
            sp.dma_start(bias_sb[:, :], bias_scr[:, :]).then_inc(b_loaded, 16)

            def store_out(b, u):
                sp.wait_ge(normed, b + 1)
                sp.dma_start(out[b], res[u][:, :]).then_inc(out_stored[u], 16)

            sweep(sp, [(3, store_out)])
            for u in range(2):
                sp.wait_ge(out_stored[u], B // 2 * 16)

        @block.tensor
        def _(pe):
            pe.wait_ge(consts, 16 * 6)

            def turn_x2(b, u):
                pe.wait_ge(x2_loaded[u], per_parity(b, u, 16))
                reached(pe, xt_copied, b - 1)
                for c in range(2):
                    last = pe.transpose(ps_t[u][:, c * 128:(c + 1) * 128], x2_sb[u][:, c * 128:(c + 1) * 128],
                                        id_sb[:, :])
                last.then_inc(xt_made, 1)

            def logits(b, u):
                pe.wait_ge(xt_moved, b + 1)
                for c in range(2):
                    last = pe.matmul(ps_l[:, bass.ds(b * E, E)], xt[u][:, c, :], rw_sb[:, c, :],
                                     start=(c == 0), stop=(c == 1))
                last.then_inc(logits_made, 1)

            sweep(pe, [(0, turn_x2), (1, logits)])
            pe.wait_ge(weights, 64)
            pe.wait_ge(b_loaded, 16)

            def expert(j):
                def body(b, u):
                    if j == 0:
                        pe.wait_ge(xt_moved, B + b + 1)
                    reached(pe, gelu_made, PAIRS * (b - 1) + j + 1)
                    pe.matmul(ps_e[j][:, :], ones[:, :], bias_sb[:, 2 * j * D:2 * (j + 1) * D], start=True, stop=False)
                    for c in range(2):
                        last = pe.matmul(ps_e[j][:, :], xt[u][:, c, :],
                                         ew_sb[:, c, 2 * j:2 * j + 2, :].rearrange("p e d -> p (e d)"),
                                         start=False, stop=(c == 1))
                    last.then_inc(expert_made, 1)
                return body

            def turn_comb(b, u):
                pe.wait_ge(combined, b + 1)
                reached(pe, comb_copied, b)
                for c in range(2):
                    last = pe.transpose(ps_c[:, c * 128:(c + 1) * 128], comb[u][:, c * 128:(c + 1) * 128], id_sb[:, :])
                last.then_inc(comb_turned, 1)

            def output(b, u):
                pe.wait_ge(comb_copied, b + 1)
                reached(pe, norm_step, (1 + NORM_OPS) * (b - 1) + 1)
                pe.matmul(ps_o[:, 0:D], ones[:, :], bias_sb[:, E * D:], start=True, stop=False)
                for c in range(2):
                    last = pe.matmul(ps_o[:, 0:D], combt[u][:, c, :], ow_sb[:, c, :], start=False, stop=(c == 1))
                last.then_inc(out_made, 1)

            sweep(pe, [(0, expert(0)), (0, expert(1)), (1, turn_comb), (0, expert(2)), (1, output), (0, expert(3))])

        @block.scalar
        def _(act):
            def copy_xt(b, u):
                act.wait_ge(xt_made, b + 1)
                act.activation(entry(xt_all, b), ps_t[u][:, 0:D].rearrange("p (c n) -> p c n", c=2), ACT.Copy)\
                   .then_inc(xt_copied, 1)

            sweep(act, [(0, copy_xt)])
            act.wait_ge(logits_less_max, 1)
            act.activation(probs[:, :, :], probs[:, :, :], ACT.Exp).then_inc(exps_made, 1)

            def gelus(j):
                def body(b, u):
                    act.wait_ge(expert_made, PAIRS * b + j + 1)
                    if j == 0:
                        reached(act, combined, b - 1)
                    act.activation(ge[u][:, 2 * j:2 * j + 2, :], ps_e[j][:, :].rearrange("p (e d) -> p e d", e=2),
                                   ACT.Gelu_apprx_tanh).then_inc(gelu_made, 1)
                return body

            def copy_combt(b, u):
                act.wait_ge(comb_turned, b + 1)
                reached(act, out_made, b - 1)
                act.activation(combt[u][:, :, :], ps_c[:, 0:D].rearrange("p (c n) -> p c n", c=2), ACT.Copy)\
                   .then_inc(comb_copied, 1)

            sweep(act, [(0, gelus(0)), (0, gelus(1)), (1, copy_combt), (0, gelus(2)), (0, gelus(3))])

        @block.vector
        def _(dve):
            dve.wait_ge(consts, 16 * 6)
            dve.memset(ones[:, :], 1.0).then_inc(b_step, 1)
            chain = Chain(dve, b_step, 0, 0)
            chain.n = 1
            chain.link(dve.tensor_copy(bias_parts[:, 0, :], bias[:, :]))
            chain.link(dve.tensor_tensor(bias_rest[:, :], bias[:, :], bias_parts[:, 0, :], ALU.subtract))
            chain.link(dve.tensor_copy(bias_parts[:, 1, :], bias_rest[:, :]))
            chain.link(dve.tensor_tensor(bias_rest[:, :], bias_rest[:, :], bias_parts[:, 1, :], ALU.subtract))
            chain.link(dve.tensor_copy(bias_parts[:, 2, :], bias_rest[:, :]))

            def by_expert(a):
                return a.unsqueeze(len(a.shape)).broadcast_to([*a.shape, E])

            chain = Chain(dve, gate_step, 0, 0)
            dve.wait_ge(logits_made, B)
            chain.link(dve.tensor_tensor(probs[:, :, :], ps_l[:, 0:B * E].rearrange("p (b e) -> p b e", e=E),
                                         rb_sb[:, :].unsqueeze(1).broadcast_to([128, B, E]), ALU.add))
            chain.link(dve.tensor_reduce(row[:, :], probs[:, :, :], AX.X, ALU.max))
            chain.link(dve.tensor_tensor(probs[:, :, :], probs[:, :, :], by_expert(row[:, :]), ALU.subtract))
            dve.tensor_copy(row_inv[:, :], row[:, :]).then_inc(logits_less_max, 1)
            dve.wait_ge(exps_made, 1)
            chain.link(dve.tensor_reduce(row[:, :], probs[:, :, :], AX.X, ALU.add))
            dve.wait_ge(logits_less_max, 1)
            chain.link(dve.reciprocal(row_inv[:, :], row[:, :]))
            chain.link(dve.tensor_tensor(probs[:, :, :], probs[:, :, :], by_expert(row_inv[:, :]), ALU.mult))
            for b in range(B):
                dve.max(best[:, b, :], probs[:, b, :]).then_inc(gate_step, 1)
                chain.n += 1
            dve.wait_ge(gate_step, chain.n)
            for b in range(B):
                dve.max_index(best_at[:, b, :], best[:, b, :], probs[:, b, :]).then_inc(gate_step, 1)
                chain.n += 1
            dve.wait_ge(gate_step, chain.n)
            chain.link(dve.tensor_tensor(row[:, :], best[:, :, 0], best[:, :, 1], ALU.add))
            chain.link(dve.reciprocal(row_inv[:, :], row[:, :]))
            chain.link(dve.tensor_tensor(share[:, :, :], best[:, :, 0:TOP].rearrange("p b k -> p k b"),
                                         row_inv[:, :].unsqueeze(1).broadcast_to([128, TOP, B]), ALU.mult))
            chain.link(dve.tensor_copy(at[:, :, :], best_at[:, :, 0:TOP].rearrange("p b k -> p k b")))
            for k in range(TOP):
                chain.link(dve.tensor_tensor(chosen[:, k, :, :], ids_sb[:, :].unsqueeze(1).broadcast_to([128, B, E]),
                                             by_expert(at[:, k, :]), ALU.is_equal))
                chain.link(dve.tensor_tensor(chosen[:, k, :, :], chosen[:, k, :, :], by_expert(share[:, k, :]), ALU.mult))
            dve.tensor_tensor(gates[:, :, :], chosen[:, 0, :, :], chosen[:, 1, :, :], ALU.add).then_inc(gates_made, 1)
            dve.wait_ge(gates_made, 1)

            def combine(half):
                def body(b, u):
                    chain = Chain(dve, comb_step, b, E - 1)
                    chain.n = half * E // 2
                    for e in range(half * E // 2, (half + 1) * E // 2):
                        if e % 2 == 0:
                            dve.wait_ge(gelu_made, PAIRS * b + e // 2 + 1)
                        gate = entry(gates, b)[:, e:e + 1]
                        if e == 0:
                            reached(dve, comb_turned, b - 1)
                            ins = dve.tensor_scalar(comb[u][:, :], ge[u][:, e, :], gate, None, ALU.mult)
                        else:
                            ins = dve.scalar_tensor_tensor(comb[u][:, :], ge[u][:, e, :], gate, comb[u][:, :], ALU.mult,
                                                           ALU.add)
                        if e == E - 1:
                            ins.then_inc(combined, 1)
                            dve.wait_ge(combined, b + 1)
                        else:
                            chain.link(ins)
                return body

            def residual_norm(b, u):
                chain = Chain(dve, norm_step, b, 1 + NORM_OPS)
                dve.wait_ge(out_made, b + 1)
                reached(dve, normed, b)
                chain.link(dve.tensor_tensor(y[:, :], ps_o[:, 0:D], entry(x2_all, b), ALU.add))
                layer_norm_stats(dve, chain, y[:, :], stats[:, :], moments[:, :], rstd[:, :], tmp[:, :], bits[:, :])
                chain.done()
                stored_before(dve, out_stored, b, u, 16)
                dve.tensor_scalar(res[u][:, :], y[:, :], moments[:, 0:1], rstd[:, 0:1], ALU.subtract, ALU.mult)\
                   .then_inc(normed, 1)

            sweep(dve, [(0, combine(0)), (2, residual_norm), (0, combine(1))])

        @block.gpsimd
        def _(pool):
            def move_xt(first):
                def body(b, u):
                    if first:
                        pool.wait_ge(xt_copied, b + 1)
                        reached(pool, logits_made, b - 1)
                    else:
                        reached(pool, logits_made, B)
                        reached(pool, expert_made, PAIRS * (b - 1))
                    pool.tensor_copy(xt[u][:, :, :], entry(xt_all, b)).then_inc(xt_moved, 1)
                return body

            sweep(pool, [(0, move_xt(True))])
            sweep(pool, [(0, move_xt(False))])


def decoder_layer(nc, x, ctx_in, mask, attn_w, attn_wo, xattn_wq, xattn_wk, xattn_wv, xattn_bias_qk, xattn_bv,
                  router_w, router_b, expert_w, expert_b, out_w, out_b, rope, identity, in_block, same_head, hidden,
                  self_gather, gather, expert_ids, out):
    scratch = lambda name, shape, dt=F32: nc.dram_tensor(f"scratch_{name}", shape, dt, kind="Internal").ap()
    self_parts = scratch("self_parts", [B, 3, PARTS, HD, H, N], BF16)
    cross_stacks = scratch("cross_stacks", [B, 2, TERMS, XD + 1, H, D], BF16)
    bias_parts = scratch("bias_parts", [PARTS, (E + 1) * D], BF16)
    vk, kb = scratch("vk", [B, N, 2 * D]), scratch("kb", [B, N, D])
    a, t = (scratch(n, [B, H, NC, C, C]) for n in ("a", "t"))
    x1, x2 = (scratch(n, [B, N, D]) for n in ("x1", "x2"))
    with ExitStack() as sems:
        project(nc, sems, x, attn_w, rope, identity, in_block, self_parts, vk, kb, a)
        invert_first(nc, sems, a, t)
        attend(nc, sems, x, attn_wo, identity, same_head, hidden, self_gather, self_parts, vk, kb, a, t, x1)
        cross_attend(nc, sems, x1, ctx_in, mask, xattn_wq, xattn_wk, xattn_wv, xattn_bias_qk, xattn_bv, identity,
                     gather, cross_stacks, x2)
        feed_forward(nc, sems, x2, router_w, router_b, expert_w, expert_b, out_w, out_b, identity, expert_ids,
                     bias_parts, out)


def features_first(w):
    return w.reshape(D, H, HD).transpose(0, 2, 1).reshape(D, D)


def features_first_rows(w):
    return w.reshape(H, XD, -1).swapaxes(0, 1).reshape(w.shape)


def shape_constants():
    import numpy as np

    bf16 = np.dtype("bfloat16")
    f32 = np.float32
    inv = (1.0 / f32(10000.0) ** (np.arange(0, HD, 2, dtype=f32) / f32(HD))).astype(f32)
    angle = np.arange(N, dtype=f32)[:, None] * inv
    cos, sin = np.cos(angle), np.sin(angle)
    cos = np.repeat(np.concatenate([cos, cos], 1), H, 1)
    sin = np.repeat(np.concatenate([-sin, sin], 1), H, 1)
    scale = f32(HD ** -0.5)
    seen = np.tril(np.ones((N, N), bool))
    hidden = np.where(seen, 0.0, OUT_OF_SIGHT)
    self_gather = np.zeros((128, 2, 4 * HD), f32)
    gather = np.zeros((128, 2, 32), f32)
    for j in range(4):
        for d in range(HD):
            self_gather[32 * j + d, 0, HD * j + d] = 1
            self_gather[32 * j + HD, 1, HD * j + d] = 1
        for d in range(XD):
            gather[32 * j + d, 0, XD * j + d] = 1
            gather[32 * j + XD, 1, XD * j + d] = 1
    return {
        "rope": np.stack([np.concatenate([cos * scale, cos], 1), np.concatenate([sin * scale, sin], 1)], 1).astype(f32),
        "identity": np.eye(128, dtype=f32),
        "in_block": -np.tile(np.tril(np.ones((C, C), f32), -1), (NC, 1)),
        "same_head": np.kron(np.eye(8), np.ones((HD, HD))).astype(f32),
        "hidden": np.stack([hidden, hidden.T], 1).astype(bf16),
        "self_gather": self_gather,
        "gather": gather,
        "expert_ids": np.arange(E, dtype=f32),
    }


def kernel(x, ctx_2048, mask_Bx1x2048_fk1, L0_attn_Wq, L0_attn_Wk, L0_attn_Wv, L0_attn_Wo, L0_attn_Wb,
           L0_xattn_Wq, L0_xattn_bq, L0_xattn_Wk, L0_xattn_bk, L0_xattn_Wv, L0_xattn_bv, L0_ffn_router_w,
           L0_ffn_router_b, L0_ffn_expert_w, L0_ffn_expert_b, L0_ffn_out_w, L0_ffn_out_b):
    import numpy as np
    import concourse.bacc as bacc
    from concourse.bass_utils import run_bass_kernel_spmd

    a = np.asarray
    arrays = {
        "x": a(x), "ctx": a(ctx_2048), "mask": a(mask_Bx1x2048_fk1),
        "attn_w": np.concatenate([*(features_first(a(w)) for w in (L0_attn_Wq, L0_attn_Wk, L0_attn_Wv)),
                                  a(L0_attn_Wb)], 1),
        "attn_wo": a(L0_attn_Wo),
        "xattn_wq": features_first_rows(a(L0_xattn_Wq)).T,
        "xattn_wk": features_first_rows(a(L0_xattn_Wk)).T,
        "xattn_wv": a(L0_xattn_Wv).T,
        "xattn_bias_qk": np.stack([features_first_rows(a(L0_xattn_bq)), features_first_rows(a(L0_xattn_bk))], 1),
        "xattn_bv": a(L0_xattn_bv),
        "router_w": a(L0_ffn_router_w), "router_b": a(L0_ffn_router_b),
        "expert_w": a(L0_ffn_expert_w), "expert_b": a(L0_ffn_expert_b),
        "out_w": a(L0_ffn_out_w), "out_b": a(L0_ffn_out_b),
        **shape_constants(),
    }
    nc = bacc.Bacc("TRN2", target_bir_lowering=False, num_devices=1)
    arrays = {f"in_{name}": np.ascontiguousarray(v) for name, v in arrays.items()}
    args = [nc.dram_tensor(name, v.shape, mybir.dt.from_np(v.dtype), kind="ExternalInput").ap()
            for name, v in arrays.items()]
    out = nc.dram_tensor("out", (B, N, D), F32, kind="ExternalOutput").ap()
    decoder_layer(nc, *args, out)
    results = run_bass_kernel_spmd(nc, [arrays], core_ids=[0])
    return results.results[0]["out"]
```

```python
from contextlib import ExitStack

import concourse.bass as bass
from concourse import mybir

F32 = mybir.dt.float32
BF16 = mybir.dt.bfloat16
I32 = mybir.dt.int32
U32 = mybir.dt.uint32
ALU = mybir.AluOpType
ACT = mybir.ActivationFunctionType
AX = mybir.AxisListType

B = 16
N = 128
D = 256
H = 16
HD = D // H
XD = N // H
C = 32
NC = N // C
E = 8
TERMS = 6
PARTS = 3
Q_PARTS = ((0, 3), (1, 2), (2, 1))
K_PARTS = ((0, 3), (0, 2), (0, 1))
NEG = 1.0e6
CROSS_MAX_ROW = 96
OUT_OF_SIGHT = -1.0e30
LN_EPS = 1e-5
L2_EPS = 1e-6
RSQRT_MAGIC = 0x5F3759DF


def reached(eng, sem, count):
    if not (isinstance(count, int) and count <= 0):
        eng.wait_ge(sem, count)


def sweep(eng, stages):
    deepest = max(lag for lag, _ in stages)
    first = (deepest + 3) // 2 * 2
    for t in range(first):
        for lag, body in stages:
            if t >= lag:
                body(t - lag, (t - lag) % 2)
    with eng.Fori(0, (B - first) // 2) as i:
        for half in range(2):
            for lag, body in stages:
                body(2 * i + (first + half - lag), (half - lag) % 2)
    for t in range(B, B + deepest):
        for lag, body in stages:
            if t - lag < B:
                body(t - lag, (t - lag) % 2)


class Chain:

    def __init__(self, eng, sem, b, per):
        self.eng, self.sem, self.base, self.per, self.n = eng, sem, b * per, per, 0

    def link(self, ins):
        self.n += 1
        ins.then_inc(self.sem, 1)
        self.eng.wait_ge(self.sem, self.base + self.n)

    def done(self):
        assert self.n == self.per, (self.n, self.per)


RSQRT_OPS = 11


def rsqrt_op(eng, k, y, x, tmp, bits):
    if k == 0:
        return eng.tensor_scalar(bits, x.bitcast(I32), 1, None, ALU.logical_shift_right)
    if k == 1:
        return eng.tensor_scalar(y.bitcast(I32), bits, -1.0, float(RSQRT_MAGIC), ALU.mult, ALU.add)
    if k % 3 == 2:
        return eng.tensor_tensor(tmp, y, y, ALU.mult)
    if k % 3 == 0:
        return eng.scalar_tensor_tensor(tmp, tmp, -0.5, x, ALU.mult, ALU.mult)
    return eng.scalar_tensor_tensor(y, tmp, 1.5, y, ALU.add, ALU.mult)


NORM_OPS = 3 + RSQRT_OPS


def layer_norm_op(eng, k, y, stats, moments, rstd, tmp, bits):
    if k == 0:
        return eng.bn_stats(stats, y)
    if k == 1:
        eng.memset(bits, 0)
        return eng.bn_aggr(moments, stats)
    if k == 2:
        return eng.tensor_scalar(moments[:, 1:2], moments[:, 1:2], LN_EPS, None, ALU.add)
    return rsqrt_op(eng, k - 3, rstd, moments[:, 1:2], tmp, bits)


def rsqrt(eng, chain, y, x, tmp, bits):
    for k in range(RSQRT_OPS):
        chain.link(rsqrt_op(eng, k, y, x, tmp, bits))


def layer_norm_stats(eng, chain, y, stats, moments, rstd, tmp, bits):
    for k in range(NORM_OPS):
        chain.link(layer_norm_op(eng, k, y, stats, moments, rstd, tmp, bits))


class Phase:

    def __init__(self, nc, ctx, name):
        self.nc, self.ctx, self.name = nc, ctx, name

    def sb(self, name, shape, dt=F32):
        return self.ctx.enter_context(self.nc.sbuf_tensor(f"{self.name}_{name}", shape, dt))

    def two(self, name, shape, dt=F32):
        return [self.sb(f"{name}{u}", shape, dt) for u in range(2)]

    def bank(self, name):
        return self.ctx.enter_context(self.nc.psum_tensor(f"{self.name}_{name}", [128, 512], F32))

    def sem(self, name):
        return self.ctx.enter_context(self.nc.semaphore(f"{self.name}_{name}"))


class Constants:

    def __init__(self, nc, ctx):
        self.nc, self.ctx, self.pairs = nc, ctx, []
        self.loaded = ctx.enter_context(nc.semaphore("constants_loaded"))

    def tile(self, name, shape, dt=F32):
        return self.ctx.enter_context(self.nc.sbuf_tensor(f"const_{name}", shape, dt))

    def wait(self, eng):
        eng.wait_ge(self.loaded, 16 * len(self.pairs))


def cross_constants(c, mask, wq, wk, wv, bias_qk, bv, identity, gather, stack_rows):
    c.id_sb = c.tile("id", [128, 128])
    c.m16 = c.tile("m16", [B, 2, D])
    c.w_sb = c.tile("w", [128, 3, N])
    c.b_sb = c.tile("b", [128, 2])
    c.bv_sb = c.tile("bv", [128, N])
    c.gather_sb = c.tile("gather", [128, 2, 32])
    c.qst, c.kst = ([c.tile(f"{side}st{u}", [CROSS_MAX_ROW + 2, H, D], BF16) for u in range(2)] for side in "qk")
    fixed = TERMS * (XD + 1)
    c.pairs += [(stack[u][fixed:, :, :], stack_rows[side].unsqueeze(1).broadcast_to([CROSS_MAX_ROW + 2 - fixed, H, D]))
                for side, stack in enumerate((c.qst, c.kst)) for u in range(2)]
    c.pairs += [(c.id_sb[:, :], identity[:, :]), (c.b_sb[:, :], bias_qk[:, :]),
                (c.bv_sb[:, :], bv.partition_broadcast(128)), (c.gather_sb[:, :, :], gather[:, :, :])]
    c.pairs += [(c.m16[:, side, :], mask.rearrange("b a t -> (b a) t")) for side in range(2)]
    c.pairs += [(c.w_sb[:, n, :], w[:, :]) for n, w in enumerate((wq, wk, wv))]


def feed_forward_constants(c, router_w, router_b, expert_w, expert_b, out_w, out_b, expert_ids):
    rows = (E + 1) * D // 128
    c.rw_sb = c.tile("rw", [128, 2, E])
    c.rb_sb = c.tile("rb", [128, E])
    c.ids_sb = c.tile("ids", [128, E])
    c.bias = c.tile("bias", [rows, 128])
    c.ew_sb = c.tile("ew", [128, 2, E, D])
    c.ow_sb = c.tile("ow", [128, 2, D])
    c.pairs += [(c.rw_sb[:, :, :], router_w.rearrange("(c p) e -> p c e", p=128)),
                (c.rb_sb[:, :], router_b.partition_broadcast(128)), (c.ids_sb[:, :], expert_ids.partition_broadcast(128)),
                (c.bias[0:rows - 2, :], expert_b.rearrange("e (r n) -> (e r) n", n=128)),
                (c.bias[rows - 2:rows, :], out_b.rearrange("(r n) -> r n", n=128)),
                (c.ow_sb[:, :, :], out_w.rearrange("(c p) n -> p c n", p=128))]
    c.pairs += [(c.ew_sb[:, n, :, :], expert_w[:, n * 128:(n + 1) * 128, :].rearrange("e p d -> p e d"))
                for n in range(2)]


BATCH = 4
FIRST = 2 * BATCH
PIECES = 7


def invert_step(eng, j, half, t, a, product):
    n, rows = a.shape[1], C - 1 - j
    shape = [128, n, j, rows]
    part = product[:, :, 0:j * rows].rearrange("p n (c i) -> p n c i", c=j)
    below = t[:, :, 0:j, j + 1:C]
    if half == 0:
        return eng.tensor_tensor(part, a[:, :, j + 1:C, j].unsqueeze(2).broadcast_to(shape),
                                 t[:, :, 0:j, j:j + 1].broadcast_to(shape), ALU.mult)
    return eng.tensor_tensor(below, below, part, ALU.add)


INVERT_STEPS = 2 * (C - 2)
DIAGONAL = slice(0, C * C, C + 1)


def invert_piece(eng, step, first, last, a, t, product):
    for k in range(first, min(last, 2 + INVERT_STEPS)):
        if k:
            eng.wait_ge(step, k)
        if k == 0:
            ins = eng.tensor_copy(t[:, :, :, :].rearrange("p n j i -> p n i j"), a[:, :, :, :])
        elif k == 1:
            ins = eng.memset(t[:, :, :, :].rearrange("p n j i -> p n (j i)")[:, :, DIAGONAL], 1.0)
        else:
            ins = invert_step(eng, k // 2, k % 2, t, a, product)
        ins.then_inc(step, 1)


def systems(scr, batch):
    return scr[batch * BATCH:(batch + 1) * BATCH].rearrange("(g b) h c i j -> (b h c) g (i j)", b=2)


def project(nc, sems, x, w, rope, identity, in_block, parts_scr, vk_scr, kb_scr, a_scr, t_scr):
    with ExitStack() as ctx:
        ph = Phase(nc, ctx, "pr")
        sem = lambda name: sems.enter_context(nc.semaphore(f"pr_{name}"))
        w_sb = ph.sb("w", [128, 2, 3 * D + H])
        rope_sb = ph.sb("rope", [128, 2, 2 * D])
        id_sb = ph.sb("id", [128, 128])
        below_sb = ph.sb("below", [128, C])
        x_sb = ph.two("x", [128, D])
        xt_sb = ph.two("xt", [128, 2, 128])
        with_cos = ph.sb("with_cos", [128, 2 * D])
        with_sin = ph.sb("with_sin", [128, 2 * D])
        qk = ph.two("qk", [128, 2 * D])
        ksq = ph.two("ksq", [128, D])
        ez = ph.two("ez", [128, H])
        beta = ph.sb("beta", [128, H])
        ss = ph.sb("ss", [128, H])
        knorm = ph.sb("knorm", [128, 2, H])
        tmp = ph.sb("tmp", [128, H])
        bits = ph.sb("bits", [128, H], I32)
        vk = ph.two("vk", [128, 2 * HD, H])
        kb = ph.two("kb", [128, D])
        kbh = ph.two("kbh", [128, H, HD])
        rest = ph.two("rest", [128, 3, D])
        parts = ph.two("parts", [128, 3, PARTS, 2, 128], BF16)
        kst = ph.two("kst", [TERMS * HD, H, N], BF16)
        kbst = ph.two("kbst", [TERMS * HD, H, N], BF16)
        a_sb = ph.two("a", [128, H, C])
        a_first, t_first = (ph.sb(n, [128, BATCH // 2, C, C]) for n in ("a_first", "t_first"))
        product_first = ph.sb("product_first", [128, BATCH // 2, C * C])
        ps_x, ps_qk, ps_vb, ps_qb, ps_k, ps_a = (ph.bank(n) for n in ("x", "qk", "vb", "qb", "k", "a"))

        consts = sem("consts")
        x_loaded = [sem(f"x_loaded{u}") for u in range(2)]
        xt_made, xt_copied = sem("xt_made"), sem("xt_copied")
        projected, v_copied, ez_made = sem("projected"), sem("v_copied"), sem("ez_made")
        rope_halves, rotated, squared = sem("rope_halves"), sem("rotated"), sem("squared")
        norm_step, norms_made = sem("norm_step"), sem("norms_made")
        k_scaled, kb_scaled, kb_turned = sem("k_scaled"), sem("kb_scaled"), sem("kb_turned")
        turned, part1, rest_made, part2, part3 = (
            sem("turned"), sem("part1"), sem("rest_made"), sem("part2"), sem("part3"))
        kb_stored = [sem(f"kb_stored{u}") for u in range(2)]
        vk_stored = [sem(f"vk_stored{u}") for u in range(2)]
        parts_stored = [sem(f"parts_stored{u}") for u in range(2)]
        a_stored = [sem(f"a_stored{u}") for u in range(2)]
        stacks_loaded = [sem(f"stacks_loaded{u}") for u in range(2)]
        a_made, a_masked = sem("a_made"), sem("a_masked")

        first_loaded, first_step, first_stored = sem("first_loaded"), sem("first_step"), sem("first_stored")

        block = ctx.enter_context(nc.Block())

        @block.sync
        def _(sp):
            sp.dma_start(id_sb[:, :], identity[:, :]).then_inc(consts, 16)
            sp.dma_start(w_sb[:, :, :], w.rearrange("(c p) n -> p c n", p=128)).then_inc(consts, 16)
            sp.dma_start(rope_sb[:, :, :], rope[:, :, :]).then_inc(consts, 16)
            sp.dma_start(below_sb[:, :], in_block[:, :]).then_inc(consts, 16)

            def load_x(b, u):
                reached(sp, xt_made, b - 1)
                sp.dma_start(x_sb[u][:, :], x[b]).then_inc(x_loaded[u], 16)

            def store_vk(b, u):
                sp.wait_ge(v_copied, b + 1)
                sp.wait_ge(k_scaled, b + 1)
                sp.dma_start(vk_scr[b], vk[u][:, :, :]).then_inc(vk_stored[u], 16)

            def store_kb(b, u):
                sp.wait_ge(kb_turned, b + 1)
                sp.dma_start(kb_scr[b], kbh[u][:, :, :]).then_inc(kb_stored[u], 16)

            def store_parts(b, u):
                sp.wait_ge(part3, b + 1)
                sp.dma_start(parts_scr[b].rearrange("t c (g d) h n -> (d h) (t c g) n", g=2),
                             parts[u][:, :, :, :, :]).then_inc(parts_stored[u], 16)

            def load_stacks(b, u):
                reached(sp, a_made, b - 1)
                stored(sp, parts_stored, b, u)
                load_stack(sp, kst[u], parts_scr[b, 2], Q_PARTS, True, stacks_loaded[u])
                load_stack(sp, kbst[u], parts_scr[b, 1], K_PARTS, False, stacks_loaded[u])

            def store_a(b, u):
                sp.wait_ge(a_masked, b + 1)
                sp.dma_start(a_scr[b].rearrange("h c i j -> (c i) h j"), a_sb[u][:, :, :])\
                    .then_inc(a_stored[u], 16)

            def stored(eng, pair, b, u):
                eng.wait_ge(pair[u], per_parity(b, u, 16))

            def load_first(b, u):
                if isinstance(b, int) and b == B - 9:
                    for parity in range(2):
                        sp.wait_ge(a_stored[parity], BATCH // 2 * 16)
                    sp.dma_start(a_first[:, :, :, :].rearrange("p n i j -> p n (i j)"), systems(a_scr, 0))\
                        .then_inc(first_loaded, 16)

            sweep(sp, [(9, load_first), (0, load_x), (4, store_kb), (5, store_parts), (9, store_a),
                       (6, load_stacks), (3, store_vk)])
            sp.wait_ge(first_step, 2 + INVERT_STEPS)
            sp.dma_start(systems(t_scr, 0), t_first[:, :, :, :].rearrange("p n j i -> p n (j i)"))\
                .then_inc(first_stored, 16)
            sp.wait_ge(first_stored, 16)
            for u in range(2):
                sp.wait_ge(vk_stored[u], B // 2 * 16)
                sp.wait_ge(kb_stored[u], B // 2 * 16)
                sp.wait_ge(parts_stored[u], B // 2 * 16)
                sp.wait_ge(a_stored[u], B // 2 * 16)

        @block.tensor
        def _(pe):
            pe.wait_ge(consts, 64)

            def transpose_x(b, u):
                pe.wait_ge(x_loaded[u], per_parity(b, u, 16))
                reached(pe, xt_copied, b)
                for c in range(2):
                    last = pe.transpose(ps_x[:, c * 128:(c + 1) * 128], x_sb[u][:, c * 128:(c + 1) * 128],
                                        id_sb[:, :])
                last.then_inc(xt_made, 1)

            def gram(b, u):
                pe.wait_ge(stacks_loaded[u], per_parity(b, u, 96))
                reached(pe, a_masked, b)
                for h in range(H):
                    for c in range(NC):
                        t = slice(c * C, (c + 1) * C)
                        last = pe.matmul(ps_a[t, h * C:(h + 1) * C], kst[u][:, h, t], kbst[u][:, h, t],
                                         start=True, stop=True)
                last.then_inc(a_made, 1)

            def transpose_qk(b, u):
                pe.wait_ge(kb_scaled, b + 1)
                reached(pe, part1, b)
                reached(pe, rest_made, b)
                k = vk[u][:, HD:2 * HD, :].rearrange("p d h -> p (d h)")
                for g in range(2):
                    half = slice(g * 128, (g + 1) * 128)
                    pe.transpose(ps_qb[:, g * 128:(g + 1) * 128], qk[u][:, half], id_sb[:, :])
                    pe.transpose(ps_qb[:, D + g * 128:D + (g + 1) * 128], kb[u][:, half], id_sb[:, :])
                    last = pe.transpose(ps_k[:, g * 128:(g + 1) * 128], k[:, half], id_sb[:, :])
                last.then_inc(turned, 1)

            def products(b, u):
                pe.wait_ge(xt_copied, b + 1)
                reached(pe, rope_halves, b)
                reached(pe, v_copied, b)
                reached(pe, ez_made, b)
                for c in range(2):
                    pe.matmul(ps_qk[:, :], xt_sb[u][:, c, :], w_sb[:, c, 0:2 * D], start=(c == 0), stop=(c == 1))
                for c in range(2):
                    last = pe.matmul(ps_vb[:, 0:D + H], xt_sb[u][:, c, :], w_sb[:, c, 2 * D:3 * D + H],
                                     start=(c == 0), stop=(c == 1))
                last.then_inc(projected, 1)

            sweep(pe, [(1, products), (3, transpose_qk), (0, transpose_x), (7, gram)])

        @block.scalar
        def _(act):
            def copy_xt(b, u):
                act.wait_ge(xt_made, b + 1)
                reached(act, projected, b - 1)
                act.activation(xt_sb[u][:, :, :], ps_x[:, 0:D].rearrange("p (c n) -> p c n", c=2),
                               ACT.Copy).then_inc(xt_copied, 1)

            def first_part(b, u):
                act.wait_ge(turned, b + 1)
                stored_before(act, parts_stored, b, u, 16)
                act.activation(parts[u][:, 0:2, 0, :, :],
                               ps_qb[:, :].rearrange("p (t g n) -> p t g n", t=2, g=2), ACT.Copy)
                act.activation(parts[u][:, 2, 0, :, :],
                               ps_k[:, 0:D].rearrange("p (g n) -> p g n", g=2), ACT.Copy)\
                   .then_inc(part1, 1)

            def second_part(b, u):
                act.wait_ge(rest_made, b + 1)
                act.activation(parts[u][:, :, 1, :, :], rest[u][:, :, :].rearrange("p t (g n) -> p t g n", g=2),
                               ACT.Copy).then_inc(part2, 1)

            def v_and_beta(b, u):
                act.wait_ge(projected, b + 1)
                stored_before(act, vk_stored, b, u, 16)
                reached(act, norms_made, b - 1)
                act.activation(ez[u][:, :], ps_vb[:, D:D + H], ACT.Exp, scale=-1.0).then_inc(ez_made, 1)
                act.activation(vk[u][:, 0:HD, :].rearrange("p d h -> p (d h)"), ps_vb[:, 0:D],
                               ACT.Copy).then_inc(v_copied, 1)

            def turn_kb(b, u):
                act.wait_ge(kb_scaled, b + 1)
                stored_before(act, kb_stored, b, u, 16)
                act.activation(kbh[u][:, :, :], kb[u][:, :].rearrange("p (d h) -> p h d", h=H), ACT.Copy)\
                   .then_inc(kb_turned, 1)

            sweep(act, [(4, second_part), (3, turn_kb), (1, v_and_beta), (3, first_part), (0, copy_xt)])

        @block.vector
        def _(dve):
            dve.wait_ge(consts, 64)

            def mask_a(b, u):
                dve.wait_ge(a_made, b + 1)
                stored_before(dve, a_stored, b, u, 16)
                dve.tensor_tensor(a_sb[u][:, :, :], ps_a[:, :].rearrange("p (h j) -> p h j", h=H),
                                  below_sb[:, :].unsqueeze(1).broadcast_to([128, H, C]), ALU.mult)\
                   .then_inc(a_masked, 1)

            def residue(b, u):
                dve.wait_ge(part1, b + 1)
                reached(dve, part3, b - 1)
                dve.tensor_tensor(rest[u][:, 0:2, :].rearrange("p t n -> p (t n)"), ps_qb[:, :],
                                  parts[u][:, 0:2, 0, :, :], ALU.subtract)
                dve.tensor_tensor(rest[u][:, 2, :], ps_k[:, 0:D], parts[u][:, 2, 0, :, :],
                                  ALU.subtract).then_inc(rest_made, 1)

            def rotate(b, u):
                dve.wait_ge(projected, b + 1)
                reached(dve, rotated, b)
                dve.tensor_tensor(with_cos[:, :], ps_qk[:, :], rope_sb[:, 0, :], ALU.mult)
                swapped = ps_qk[:, :].rearrange("p (t s m) -> p t s m", t=2, s=2)[:, :, ::-1, :]
                dve.tensor_tensor(with_sin[:, :].rearrange("p (t s m) -> p t s m", t=2, s=2), swapped,
                                  rope_sb[:, 1, :].rearrange("p (t s m) -> p t s m", t=2, s=2),
                                  ALU.mult).then_inc(rope_halves, 1)

            def norms(b, u):
                chain = Chain(dve, norm_step, b, RSQRT_OPS + 5)
                dve.wait_ge(ez_made, b + 1)
                chain.link(dve.tensor_scalar(beta[:, :], ez[u][:, :], 0.5, 0.5, ALU.mult, ALU.add))
                reached(dve, kb_scaled, b)
                chain.link(dve.reciprocal(knorm[:, 1, :], beta[:, :]))
                dve.wait_ge(squared, b + 1)
                chain.link(dve.tensor_reduce(ss[:, :], ksq[u][:, :].rearrange("p (d h) -> p h d", h=H), AX.X, ALU.add))
                chain.link(dve.tensor_scalar(ss[:, :], ss[:, :], L2_EPS, None, ALU.add))
                rsqrt(dve, chain, knorm[:, 0, :], ss[:, :], tmp[:, :], bits[:, :])
                chain.link(dve.tensor_tensor(knorm[:, 1, :], knorm[:, 1, :], knorm[:, 0, :], ALU.mult))
                chain.done()
                dve.tensor_copy(tmp[:, 0:1], knorm[:, 0, 0:1]).then_inc(norms_made, 1)

            def invert_first(b, u):
                if isinstance(b, int) and b >= B - PIECES:
                    if b == B - PIECES:
                        dve.wait_ge(first_loaded, 16)
                    length = -(-(2 + INVERT_STEPS) // PIECES)
                    start = (b - (B - PIECES)) * length
                    invert_piece(dve, first_step, start, start + length, a_first, t_first, product_first)

            sweep(dve, [(1, rotate), (2, norms), (3, residue), (7, mask_a), (7, invert_first)])

        @block.gpsimd
        def _(pool):
            def third_part(b, u):
                pool.wait_ge(part2, b + 1)
                pool.tensor_tensor(parts[u][:, :, 2, :, :].rearrange("p t g n -> p t (g n)"), rest[u][:, :, :],
                                   parts[u][:, :, 1, :, :].rearrange("p t g n -> p t (g n)"),
                                   ALU.subtract).then_inc(part3, 1)

            def rotate_sum(b, u):
                pool.wait_ge(rope_halves, b + 1)
                reached(pool, turned, b - 1)
                pool.tensor_tensor(qk[u][:, :], with_cos[:, :], with_sin[:, :], ALU.add).then_inc(rotated, 1)
                pool.wait_ge(rotated, b + 1)
                pool.tensor_tensor(ksq[u][:, :], qk[u][:, D:2 * D], qk[u][:, D:2 * D], ALU.mult)\
                    .then_inc(squared, 1)

            def scale_k(b, u):
                pool.wait_ge(norms_made, b + 1)
                stored_before(pool, vk_stored, b, u, 16)
                reached(pool, turned, b - 1)
                reached(pool, kb_turned, b - 1)
                k = qk[u][:, D:2 * D].rearrange("p (d h) -> p d h", h=H)
                pool.tensor_tensor(vk[u][:, HD:2 * HD, :], k,
                                   knorm[:, 0, :].unsqueeze(1).broadcast_to([128, HD, H]),
                                   ALU.mult).then_inc(k_scaled, 1)
                pool.tensor_tensor(kb[u][:, :].rearrange("p (d h) -> p d h", h=H), k,
                                   knorm[:, 1, :].unsqueeze(1).broadcast_to([128, HD, H]),
                                   ALU.mult).then_inc(kb_scaled, 1)

            sweep(pool, [(4, third_part), (1, rotate_sum), (2, scale_k)])


def per_parity(b, u, per):
    return b * (per // 2) + (2 - u) * (per // 2)


def stored_before(eng, pair, b, u, per):
    reached(eng, pair[u], (b - u) * (per // 2))


def at_most(eng, sem, b, ahead):
    eng.wait_ge(sem, min(b + ahead, B) if isinstance(b, int) else b + ahead)


def entry(a, b):
    rest = " ".join("abcd"[:len(a.shape) - 3])
    return a[:, bass.ds(b, 1)].rearrange(f"p o n {rest} -> p (o n) {rest}")


def load_stack(eng, stack, parts, which, repeats, loaded):
    row = 0
    d = parts.shape[1]
    for part, n in which:
        src = parts[part:part + (1 if repeats else n)].rearrange("c d h n -> c d (h n)")
        if repeats:
            src = src.broadcast_to([n, d, src.shape[2]])
        else:
            src = src.rearrange("c d m -> (c d) m")
        eng.dma_start(stack[row:row + n * d, :, :].rearrange("p h n -> p (h n)"), src).then_inc(loaded, 16)
        row += n * d


def attend(nc, sems, x, wo, identity, same_head, hidden, gather, parts_scr, vk_scr, kb_scr, a_scr, t_scr,
           x1_scr, later):
    HV = 32
    G = 2
    QUADS = H // 4
    MAX_ROW = TERMS * HD
    with ExitStack() as ctx:
        ph = Phase(nc, ctx, "at")
        sem = lambda name: sems.enter_context(nc.semaphore(f"at_{name}"))
        wo_sb = ph.sb("wo", [128, 2, D])
        id_sb = ph.sb("id", [128, 128])
        idb_sb = ph.sb("idb", [128, 128], BF16)
        same_sb = ph.sb("same", [128, 128])
        hidden_sb = ph.sb("hidden", [128, 2, 128], BF16)
        a_second, t_second = (ph.sb(n, [128, BATCH // 2, C, C]) for n in ("a_second", "t_second"))
        product_second = ph.sb("product_second", [128, BATCH // 2, C * C])
        a_sys = ph.sb("a_sys", [128, 2, C, C])
        t_sys = ph.sb("t_sys", [128, 2, C, C])
        product = ph.sb("product", [128, 2, C * C])
        unit = ph.sb("unit", [128, C * C])
        t_sb = ph.two("t", [128, H, C])
        vk = ph.two("vk", [128, 2 * HD, H])
        kb = ph.two("kb", [128, D])
        qst = ph.two("qst", [MAX_ROW + 2, H, N], BF16)
        kst = ph.two("kst", [MAX_ROW + 2, H, N], BF16)
        x_sb = ph.two("x", [128, D])
        xa = ph.two("xa", [128, H, HV])
        tk = ph.two("tk", [128, H, HD])
        tkt = ph.two("tkt", [128, G, 128])
        state = ph.sb("state", [128, G, 128])
        nmax = ph.two("nmax", [128, H])
        nmaxt = ph.two("nmaxt", [H, 2, N], BF16)
        p = ph.two("p", [128, 4, N])
        gather_sb = ph.sb("gather", [128, 2, 4 * HD])
        r_sb = ph.sb("r", [128, QUADS, N])
        rden = ph.sb("rden", [128, 2 * N])
        ot = ph.two("ot", [128, 2, N])
        y = ph.two("y", [128, D])
        x1 = ph.two("x1", [128, D])
        stats, moments = ph.sb("stats", [128, 6]), ph.sb("moments", [128, 2])
        rstd, tmp, bits = ph.sb("rstd", [128, 1]), ph.sb("tmp", [128, 1]), ph.sb("bits", [128, 1], I32)
        ps_x, ps_c, ps_o, ps_w = (ph.bank(n) for n in ("x", "c", "o", "w"))
        ps_s1 = [ph.bank(f"s1{i}") for i in range(2)]
        ps_s2 = [ph.bank(f"s2{i}") for i in range(2)]
        nmaxt_ps = ps_w[0:H, 0:128]

        consts, consts_made = sem("consts"), sem("consts_made")
        kb_loaded = [sem(f"kb_loaded{u}") for u in range(2)]
        y_made, ones_step = sem("y_made"), sem("ones_step")
        tv_loaded = [sem(f"tv_loaded{u}") for u in range(2)]
        st_loaded = [sem(f"st_loaded{u}") for u in range(2)]
        x_loaded = [sem(f"x_loaded{u}") for u in range(2)]
        applied, x_copied, tk_turned, tkt_copied = (
            sem("applied"), sem("x_copied"), sem("tk_turned"), sem("tkt_copied"))
        u_made, state_made, r_made, xa_made = sem("u_made"), sem("state_made"), sem("r_made"), sem("xa_made")
        s1_made, max_made, max_turned = sem("s1_made"), sem("max_made"), sem("max_turned")
        max_hi, max_lo = sem("max_hi"), sem("max_lo")
        s2_made, exp_made, pv_made, rden_made, o_made = (
            sem("s2_made"), sem("exp_made"), sem("pv_made"), sem("rden_made"), sem("o_made"))
        r_copied, gathered, wo_made, norm_step, x1_made = (
            sem("r_copied"), sem("gathered"), sem("wo_made"), sem("norm_step"), sem("x1_made"))
        x1_stored = [sem(f"x1_stored{u}") for u in range(2)]
        max_placed = [sem(f"max_placed{u}") for u in range(2)]
        second_loaded, second_step, second_stored = sem("second_loaded"), sem("second_step"), sem("second_stored")
        t_ready = sem("t_ready")
        a_loaded, t_stored, t_step, unit_made = sem("a_loaded"), sem("t_stored"), sem("t_step"), sem("unit_made")
        STEPS = NC - 1
        SPREAD, BETWEEN = 2, 13

        block = ctx.enter_context(nc.Block())

        @block.gpsimd
        def _(pool):
            def batch(n):
                base = n * (2 + INVERT_STEPS)
                entries = FIRST // BATCH + n
                pool.dma_start(a_sys[:, :, :, :].rearrange("p n i j -> p n (i j)"), systems(a_scr, entries))\
                    .then_inc(a_loaded, 16)
                pool.wait_ge(a_loaded, n * 16 + 16)
                for g in range(2):
                    pool.tensor_tensor(t_sys[:, g, :, :].rearrange("p j i -> p i j"), a_sys[:, g, :, :],
                                       unit[:, :].rearrange("p (i j) -> p i j", i=C), ALU.add).then_inc(t_step, 1)
                for j in range(1, C - 1):
                    for half in range(2):
                        pool.wait_ge(t_step, base + 2 * j + half)
                        invert_step(pool, j, half, t_sys, a_sys, product).then_inc(t_step, 1)
                pool.wait_ge(t_step, base + 2 + INVERT_STEPS)
                pool.dma_start(systems(t_scr, entries), t_sys[:, :, :, :].rearrange("p n j i -> p n (j i)"))\
                    .then_inc(t_stored, 16)
                pool.wait_ge(t_stored, n * 16 + 16)
                pool.tensor_tensor(product[:, 0, 0:1], unit[:, 0:1], unit[:, 0:1], ALU.add).then_inc(t_ready, BATCH)

            pool.memset(unit[:, :], 0.0).then_inc(unit_made, 1)
            pool.wait_ge(unit_made, 1)
            pool.memset(unit[:, DIAGONAL], 1.0).then_inc(unit_made, 1)
            pool.wait_ge(unit_made, 2)
            for n in range((B - FIRST) // BATCH):
                batch(n)

        @block.sync
        def _(sp):
            sp.dma_start(a_second[:, :, :, :].rearrange("p n i j -> p n (i j)"),
                         systems(a_scr, 1)).then_inc(second_loaded, 16)
            sp.dma_start(id_sb[:, :], identity[:, :]).then_inc(consts, 16)
            sp.dma_start(wo_sb[:, :, :], wo.rearrange("(c p) n -> p c n", p=128)).then_inc(consts, 16)
            sp.dma_start(same_sb[:, :], same_head[:, :]).then_inc(consts, 16)
            sp.dma_start(hidden_sb[:, :, :], hidden[:, :, :]).then_inc(consts, 16)
            sp.dma_start(gather_sb[:, :, :], gather[:, :, :]).then_inc(consts, 16)

            for tile, source in later.pairs:
                sp.dma_start(tile, source).then_inc(later.loaded, 16)

            def store_second(b, u):
                if isinstance(b, int) and b == BATCH:
                    sp.wait_ge(second_step, 2 + INVERT_STEPS)
                    sp.dma_start(systems(t_scr, 1), t_second[:, :, :, :].rearrange("p n j i -> p n (j i)"))\
                        .then_inc(second_stored, 16)

            def load_tv(b, u):
                reached(sp, applied, b - 1)
                if isinstance(b, int) and BATCH <= b < FIRST:
                    sp.wait_ge(second_stored, 16)
                reached(sp, t_ready, b - (FIRST - 1))
                sp.dma_start(t_sb[u][:, :, :], t_scr[b].rearrange("h c j i -> (c j) h i")).then_inc(tv_loaded[u], 16)
                sp.dma_start(vk[u][:, :, :], vk_scr[b].rearrange("p (d h) -> p d h", h=H)).then_inc(tv_loaded[u], 16)

            def load_kb(b, u):
                reached(sp, u_made, STEPS * (b - 1))
                sp.dma_start(kb[u][:, :], kb_scr[b]).then_inc(kb_loaded[u], 16)

            def load_st(b, u):
                reached(sp, s2_made, QUADS * (b - 1))
                load_stack(sp, qst[u][0:MAX_ROW], parts_scr[b, 0], Q_PARTS, True, st_loaded[u])
                load_stack(sp, kst[u][0:MAX_ROW], parts_scr[b, 1], K_PARTS, False, st_loaded[u])

            def place_max(b, u):
                sp.wait_ge(max_lo, b + 1)
                for part in range(2):
                    row = MAX_ROW + part
                    sp.dma_start(qst[u][row:row + 1, :, :], nmaxt[u][:, part, :]).then_inc(max_placed[u], 16)

            def load_x(b, u):
                reached(sp, y_made, b - 1)
                sp.dma_start(x_sb[u][:, :], x[b]).then_inc(x_loaded[u], 16)

            def store_x1(b, u):
                sp.wait_ge(x1_made, b + 1)
                sp.dma_start(x1_scr[b], x1[u][:, :]).then_inc(x1_stored[u], 16)

            sweep(sp, [(4, place_max), (2, load_st), (7, store_x1), (2, load_kb), (0, store_second),
                       (0, load_tv), (4, load_x)])
            for u in range(2):
                sp.wait_ge(x1_stored[u], B // 2 * 16)

        @block.tensor
        def _(pe):
            pe.wait_ge(consts, 80)
            pe.wait_ge(consts_made, 5)

            def apply_t(q):
                def body(b, u):
                    if q == 0:
                        pe.wait_ge(tv_loaded[u], per_parity(b, u, 32))
                        reached(pe, x_copied, b)
                        pe.matmul(ps_x[:, 0:1], idb_sb[:, :], idb_sb[:, 0:1], start=True, stop=True)
                    for h in range(4 * q, 4 * q + 4):
                        for c in range(NC):
                            t = slice(c * C, (c + 1) * C)
                            last = pe.matmul(ps_x[t, h * C:(h + 1) * C], t_sb[u][t, h, :], vk[u][t, :, h],
                                             start=True, stop=True)
                    if q == QUADS - 1:
                        last.then_inc(applied, 1)
                return body

            def turn_tk(b, u):
                pe.wait_ge(x_copied, b + 1)
                reached(pe, xa_made, STEPS * b)
                for g in range(G):
                    last = pe.transpose(ps_c[:, D + g * 128:D + (g + 1) * 128],
                                        tk[u][:, g * 8:(g + 1) * 8, :].rearrange("p h d -> p (h d)"), id_sb[:, :])
                last.then_inc(tk_turned, 1)

            def new_state(c):
                def body(b, u):
                    if c == 1:
                        pe.wait_ge(kb_loaded[u], per_parity(b, u, 16))
                        pe.wait_ge(tkt_copied, b + 1)
                    else:
                        pe.wait_ge(xa_made, STEPS * b + c - 1)
                    for g in range(G):
                        last = pe.matmul(ps_c[:, g * 128:(g + 1) * 128], kb[u][0:c * C, g * 128:(g + 1) * 128],
                                         xa[u][0:c * C, g * 8:(g + 1) * 8, 0:HD], start=True, stop=True)
                    last.then_inc(u_made, 1)
                return body

            def read_state(c):
                def body(b, u):
                    pe.wait_ge(state_made, STEPS * b + c)
                    t = slice(c * C, (c + 1) * C)
                    for g in range(G):
                        last = pe.matmul(ps_c[t, D + g * 128:D + (g + 1) * 128], tkt[u][:, g, t], state[:, g, :],
                                         start=True, stop=True)
                    last.then_inc(r_made, 1)
                return body

            def scores(ps, kind, left, right, q, rows):
                pe.matmul(ps[:, :], idb_sb[:, :], hidden_sb[:, kind, :].unsqueeze(1).broadcast_to([128, 4, 128]),
                          start=True, stop=False, skip_group_check=True)
                for j in range(4):
                    h = 4 * q + j
                    out = ps[:, j * 128:(j + 1) * 128]
                    last = pe.matmul(out, left[0:rows, h, :], right[0:rows, h, :], start=False, stop=True,
                                     skip_group_check=True)
                return last

            def by_query(q):
                def body(b, u):
                    if q == 0:
                        pe.wait_ge(st_loaded[u], per_parity(b, u, 96))
                    reached(pe, max_made, QUADS * b + q - 1)
                    scores(ps_s1[q % 2], 0, qst[u], kst[u], q, MAX_ROW).then_inc(s1_made, 1)
                return body

            def turn_max(b, u):
                pe.wait_ge(max_made, QUADS * (b + 1))
                reached(pe, y_made, b - 1)
                pe.transpose(nmaxt_ps, nmax[u][:, :], id_sb[:, :]).then_inc(max_turned, 1)

            def by_key(q):
                def body(b, u):
                    if q == 0:
                        pe.wait_ge(max_placed[u], per_parity(b, u, 32))
                    reached(pe, exp_made, QUADS * b + q - 1)
                    scores(ps_s2[q % 2], 1, kst[u], qst[u], q, MAX_ROW + 2).then_inc(s2_made, 1)
                return body

            def values(q):
                def body(b, u):
                    if q == 0:
                        pe.wait_ge(xa_made, STEPS * (b + 1))
                        reached(pe, o_made, b)
                    pe.wait_ge(exp_made, QUADS * b + q + 1)
                    for j in range(4):
                        h = 4 * q + j
                        last = pe.matmul(ps_o[32 * j:32 * j + 32, q * N:(q + 1) * N], xa[u][:, h, :], p[q % 2][:, j, :],
                                         start=True, stop=True)
                    last.then_inc(pv_made, 1)
                return body

            def gather_quads(b, u):
                pe.wait_ge(r_copied, b + 1)
                for n in range(2):
                    for q in range(QUADS):
                        rows = slice(64 * (q % 2), 64 * (q % 2) + 64)
                        col = n * 2 * N + q // 2 * N
                        last = pe.matmul(ps_o[rows, col:col + N], gather_sb[:, n, :], r_sb[:, q, :], start=True, stop=True)
                last.then_inc(gathered, 1)

            def times_wo(b, u):
                pe.wait_ge(o_made, b + 1)
                reached(pe, y_made, b)
                at_most(pe, max_hi, b, 2)
                at_most(pe, max_lo, b, 2)
                for c in range(2):
                    last = pe.matmul(ps_w[:, D:2 * D], ot[u][:, c, :], wo_sb[:, c, :], start=(c == 0), stop=(c == 1))
                last.then_inc(wo_made, 1)

            sweep(pe, [(4, turn_max), (5, gather_quads), (3, turn_tk), (2, apply_t(0)), (3, new_state(1)),
                       (2, apply_t(1)), (4, by_key(0)), (3, read_state(1)), (4, by_key(1)), (3, new_state(2)),
                       (4, values(0)), (4, by_key(2)), (3, read_state(2)), (4, values(1)), (2, apply_t(2)),
                       (4, by_key(3)), (3, new_state(3)), (4, values(2)), (5, times_wo), (3, by_query(0)),
                       (4, values(3)), (3, read_state(3)), (3, by_query(1)), (2, apply_t(3)), (3, by_query(2)),
                       (3, by_query(3))])

        @block.scalar
        def _(act):
            act.wait_ge(consts, 80)
            act.activation(idb_sb[:, :], id_sb[:, :], ACT.Copy).then_inc(consts_made, 1)

            def copy_x(b, u):
                act.wait_ge(applied, b + 1)
                reached(act, pv_made, QUADS * (b - 1))
                reached(act, tk_turned, b - 1)
                both = ps_x[:, :].rearrange("p (h s d) -> p h s d", s=2, d=HD)
                act.activation(xa[u][:, :, 0:HD], both[:, :, 0, :], ACT.Copy)
                act.activation(tk[u][:, :, :], both[:, :, 1, :], ACT.Copy).then_inc(x_copied, 1)

            def copy_tkt(b, u):
                act.wait_ge(tk_turned, b + 1)
                reached(act, r_made, STEPS * (b - 1))
                act.activation(tkt[u][:, :, :], ps_c[:, D:2 * D].rearrange("p (g n) -> p g n", g=G), ACT.Copy)\
                   .then_inc(tkt_copied, 1)

            def max_parts(b, u):
                act.wait_ge(max_turned, b + 1)
                stored_before(act, max_placed, b, u, 32)
                act.activation(nmaxt[u][:, 0, :], nmaxt_ps, ACT.Copy).then_inc(max_hi, 1)

            def exps(q):
                def body(b, u):
                    act.wait_ge(s2_made, QUADS * b + q + 1)
                    reached(act, pv_made, QUADS * b + q - 1)
                    act.activation(p[q % 2][:, :, :], ps_s2[q % 2][:, :].rearrange("p (h n) -> p h n", h=4),
                                   ACT.Exp).then_inc(exp_made, 1)
                return body

            def copy_r(b, u):
                act.wait_ge(pv_made, QUADS * (b + 1))
                reached(act, gathered, b)
                act.activation(r_sb[:, :, :], ps_o[:, :].rearrange("p (q n) -> p q n", q=QUADS), ACT.Copy)\
                   .then_inc(r_copied, 1)

            sweep(act, [(4, max_parts), (3, copy_tkt), (4, exps(0)), (4, exps(1)), (4, exps(2)), (4, exps(3)),
                        (4, copy_r), (2, copy_x)])

        @block.vector
        def _(dve):
            for u in range(2):
                dve.memset(xa[u][:, :, :], 0.0).then_inc(ones_step, 1)
                dve.wait_ge(ones_step, u + 1)
                dve.memset(xa[u][:, :, HD:HD + 1], 1.0).then_inc(consts_made, 1)
                dve.memset(kst[u][MAX_ROW:MAX_ROW + 2, :, :], 1.0).then_inc(consts_made, 1)
            dve.wait_ge(consts_made, 5)
            dve.wait_ge(consts, 80)

            def maxima(q):
                def body(b, u):
                    if q == 0:
                        reached(dve, max_turned, b - 1)
                    dve.wait_ge(s1_made, QUADS * b + q + 1)
                    dve.tensor_reduce(nmax[u][:, 4 * q:4 * q + 4], ps_s1[q % 2][:, :].rearrange("p (h k) -> p h k", h=4),
                                      AX.X, ALU.max, negate=True).then_inc(max_made, 1)
                return body

            def keep_state(c):
                def body(b, u):
                    dve.wait_ge(u_made, STEPS * b + c)
                    reached(dve, r_made, STEPS * b + c - 1)
                    dve.tensor_tensor(state[:, :, :], ps_c[:, 0:D].rearrange("p (g n) -> p g n", g=G),
                                      same_sb[:, :].unsqueeze(1).broadcast_to([128, G, 128]), ALU.mult)\
                       .then_inc(state_made, 1)
                return body

            def new_values(c):
                def body(b, u):
                    dve.wait_ge(r_made, STEPS * b + c)
                    t = slice(c * C, (c + 1) * C)
                    dve.tensor_tensor(xa[u][t, :, 0:HD], xa[u][t, :, 0:HD],
                                      ps_c[t, D:2 * D].rearrange("p (h d) -> p h d", h=H), ALU.subtract)\
                       .then_inc(xa_made, 1)
                return body

            def max_rest(b, u):
                dve.wait_ge(max_hi, b + 1)
                dve.tensor_tensor(nmaxt[u][:, 1, :], nmaxt_ps, nmaxt[u][:, 0, :], ALU.subtract)\
                   .then_inc(max_lo, 1)

            def invert_half(n):
                def body(b, u):
                    if n == 0:
                        dve.wait_ge(gathered, b + 1)
                        reached(dve, o_made, b)
                    half = slice(n * N, (n + 1) * N)
                    dve.reciprocal(rden[:, half], ps_o[:, 2 * N:4 * N][:, half]).then_inc(rden_made, 1)
                return body

            def normalise(b, u):
                dve.wait_ge(rden_made, 2 * (b + 1))
                reached(dve, wo_made, b - 1)
                dve.tensor_tensor(ot[u][:, :, :].rearrange("p c n -> p (c n)"), ps_o[:, 0:2 * N], rden[:, :],
                                  ALU.mult).then_inc(o_made, 1)

            def residual(b, u):
                dve.wait_ge(wo_made, b + 1)
                dve.wait_ge(x_loaded[u], per_parity(b, u, 16))
                reached(dve, x1_made, b - 1)
                dve.tensor_tensor(y[u][:, :], ps_w[:, D:2 * D], x_sb[u][:, :], ALU.add).then_inc(y_made, 1)

            def norm(k):
                def body(b, u):
                    if k == 0:
                        dve.wait_ge(y_made, b + 1)
                    else:
                        dve.wait_ge(norm_step, NORM_OPS * b + k)
                    if k < NORM_OPS:
                        layer_norm_op(dve, k, y[u][:, :], stats[:, :], moments[:, :], rstd[:, :], tmp[:, :],
                                      bits[:, :]).then_inc(norm_step, 1)
                    else:
                        stored_before(dve, x1_stored, b, u, 16)
                        dve.tensor_scalar(x1[u][:, :], y[u][:, :], moments[:, 0:1], rstd[:, 0:1], ALU.subtract,
                                          ALU.mult).then_inc(x1_made, 1)
                return body

            def invert_second(n):
                def body(b, u):
                    if not isinstance(b, int) or b > BATCH:
                        return
                    before = 2 + INVERT_STEPS - SPREAD * BETWEEN
                    if b == 0 and n == 0:
                        dve.wait_ge(second_loaded, 16)
                        invert_piece(dve, second_step, 0, before, a_second, t_second, product_second)
                    elif b > BATCH - SPREAD and n < BETWEEN:
                        k = before + (b - (BATCH - SPREAD + 1)) * BETWEEN + n
                        invert_piece(dve, second_step, k, k + 1, a_second, t_second, product_second)
                return body

            main = [(4, max_rest), (5, invert_half(0)), (5, invert_half(1)), (5, normalise), (3, keep_state(1)),
                    (3, new_values(1)), (3, keep_state(2)), (3, new_values(2)), (3, keep_state(3)), (5, residual),
                    (3, maxima(0)), (3, new_values(3)), (3, maxima(1)), (3, maxima(2)), (3, maxima(3))]
            stages = []
            for n, stage in enumerate(main):
                stages += [(0, invert_second(n)), stage, (6, norm(n))]
            sweep(dve, stages + [(6, norm(k)) for k in range(len(main), NORM_OPS + 1)])


def cross_attend(nc, sems, x1_scr, ctx_in, mask, const, stacks_scr, x2_scr):
    T = D
    XF = XD + 1
    SCALE = float(XD) ** -0.5
    SIDES = 2
    HALF = H // 2
    NG = H // 4
    MAX_ROW = CROSS_MAX_ROW
    P_BUFS = 8
    ORDER = ((0, 0, 0, 1, 1, 2), (0, 1, 2, 0, 1, 0))
    OFF = 5
    with ExitStack() as ctx:
        ph = Phase(nc, ctx, "xa")
        sem = lambda name: sems.enter_context(nc.semaphore(f"xa_{name}"))
        w_sb, b_sb, bv_sb, id_sb, gather_sb = const.w_sb, const.b_sb, const.bv_sb, const.id_sb, const.gather_sb
        m16 = const.m16
        mcol_sb = ph.sb("mcol", [128, 2, B])
        m16_rest = ph.sb("m16_rest", [B, SIDES, T])
        m16_parts = ph.sb("m16_parts", [B, SIDES, PARTS, T], BF16)
        x1 = ph.two("x1", [128, T])
        cx = ph.two("cx", [128, T])
        mrow = ph.two("mrow", [128, T])
        mq = ph.sb("mq", [128, T])
        scale_sb = ph.sb("scale", [128, 1])
        qk = ph.two("qk", [128, SIDES, T])
        rest = ph.two("rest", [128, SIDES, T])
        parts = ph.two("parts", [128, SIDES, PARTS, T], BF16)
        qst, kst = const.qst, const.kst
        va = ph.two("va", [128, 2, H, 32])
        vb = ph.sb("vb", [128, 2, N])
        nmax = ph.two("nmax", [128, 2, H])
        nmaxt = ph.two("nmaxt", [H, 2, T], BF16)
        p = [ph.sb(f"p{i}", [128, 2, T]) for i in range(P_BUFS)]
        r = ph.sb("r", [128, NG, T])
        rden = ph.sb("rden", [128, T])
        o = ph.two("o", [128, T])
        y = ph.two("y", [128, T])
        cv = ph.two("cv", [128, T])
        x1r = ph.two("x1r", [128, T])
        mr = ph.two("mr", [128, T])
        x2 = ph.two("x2", [128, T])
        stats, moments = ph.sb("stats", [128, 6]), ph.sb("moments", [128, 2])
        rstd, tmp, bits = ph.sb("rstd", [128, 1]), ph.sb("tmp", [128, 1]), ph.sb("bits", [128, 1], I32)
        ps_a, ps_n = ph.bank("projections"), ph.bank("gathered")
        ps_s1 = [ph.bank(f"s1{i}") for i in range(2)]
        ps_s2 = [ph.bank(f"s2{i}") for i in range(2)]
        ps_r = [ph.bank(f"group{i}") for i in range(2)]
        nmaxt_ps = ps_a[0:H, 0:T]

        made, m_step, m_part = sem("made"), sem("m_step"), sem("m_part")
        m_stored = sem("m_stored")
        in_loaded = [sem(f"in_loaded{u}") for u in range(2)]
        qk_made, mq_made, qk_masked, part1, rest_made, part2, part3 = (
            sem(n) for n in ("qk_made", "mq_made", "qk_masked", "part1", "rest_made", "part2", "part3"))
        v_made, vb_made, v_masked = sem("v_made"), sem("vb_made"), sem("v_masked")
        parts_stored = [sem(f"parts_stored{u}") for u in range(2)]
        max_placed = [sem(f"max_placed{u}") for u in range(2)]
        st_loaded = [[sem(f"st_loaded{u}{i}") for i in range(2)] for u in range(2)]
        s1_made, max_made, max_turned, max_hi, max_lo = (
            sem(n) for n in ("s1_made", "max_made", "max_turned", "max_hi", "max_lo"))
        s2_made, exp_made, pv_made, r_copied, gathered = (
            sem(n) for n in ("s2_made", "exp_made", "pv_made", "r_copied", "gathered"))
        rden_made, o_made, o_masked, y_made, norm_step, x2_made = (
            sem(n) for n in ("rden_made", "o_made", "o_masked", "y_made", "norm_step", "x2_made"))
        cv_loaded = [sem(f"cv_loaded{u}") for u in range(2)]
        res_loaded = [sem(f"res_loaded{u}") for u in range(2)]
        x2_stored = [sem(f"x2_stored{u}") for u in range(2)]
        mcol_turned, scale_made = sem("mcol_turned"), sem("scale_made")
        MADE = 3
        LAG = 4

        def shifted(slot):
            return (slot - OFF) % H, LAG + 1 if slot >= OFF else LAG + 2

        block = ctx.enter_context(nc.Block())

        @block.sync
        def _(sp):
            def load_in(b, u):
                reached(sp, qk_masked, b - 1)
                sp.dma_start(x1[u][:, :], x1_scr[b]).then_inc(in_loaded[u], 16)
                sp.dma_start(cx[u][:, :], ctx_in[b]).then_inc(in_loaded[u], 16)
                sp.dma_start(mrow[u][:, :], mask[b, 0].partition_broadcast(128)).then_inc(in_loaded[u], 16)

            def store_parts(b, u):
                sp.wait_ge(part3, b + 1)
                rows = stacks_scr[b].rearrange("s c f h t -> s c (f h) t")[:, :, 0:XD * H]
                row = 0
                for part, n in Q_PARTS:
                    sp.dma_start(rows[0, row:row + n].rearrange("c m t -> m c t"),
                                 parts[u][:, 0, part, :].unsqueeze(1).broadcast_to([128, n, T]))\
                        .then_inc(parts_stored[u], 16)
                    row += n
                row = 0
                for part, n in K_PARTS:
                    sp.dma_start(rows[1, row:row + n].rearrange("c m t -> m c t"), parts[u][:, 1, part:part + n, :])\
                        .then_inc(parts_stored[u], 16)
                    row += n

            def load_stacks(half):
                heads = slice(half * HALF, (half + 1) * HALF)

                def body(b, u):
                    if isinstance(b, int) and b == 0:
                        const.wait(sp)
                    if half == 0:
                        if isinstance(b, int) and b == 0:
                            sp.wait_ge(m_stored, 16 * SIDES * TERMS)
                        sp.wait_ge(parts_stored[u], per_parity(b, u, 16 * TERMS))
                    reached(sp, s2_made, H * (b - 2) + (half + 1) * HALF)
                    for side, stack in enumerate((qst, kst)):
                        sp.dma_start(stack[u][0:TERMS * XF, heads, :],
                                     stacks_scr[b, side].rearrange("c f h t -> (c f) h t")[:, heads, :])\
                            .then_inc(st_loaded[u][half], 16)
                return body

            def place_max(b, u):
                sp.wait_ge(max_lo, b + 1)
                for part in range(2):
                    row = MAX_ROW + part
                    sp.dma_start(qst[u][row:row + 1, :, :], nmaxt[u][:, part, :]).then_inc(max_placed[u], 16)

            def load_cv(b, u):
                reached(sp, v_made, b - 1)
                sp.dma_start(cv[u][:, :], ctx_in[b]).then_inc(cv_loaded[u], 16)

            def load_residual(b, u):
                reached(sp, y_made, b - 1)
                sp.dma_start(x1r[u][:, :], x1_scr[b]).then_inc(res_loaded[u], 16)
                sp.dma_start(mr[u][:, :], mask[b, 0].partition_broadcast(128)).then_inc(res_loaded[u], 16)

            def store_x2(b, u):
                sp.wait_ge(x2_made, b + 1)
                sp.dma_start(x2_scr[b], x2[u][:, :]).then_inc(x2_stored[u], 16)

            sweep(sp, [(LAG + 1, place_max), (LAG, load_stacks(1)), (2, store_parts), (LAG + 4, store_x2), (0, load_in),
                       (LAG - 1, load_cv), (LAG + 1, load_residual), (LAG - 1, load_stacks(0))])
            for u in range(2):
                sp.wait_ge(x2_stored[u], B // 2 * 16)

        @block.tensor
        def _(pe):
            const.wait(pe)
            for c in range(2):
                last = pe.transpose(ps_n[:, c * B:(c + 1) * B], m16[:, 0, c * 128:(c + 1) * 128], id_sb[0:B, 0:B])
            last.then_inc(mcol_turned, 1)

            def project_qk(b, u):
                pe.wait_ge(in_loaded[u], per_parity(b, u, 48))
                reached(pe, qk_masked, b)
                reached(pe, max_lo, b - LAG + 1)
                pe.matmul(ps_a[:, 0:T], w_sb[:, 0, :], x1[u][:, :], start=True, stop=True)
                pe.matmul(ps_a[:, T:2 * T], w_sb[:, 1, :], cx[u][:, :], start=True, stop=True).then_inc(qk_made, 1)

            def project_v(b, u):
                pe.wait_ge(cv_loaded[u], per_parity(b, u, 16))
                at_most(pe, qk_masked, b, LAG)
                reached(pe, max_lo, b)
                for c in range(2):
                    last = pe.matmul(ps_a[:, c * N:(c + 1) * N], cv[u][:, c * 128:(c + 1) * 128], w_sb[:, 2, :],
                                     start=True, stop=True)
                last.then_inc(v_made, 1)

            def by_query(h):
                def body(b, u):
                    if h == 0 and isinstance(b, int) and b == 0:
                        pe.wait_ge(made, MADE)
                    if h % HALF == 0:
                        pe.wait_ge(st_loaded[u][h // HALF], per_parity(b, u, 32))
                    reached(pe, max_made, H * b + h - 1)
                    for c in range(2):
                        last = pe.matmul(ps_s1[h % 2][:, c * T:(c + 1) * T], qst[u][0:MAX_ROW, h, c * 128:(c + 1) * 128],
                                         kst[u][0:MAX_ROW, h, :], start=True, stop=True)
                    last.then_inc(s1_made, 1)
                return body

            def turn_max(b, u):
                pe.wait_ge(max_made, H * (b + 1))
                pe.wait_ge(v_masked, b + 1)
                for c in range(2):
                    last = pe.transpose(ps_a[0:H, c * 128:(c + 1) * 128], nmax[u][:, c, :], id_sb[:, :])
                last.then_inc(max_turned, 1)

            def by_key(h):
                def body(b, u):
                    if h == 0:
                        pe.wait_ge(max_placed[u], per_parity(b, u, 32))
                    reached(pe, exp_made, H * b + h - 1)
                    for c in range(2):
                        last = pe.matmul(ps_s2[h % 2][:, c * T:(c + 1) * T], kst[u][:, h, c * 128:(c + 1) * 128],
                                         qst[u][:, h, :], start=True, stop=True)
                    last.then_inc(s2_made, 1)
                return body

            def values(g, c):
                def body(b, u):
                    if c == 0:
                        reached(pe, r_copied, NG * b + g - 1)
                        pe.wait_ge(exp_made, H * b + 4 * g + 4)
                    for j in range(4):
                        h = 4 * g + j
                        last = pe.matmul(ps_r[g % 2][32 * j:32 * j + 32, 0:T], va[u][:, c, h, :],
                                         p[h % P_BUFS][:, c, :], start=(c == 0), stop=(c == 1))
                    if c == 1:
                        last.then_inc(pv_made, 1)
                return body

            def gather_groups(n):
                def body(b, u):
                    if n == 0:
                        pe.wait_ge(r_copied, NG * (b + 1))
                        reached(pe, o_made, b)
                    for g in range(NG):
                        last = pe.matmul(ps_n[32 * g:32 * g + 32, n * T:(n + 1) * T], gather_sb[:, n, :], r[:, g, :],
                                         start=True, stop=True)
                    if n == 1:
                        last.then_inc(gathered, 1)
                return body

            stages = []
            for slot in range(H):
                stages.append((LAG, by_query(slot)))
                h, lag = shifted(slot)
                stages.append((lag, by_key(h)))
                if h % 4 in (1, 2):
                    c = h % 4 - 1
                    stages.append((lag, values(h // 4 - 1, c)) if h > 4 else (lag + 1, values(NG - 1, c)))
                if slot == 0:
                    stages.append((LAG + 1, turn_max))
                if slot == 3:
                    stages.append((1, project_qk))
                if h in (6, 7):
                    stages.append((lag + 1, gather_groups(h // 7)))
                if slot == 6:
                    stages.append((LAG, project_v))
            sweep(pe, stages)

        @block.scalar
        def _(act):
            act.wait_ge(m_part, 3 * 1)
            for side in range(SIDES):
                for row, part in enumerate(ORDER[side]):
                    act.dma_start(stacks_scr[:, side, row, XD],
                                 m16_parts[:, side, part, :].unsqueeze(1).broadcast_to([B, H, T])).then_inc(m_stored, 16)
            act.wait_ge(mcol_turned, 1)
            act.activation(mcol_sb[:, :, :], ps_n[:, 0:2 * B].rearrange("p (c b) -> p c b", c=2), ACT.Copy)\
               .then_inc(made, 1)

            def first_part(b, u):
                act.wait_ge(qk_masked, b + 1)
                stored_before(act, parts_stored, b, u, 16 * TERMS)
                act.activation(parts[u][:, :, 0, :], qk[u][:, :, :], ACT.Copy).then_inc(part1, 1)

            def second_part(b, u):
                act.wait_ge(rest_made, b + 1)
                act.activation(parts[u][:, :, 1, :], rest[u][:, :, :], ACT.Copy).then_inc(part2, 1)

            def max_parts(b, u):
                act.wait_ge(max_turned, b + 1)
                stored_before(act, max_placed, b, u, 32)
                act.activation(nmaxt[u][:, 0, :], nmaxt_ps, ACT.Copy).then_inc(max_hi, 1)

            def exps(h):
                def body(b, u):
                    act.wait_ge(s2_made, H * b + h + 1)
                    if h % 4 == 0:
                        reached(act, pv_made, NG * b + h // 4 + 1 - P_BUFS // 4)
                    act.activation(p[h % P_BUFS][:, :, :], ps_s2[h % 2][:, :].rearrange("p (c t) -> p c t", c=2),
                                   ACT.Exp).then_inc(exp_made, 1)
                return body

            def copy_r(g):
                def body(b, u):
                    act.wait_ge(pv_made, NG * b + g + 1)
                    if g == 0:
                        reached(act, gathered, b)
                    act.activation(r[:, g, :], ps_r[g % 2][:, 0:T], ACT.Copy).then_inc(r_copied, 1)
                return body

            stages = []
            for slot in range(H):
                h, lag = shifted(slot)
                stages.append((lag, exps(h)))
                if h % 4 == 3:
                    stages.append((lag, copy_r(h // 4 - 1)) if h > 4 else (lag + 1, copy_r(NG - 1)))
                if slot == 0:
                    stages.append((LAG + 1, max_parts))
                if slot == 6:
                    stages.append((1, first_part))
                if slot == 10:
                    stages.append((1, second_part))
            sweep(act, stages)

        @block.vector
        def _(dve):
            for u in range(2):
                dve.memset(va[u][:, :, :, :], 0.0).then_inc(m_step, 1)
            dve.wait_ge(m_step, 2)
            for u in range(2):
                dve.memset(va[u][:, :, :, XD:XD + 1], 1.0).then_inc(made, 1)
            const.wait(dve)
            dve.tensor_scalar(m16[:, 1, :], m16[:, 1, :], 1.0, NEG, ALU.subtract, ALU.mult).then_inc(m_step, 1)
            dve.wait_ge(m_step, 3)
            dve.tensor_copy(m16_parts[:, :, 0, :], m16[:, :, :]).then_inc(m_part, 1)
            dve.wait_ge(m_part, 1)
            dve.tensor_tensor(m16_rest[:, :, :], m16[:, :, :], m16_parts[:, :, 0, :], ALU.subtract).then_inc(m_step, 1)
            dve.wait_ge(m_step, 4)
            dve.tensor_copy(m16_parts[:, :, 1, :], m16_rest[:, :, :]).then_inc(m_part, 1)
            dve.wait_ge(m_part, 2)
            dve.tensor_tensor(m16_parts[:, :, 2, :], m16_rest[:, :, :], m16_parts[:, :, 1, :],
                              ALU.subtract).then_inc(m_part, 1)

            def mask_qk(b, u):
                dve.wait_ge(qk_made, b + 1)
                dve.wait_ge(mq_made, b + 1)
                reached(dve, rest_made, b - 1)
                dve.scalar_tensor_tensor(qk[u][:, 0, :], ps_a[:, 0:T], b_sb[:, 0:1], mq[:, :], ALU.add, ALU.mult)
                dve.scalar_tensor_tensor(qk[u][:, 1, :], ps_a[:, T:2 * T], b_sb[:, 1:2], mrow[u][:, :], ALU.add,
                                         ALU.mult).then_inc(qk_masked, 1)

            def mask_v(b, u):
                dve.wait_ge(v_made, b + 1)
                dve.tensor_tensor(vb[:, :, :], ps_a[:, 0:2 * N].rearrange("p (c n) -> p c n", c=2),
                                  bv_sb[:, :].unsqueeze(1).broadcast_to([128, 2, N]), ALU.add).then_inc(vb_made, 1)
                dve.wait_ge(vb_made, b + 1)
                if isinstance(b, int) and b == 0:
                    dve.wait_ge(made, MADE)
                reached(dve, pv_made, NG * (b - 1))
                for c in range(2):
                    ins = dve.tensor_scalar(va[u][:, c, :, 0:XD], vb[:, c, :].rearrange("p (h d) -> p h d", h=H),
                                            mcol_sb[:, c, bass.ds(b, 1)] if not isinstance(b, int) else
                                            mcol_sb[:, c, b:b + 1], None, ALU.mult)
                ins.then_inc(v_masked, 1)

            def maximum(h):
                def body(b, u):
                    if h == 0:
                        reached(dve, max_turned, b - 1)
                    dve.wait_ge(s1_made, H * b + h + 1)
                    dve.tensor_reduce(nmax[u][:, :, h], ps_s1[h % 2][:, :].rearrange("p (c s) -> p c s", c=2),
                                      AX.X, ALU.max, negate=True).then_inc(max_made, 1)
                return body

            def max_rest(b, u):
                dve.wait_ge(max_hi, b + 1)
                dve.tensor_tensor(nmaxt[u][:, 1, :], nmaxt_ps, nmaxt[u][:, 0, :], ALU.subtract)\
                   .then_inc(max_lo, 1)

            def invert_half(n):
                def body(b, u):
                    if n == 0:
                        dve.wait_ge(gathered, b + 1)
                    half = slice(n * T // 2, (n + 1) * T // 2)
                    dve.reciprocal(rden[:, half], ps_n[:, T:2 * T][:, half]).then_inc(rden_made, 1)
                return body

            def normalise(b, u):
                dve.wait_ge(rden_made, 2 * (b + 1))
                reached(dve, o_masked, b - 1)
                dve.tensor_tensor(o[u][:, :], ps_n[:, 0:T], rden[:, :], ALU.mult).then_inc(o_made, 1)

            def norm(k):
                def body(b, u):
                    if k == 0:
                        dve.wait_ge(y_made, b + 1)
                    else:
                        dve.wait_ge(norm_step, NORM_OPS * b + k)
                    if k < NORM_OPS:
                        layer_norm_op(dve, k, y[u][:, :], stats[:, :], moments[:, :], rstd[:, :], tmp[:, :],
                                      bits[:, :]).then_inc(norm_step, 1)
                    else:
                        stored_before(dve, x2_stored, b, u, 16)
                        dve.tensor_scalar(x2[u][:, :], y[u][:, :], moments[:, 0:1], rstd[:, 0:1], ALU.subtract,
                                          ALU.mult).then_inc(x2_made, 1)
                return body

            stages = []
            for slot in range(H):
                stages.append((LAG, maximum(slot)))
                if slot == 1:
                    stages.append((LAG + 1, max_rest))
                if slot == 4:
                    stages.append((1, mask_qk))
                if slot == 10:
                    stages.append((LAG, mask_v))
                if slot in (12, 13):
                    stages.append((LAG + 2, invert_half(slot - 12)))
                if slot == 14:
                    stages.append((LAG + 2, normalise))
                if slot <= NORM_OPS:
                    stages.append((LAG + 3, norm(slot)))
            sweep(dve, stages)

        @block.gpsimd
        def _(pool):
            pool.memset(scale_sb[:, :], SCALE).then_inc(scale_made, 1)
            pool.wait_ge(scale_made, 1)

            def scale_mask(b, u):
                pool.wait_ge(in_loaded[u], per_parity(b, u, 48))
                reached(pool, qk_masked, b)
                pool.tensor_tensor(mq[:, :], mrow[u][:, :], scale_sb[:, :].broadcast_to([128, T]), ALU.mult).then_inc(mq_made, 1)

            def residue(b, u):
                pool.wait_ge(part1, b + 1)
                reached(pool, part3, b - 1)
                pool.tensor_tensor(rest[u][:, :, :], qk[u][:, :, :], parts[u][:, :, 0, :], ALU.subtract)\
                    .then_inc(rest_made, 1)

            def third_part(b, u):
                pool.wait_ge(part2, b + 1)
                pool.tensor_tensor(parts[u][:, :, 2, :], rest[u][:, :, :], parts[u][:, :, 1, :], ALU.subtract)\
                    .then_inc(part3, 1)

            def add_residual(b, u):
                pool.wait_ge(o_made, b + 1)
                pool.wait_ge(res_loaded[u], per_parity(b, u, 32))
                pool.tensor_tensor(o[u][:, :], o[u][:, :], mr[u][:, :], ALU.mult).then_inc(o_masked, 1)
                pool.wait_ge(o_masked, b + 1)
                reached(pool, x2_made, b - 1)
                pool.tensor_tensor(y[u][:, :], o[u][:, :], x1r[u][:, :], ALU.add).then_inc(y_made, 1)

            sweep(pool, [(1, scale_mask), (1, residue), (1, third_part), (LAG + 2, add_residual)])


def feed_forward(nc, sems, x2_scr, const, bias_scr, out):
    TOP = 2
    PAIRS = E // 2
    ROWS = (E + 1) * D // 128
    with ExitStack() as ctx:
        ph = Phase(nc, ctx, "ff")
        sem = lambda name: sems.enter_context(nc.semaphore(f"ff_{name}"))
        id_sb, rw_sb, rb_sb, ids_sb = const.id_sb, const.rw_sb, const.rb_sb, const.ids_sb
        ew_sb, ow_sb, bias = const.ew_sb, const.ow_sb, const.bias
        bias_rest = ph.sb("bias_rest", [ROWS, 128])
        bias_parts = ph.sb("bias_parts", [ROWS, PARTS, 128], BF16)
        bias_sb = ph.sb("bias_stack", [PARTS, (E + 1) * D], BF16)
        ones = ph.sb("ones", [PARTS, 128], BF16)
        x2_sb = ph.two("x2", [128, D])
        x2_all = ph.sb("x2_all", [128, B, D])
        xt_all = ph.sb("xt_all", [128, B, 2, 128])
        xt = ph.two("xt", [128, 2, 128])
        probs = ph.sb("probs", [128, B, E])
        row = ph.sb("row", [128, B])
        row_inv = ph.sb("row_inv", [128, B])
        best = ph.sb("best", [128, B, 8])
        best_at = ph.sb("best_at", [128, B, 8], U32)
        at = ph.sb("at", [128, TOP, B])
        share = ph.sb("share", [128, TOP, B])
        chosen = ph.sb("chosen", [128, TOP, B, E])
        gates = ph.sb("gates", [128, B, E])
        ge = ph.two("gelu", [128, E, D])
        comb = ph.two("comb", [128, D])
        combt = ph.two("combt", [128, 2, 128])
        y = ph.sb("y", [128, D])
        res = ph.two("out", [128, D])
        stats, moments = ph.sb("stats", [128, 6]), ph.sb("moments", [128, 2])
        rstd, tmp, bits = ph.sb("rstd", [128, 1]), ph.sb("tmp", [128, 1]), ph.sb("bits", [128, 1], I32)
        ps_t = [ph.bank(f"t{i}") for i in range(2)]
        ps_c, ps_o = ps_t
        ps_l = ph.bank("logits")
        ps_e = [ph.bank(f"e{i}") for i in range(PAIRS)]

        all_loaded, b_step, b_stored, b_loaded = (sem(n) for n in ("all_loaded", "b_step", "b_stored", "b_loaded"))
        xt_made, xt_copied, logits_made, logits_less_max, exps_made, gate_step, gates_made = (
            sem(n) for n in ("xt_made", "xt_copied", "logits_made", "logits_less_max", "exps_made", "gate_step",
                             "gates_made"))
        expert_made, gelu_made, comb_step, combined, comb_turned, comb_copied, out_made, norm_step, normed = (
            sem(n) for n in ("expert_made", "gelu_made", "comb_step", "combined", "comb_turned", "comb_copied",
                             "out_made", "norm_step", "normed"))
        x2_loaded = [sem(f"x2_loaded{u}") for u in range(2)]
        xt_moved = sem("xt_moved")
        out_stored = [sem(f"out_stored{u}") for u in range(2)]

        block = ctx.enter_context(nc.Block())

        @block.sync
        def _(sp):
            def load_x2(b, u):
                reached(sp, xt_made, b - 1)
                sp.dma_start(x2_sb[u][:, :], x2_scr[b]).then_inc(x2_loaded[u], 16)

            sweep(sp, [(0, load_x2)])
            sp.dma_start(x2_all[:, :, :], x2_scr.rearrange("b p d -> p b d")).then_inc(all_loaded, 16)

            def store_out(b, u):
                sp.wait_ge(normed, b + 1)
                sp.dma_start(out[b], res[u][:, :]).then_inc(out_stored[u], 16)

            sweep(sp, [(3, store_out)])
            for u in range(2):
                sp.wait_ge(out_stored[u], B // 2 * 16)

        @block.tensor
        def _(pe):
            const.wait(pe)

            def turn_x2(b, u):
                pe.wait_ge(x2_loaded[u], per_parity(b, u, 16))
                reached(pe, xt_copied, b - 1)
                for c in range(2):
                    last = pe.transpose(ps_t[u][:, c * 128:(c + 1) * 128], x2_sb[u][:, c * 128:(c + 1) * 128],
                                        id_sb[:, :])
                last.then_inc(xt_made, 1)

            def logits(b, u):
                pe.wait_ge(xt_copied, b + 1)
                for c in range(2):
                    last = pe.matmul(ps_l[:, bass.ds(b * E, E)], xt[u][:, c, :], rw_sb[:, c, :],
                                     start=(c == 0), stop=(c == 1))
                last.then_inc(logits_made, 1)

            sweep(pe, [(0, turn_x2), (1, logits)])
            pe.wait_ge(b_loaded, 16)

            def expert(j):
                def body(b, u):
                    if j == 0:
                        pe.wait_ge(xt_moved, b + 1)
                    reached(pe, gelu_made, PAIRS * (b - 1) + j + 1)
                    pe.matmul(ps_e[j][:, :], ones[:, :], bias_sb[:, 2 * j * D:2 * (j + 1) * D], start=True, stop=False)
                    for c in range(2):
                        last = pe.matmul(ps_e[j][:, :], xt[u][:, c, :],
                                         ew_sb[:, c, 2 * j:2 * j + 2, :].rearrange("p e d -> p (e d)"),
                                         start=False, stop=(c == 1))
                    last.then_inc(expert_made, 1)
                return body

            def turn_comb(b, u):
                pe.wait_ge(combined, b + 1)
                reached(pe, comb_copied, b)
                for c in range(2):
                    last = pe.transpose(ps_c[:, c * 128:(c + 1) * 128], comb[u][:, c * 128:(c + 1) * 128], id_sb[:, :])
                last.then_inc(comb_turned, 1)

            def output(b, u):
                pe.wait_ge(comb_copied, b + 1)
                reached(pe, norm_step, (1 + NORM_OPS) * (b - 1) + 1)
                pe.matmul(ps_o[:, 0:D], ones[:, :], bias_sb[:, E * D:], start=True, stop=False)
                for c in range(2):
                    last = pe.matmul(ps_o[:, 0:D], combt[u][:, c, :], ow_sb[:, c, :], start=False, stop=(c == 1))
                last.then_inc(out_made, 1)

            sweep(pe, [(0, expert(0)), (0, expert(1)), (1, turn_comb), (0, expert(2)), (1, output), (0, expert(3))])

        @block.scalar
        def _(act):
            def copy_xt(b, u):
                act.wait_ge(xt_made, b + 1)
                reached(act, logits_made, b - 1)
                act.activation(xt[u][:, :, :], ps_t[u][:, 0:D].rearrange("p (c n) -> p c n", c=2), ACT.Copy)
                act.activation(entry(xt_all, b), ps_t[u][:, 0:D].rearrange("p (c n) -> p c n", c=2), ACT.Copy)\
                   .then_inc(xt_copied, 1)

            sweep(act, [(0, copy_xt)])
            act.wait_ge(logits_less_max, 1)
            act.activation(probs[:, :, :], probs[:, :, :], ACT.Exp).then_inc(exps_made, 1)

            def gelus(j):
                def body(b, u):
                    act.wait_ge(expert_made, PAIRS * b + j + 1)
                    if j == 0:
                        reached(act, combined, b - 1)
                    act.activation(ge[u][:, 2 * j:2 * j + 2, :], ps_e[j][:, :].rearrange("p (e d) -> p e d", e=2),
                                   ACT.Gelu_apprx_tanh).then_inc(gelu_made, 1)
                return body

            def copy_combt(b, u):
                act.wait_ge(comb_turned, b + 1)
                reached(act, out_made, b - 1)
                act.activation(combt[u][:, :, :], ps_c[:, 0:D].rearrange("p (c n) -> p c n", c=2), ACT.Copy)\
                   .then_inc(comb_copied, 1)

            sweep(act, [(0, gelus(0)), (0, gelus(1)), (1, copy_combt), (0, gelus(2)), (0, gelus(3))])

        @block.vector
        def _(dve):
            const.wait(dve)
            dve.memset(ones[:, :], 1.0).then_inc(b_step, 1)
            chain = Chain(dve, b_step, 0, 0)
            chain.n = 1
            chain.link(dve.tensor_copy(bias_parts[:, 0, :], bias[:, :]))
            chain.link(dve.tensor_tensor(bias_rest[:, :], bias[:, :], bias_parts[:, 0, :], ALU.subtract))
            chain.link(dve.tensor_copy(bias_parts[:, 1, :], bias_rest[:, :]))
            chain.link(dve.tensor_tensor(bias_rest[:, :], bias_rest[:, :], bias_parts[:, 1, :], ALU.subtract))
            chain.link(dve.tensor_copy(bias_parts[:, 2, :], bias_rest[:, :]))

            def by_expert(a):
                return a.unsqueeze(len(a.shape)).broadcast_to([*a.shape, E])

            chain = Chain(dve, gate_step, 0, 0)
            dve.wait_ge(logits_made, B)
            chain.link(dve.tensor_tensor(probs[:, :, :], ps_l[:, 0:B * E].rearrange("p (b e) -> p b e", e=E),
                                         rb_sb[:, :].unsqueeze(1).broadcast_to([128, B, E]), ALU.add))
            chain.link(dve.tensor_reduce(row[:, :], probs[:, :, :], AX.X, ALU.max))
            chain.link(dve.tensor_tensor(probs[:, :, :], probs[:, :, :], by_expert(row[:, :]), ALU.subtract))
            dve.tensor_copy(row_inv[:, :], row[:, :]).then_inc(logits_less_max, 1)
            dve.wait_ge(exps_made, 1)
            chain.link(dve.tensor_reduce(row[:, :], probs[:, :, :], AX.X, ALU.add))
            dve.wait_ge(logits_less_max, 1)
            chain.link(dve.reciprocal(row_inv[:, :], row[:, :]))
            chain.link(dve.tensor_tensor(probs[:, :, :], probs[:, :, :], by_expert(row_inv[:, :]), ALU.mult))
            for b in range(B):
                dve.max(best[:, b, :], probs[:, b, :]).then_inc(gate_step, 1)
                chain.n += 1
            dve.wait_ge(gate_step, chain.n)
            for b in range(B):
                dve.max_index(best_at[:, b, :], best[:, b, :], probs[:, b, :]).then_inc(gate_step, 1)
                chain.n += 1
            dve.wait_ge(gate_step, chain.n)
            chain.link(dve.tensor_tensor(row[:, :], best[:, :, 0], best[:, :, 1], ALU.add))
            chain.link(dve.reciprocal(row_inv[:, :], row[:, :]))
            chain.link(dve.tensor_tensor(share[:, :, :], best[:, :, 0:TOP].rearrange("p b k -> p k b"),
                                         row_inv[:, :].unsqueeze(1).broadcast_to([128, TOP, B]), ALU.mult))
            chain.link(dve.tensor_copy(at[:, :, :], best_at[:, :, 0:TOP].rearrange("p b k -> p k b")))
            for k in range(TOP):
                chain.link(dve.tensor_tensor(chosen[:, k, :, :], ids_sb[:, :].unsqueeze(1).broadcast_to([128, B, E]),
                                             by_expert(at[:, k, :]), ALU.is_equal))
                chain.link(dve.tensor_tensor(chosen[:, k, :, :], chosen[:, k, :, :], by_expert(share[:, k, :]), ALU.mult))
            dve.tensor_tensor(gates[:, :, :], chosen[:, 0, :, :], chosen[:, 1, :, :], ALU.add).then_inc(gates_made, 1)
            dve.wait_ge(gates_made, 1)

            def combine(half):
                def body(b, u):
                    chain = Chain(dve, comb_step, b, E - 1)
                    chain.n = half * E // 2
                    for e in range(half * E // 2, (half + 1) * E // 2):
                        if e % 2 == 0:
                            dve.wait_ge(gelu_made, PAIRS * b + e // 2 + 1)
                        gate = entry(gates, b)[:, e:e + 1]
                        if e == 0:
                            reached(dve, comb_turned, b - 1)
                            ins = dve.tensor_scalar(comb[u][:, :], ge[u][:, e, :], gate, None, ALU.mult)
                        else:
                            ins = dve.scalar_tensor_tensor(comb[u][:, :], ge[u][:, e, :], gate, comb[u][:, :], ALU.mult,
                                                           ALU.add)
                        if e == E - 1:
                            ins.then_inc(combined, 1)
                            dve.wait_ge(combined, b + 1)
                        else:
                            chain.link(ins)
                return body

            dve.wait_ge(all_loaded, 16)

            def residual_norm(b, u):
                chain = Chain(dve, norm_step, b, 1 + NORM_OPS)
                dve.wait_ge(out_made, b + 1)
                reached(dve, normed, b)
                chain.link(dve.tensor_tensor(y[:, :], ps_o[:, 0:D], entry(x2_all, b), ALU.add))
                layer_norm_stats(dve, chain, y[:, :], stats[:, :], moments[:, :], rstd[:, :], tmp[:, :], bits[:, :])
                chain.done()
                stored_before(dve, out_stored, b, u, 16)
                dve.tensor_scalar(res[u][:, :], y[:, :], moments[:, 0:1], rstd[:, 0:1], ALU.subtract, ALU.mult)\
                   .then_inc(normed, 1)

            sweep(dve, [(0, combine(0)), (2, residual_norm), (0, combine(1))])

        @block.gpsimd
        def _(pool):
            def move_xt(b, u):
                reached(pool, expert_made, PAIRS * (b - 1))
                pool.tensor_copy(xt[u][:, :, :], entry(xt_all, b)).then_inc(xt_moved, 1)

            pool.wait_ge(b_step, 6)
            pool.dma_start(bias_scr.rearrange("c (r n) -> r c n", n=128), bias_parts[:, :, :]).then_inc(b_stored, 16)
            pool.wait_ge(b_stored, 16)
            pool.dma_start(bias_sb[:, :], bias_scr[:, :]).then_inc(b_loaded, 16)
            pool.wait_ge(logits_made, B)
            sweep(pool, [(0, move_xt)])


def decoder_layer(nc, x, ctx_in, mask, attn_w, attn_wo, xattn_wq, xattn_wk, xattn_wv, xattn_bias_qk, xattn_bv,
                  router_w, router_b, expert_w, expert_b, out_w, out_b, rope, identity, in_block, same_head, hidden,
                  self_gather, gather, stack_rows, expert_ids, out):
    scratch = lambda name, shape, dt=F32: nc.dram_tensor(f"scratch_{name}", shape, dt, kind="Internal").ap()
    self_parts = scratch("self_parts", [B, 3, PARTS, HD, H, N], BF16)
    cross_stacks = scratch("cross_stacks", [B, 2, TERMS, XD + 1, H, D], BF16)
    bias_parts = scratch("bias_parts", [PARTS, (E + 1) * D], BF16)
    vk, kb = scratch("vk", [B, N, 2 * D]), scratch("kb", [B, N, D])
    a, t = (scratch(n, [B, H, NC, C, C]) for n in ("a", "t"))
    x1, x2 = (scratch(n, [B, N, D]) for n in ("x1", "x2"))
    with ExitStack() as sems:
        const = Constants(nc, sems)
        cross_constants(const, mask, xattn_wq, xattn_wk, xattn_wv, xattn_bias_qk, xattn_bv, identity, gather,
                        stack_rows)
        feed_forward_constants(const, router_w, router_b, expert_w, expert_b, out_w, out_b, expert_ids)
        project(nc, sems, x, attn_w, rope, identity, in_block, self_parts, vk, kb, a, t)
        attend(nc, sems, x, attn_wo, identity, same_head, hidden, self_gather, self_parts, vk, kb, a, t, x1, const)
        cross_attend(nc, sems, x1, ctx_in, mask, const, cross_stacks, x2)
        feed_forward(nc, sems, x2, const, bias_parts, out)


def features_first(w):
    return w.reshape(D, H, HD).transpose(0, 2, 1).reshape(D, D)


def features_first_rows(w):
    return w.reshape(H, XD, -1).swapaxes(0, 1).reshape(w.shape)


def shape_constants():
    import numpy as np

    bf16 = np.dtype("bfloat16")
    f32 = np.float32
    inv = (1.0 / f32(10000.0) ** (np.arange(0, HD, 2, dtype=f32) / f32(HD))).astype(f32)
    angle = np.arange(N, dtype=f32)[:, None] * inv
    cos, sin = np.cos(angle), np.sin(angle)
    cos = np.repeat(np.concatenate([cos, cos], 1), H, 1)
    sin = np.repeat(np.concatenate([-sin, sin], 1), H, 1)
    scale = f32(HD ** -0.5)
    seen = np.tril(np.ones((N, N), bool))
    hidden = np.where(seen, 0.0, OUT_OF_SIGHT)
    self_gather = np.zeros((128, 2, 4 * HD), f32)
    stack_rows = np.zeros((2, CROSS_MAX_ROW + 2 - TERMS * (XD + 1), D), bf16)
    stack_rows[1, -2:] = 1
    gather = np.zeros((128, 2, 32), f32)
    for j in range(4):
        for d in range(HD):
            self_gather[32 * j + d, 0, HD * j + d] = 1
            self_gather[32 * j + HD, 1, HD * j + d] = 1
        for d in range(XD):
            gather[32 * j + d, 0, XD * j + d] = 1
            gather[32 * j + XD, 1, XD * j + d] = 1
    return {
        "rope": np.stack([np.concatenate([cos * scale, cos], 1), np.concatenate([sin * scale, sin], 1)], 1).astype(f32),
        "identity": np.eye(128, dtype=f32),
        "in_block": -np.tile(np.tril(np.ones((C, C), f32), -1), (NC, 1)),
        "same_head": np.kron(np.eye(8), np.ones((HD, HD))).astype(f32),
        "hidden": np.stack([hidden, hidden.T], 1).astype(bf16),
        "self_gather": self_gather,
        "gather": gather,
        "stack_rows": stack_rows,
        "expert_ids": np.arange(E, dtype=f32),
    }


def kernel(x, ctx_2048, mask_Bx1x2048_fk1, L0_attn_Wq, L0_attn_Wk, L0_attn_Wv, L0_attn_Wo, L0_attn_Wb,
           L0_xattn_Wq, L0_xattn_bq, L0_xattn_Wk, L0_xattn_bk, L0_xattn_Wv, L0_xattn_bv, L0_ffn_router_w,
           L0_ffn_router_b, L0_ffn_expert_w, L0_ffn_expert_b, L0_ffn_out_w, L0_ffn_out_b):
    import numpy as np
    import concourse.bacc as bacc
    from concourse.bass_utils import run_bass_kernel_spmd

    a = np.asarray
    arrays = {
        "x": a(x), "ctx": a(ctx_2048), "mask": a(mask_Bx1x2048_fk1),
        "attn_w": np.concatenate([*(features_first(a(w)) for w in (L0_attn_Wq, L0_attn_Wk, L0_attn_Wv)),
                                  a(L0_attn_Wb)], 1),
        "attn_wo": a(L0_attn_Wo),
        "xattn_wq": features_first_rows(a(L0_xattn_Wq)).T,
        "xattn_wk": features_first_rows(a(L0_xattn_Wk)).T,
        "xattn_wv": a(L0_xattn_Wv).T,
        "xattn_bias_qk": np.stack([features_first_rows(a(L0_xattn_bq)), features_first_rows(a(L0_xattn_bk))], 1),
        "xattn_bv": a(L0_xattn_bv),
        "router_w": a(L0_ffn_router_w), "router_b": a(L0_ffn_router_b),
        "expert_w": a(L0_ffn_expert_w), "expert_b": a(L0_ffn_expert_b),
        "out_w": a(L0_ffn_out_w), "out_b": a(L0_ffn_out_b),
        **shape_constants(),
    }
    nc = bacc.Bacc("TRN2", target_bir_lowering=False, num_devices=1)
    arrays = {f"in_{name}": np.ascontiguousarray(v) for name, v in arrays.items()}
    args = [nc.dram_tensor(name, v.shape, mybir.dt.from_np(v.dtype), kind="ExternalInput").ap()
            for name, v in arrays.items()]
    out = nc.dram_tensor("out", (B, N, D), F32, kind="ExternalOutput").ap()
    decoder_layer(nc, *args, out)
    results = run_bass_kernel_spmd(nc, [arrays], core_ids=[0])
    return results.results[0]["out"]
```
